# Optimizing a Trainium2 kernel written in Bass

```python
import numpy as np
import jax
import jax.numpy as jnp

def _softmax(x, axis=-1):
    return jax.nn.softmax(x, axis=axis)

def _gelu(x):
    return jax.nn.gelu(x, approximate=True)

def _silu(x):
    return jax.nn.silu(x)

def _sigmoid(x):
    return jax.nn.sigmoid(x)

def _layernorm(x, axis=-1, eps=1e-05):
    m = jnp.mean(x, axis=axis, keepdims=True)
    v = jnp.var(x, axis=axis, keepdims=True)
    return (x - m) / jnp.sqrt(v + eps)

def _scatter_add(tgt, idx, src, axis=0):
    return tgt.at[idx].add(src)

def _segment_sum(src, seg, n):
    return jax.ops.segment_sum(src, seg, n)
kernel_name = 'mk_pixart_resid_d2_seqx_r8_f3f431'

def setup_inputs(seed: int=0):
    np.random.seed(seed)
    _w = jnp.asarray

    def _rec_inputs():
        import jax
        import jax.numpy as jnp
        _rk = jax.random.key(seed)
        x = -0.003379 + 0.9984 * jax.random.normal(jax.random.fold_in(_rk, 1), (4, 512, 128), jnp.float32)
        _lenS = 512 - jax.random.randint(jax.random.fold_in(_rk, 7), (4,), 0, max(1, 512 // 4) + 1, jnp.int32)
        _lenS2 = 77 - jax.random.randint(jax.random.fold_in(_rk, 8), (4,), 0, max(1, 77 // 4) + 1, jnp.int32)
        cond_1024 = -0.0142567 + 1.00875 * jax.random.normal(jax.random.fold_in(_rk, 11), (4, 128), jnp.float32)
        _ctx_1024P = jax.random.normal(jax.random.fold_in(_rk, 12), (4, 16, 128), jnp.float32)
        _ctx_1024c = jax.random.dirichlet(jax.random.fold_in(_rk, 512), 0.3 * jnp.ones((16,), jnp.float32), (4, 77))
        _ctx_1024t = jnp.einsum('bsk,bkd->bsd', _ctx_1024c, _ctx_1024P)
        _ctx_1024t = _ctx_1024t * jax.lax.rsqrt(jnp.mean(jnp.square(_ctx_1024t)) + 1e-12) * 0.953939
        ctx_1024 = -5.72187e-05 + 0.999849 * (_ctx_1024t + 0.3 * jax.random.normal(jax.random.fold_in(_rk, 612), (4, 77, 128), jnp.float32))
        _validS = jnp.arange(512)[None, :] < _lenS[:, None]
        _validS2 = jnp.arange(77)[None, :] < _lenS2[:, None]
        _causal = jnp.tril(jnp.ones((512, 512), dtype=bool))
        mask_BxS_bf0 = jnp.logical_not(jnp.ones((4, 512), dtype=bool))
        mask_BxS2_bf0 = jnp.logical_not(jnp.ones((4, 77), dtype=bool))
        return (x, cond_1024, ctx_1024, mask_BxS_bf0, mask_BxS2_bf0)
    x, cond_1024, ctx_1024, mask_BxS_bf0, mask_BxS2_bf0 = _rec_inputs()

    def _L0_xcond_setup():
        import jax, jax.numpy as jnp
        import numpy as np
        B, N, K, D, T = (16, 512, 16, 128, 3)
        EPS_ATTN = 1e-08
        LN_EPS = 1e-05

        def _ln(x, g, b):
            mu = jnp.mean(x, axis=-1, keepdims=True)
            var = jnp.mean(jnp.square(x - mu), axis=-1, keepdims=True)
            return (x - mu) * jax.lax.rsqrt(var + LN_EPS) * g + b
        key = jax.random.key(seed)
        ks = jax.random.split(key, 16)
        w = lambda k, i, o: jax.random.normal(k, (i, o), jnp.float32) * 0.02
        inp = {'x_cls': jax.random.normal(ks[0], (B, D), jnp.float32), 'x': jax.random.normal(ks[1], (B, N, D), jnp.float32), 'noise': jax.random.normal(ks[2], (B, K, D), jnp.float32), 'q_mu': jax.random.normal(ks[3], (1, 1, D), jnp.float32), 'q_logsig': jax.random.normal(ks[4], (1, 1, D), jnp.float32) * 0.02, 'lnkv_g': jnp.ones((D,), jnp.float32), 'lnkv_b': jnp.zeros((D,), jnp.float32), 'lnq_g': jnp.ones((D,), jnp.float32), 'lnq_b': jnp.zeros((D,), jnp.float32), 'lnm_g': jnp.ones((D,), jnp.float32), 'lnm_b': jnp.zeros((D,), jnp.float32), 'lnp_g': jnp.ones((D,), jnp.float32), 'lnp_b': jnp.zeros((D,), jnp.float32), 'wk': w(ks[5], D, D), 'bk': jnp.zeros((D,), jnp.float32), 'wv': w(ks[6], D, D), 'bv': jnp.zeros((D,), jnp.float32), 'wq': w(ks[7], D, D), 'bq': jnp.zeros((D,), jnp.float32), 'wu': w(ks[8], D, D), 'bu': jnp.zeros((D,), jnp.float32), 'w1': w(ks[9], D, D), 'b1': jnp.zeros((D,), jnp.float32), 'w2': w(ks[10], D, D), 'b2': jnp.zeros((D,), jnp.float32)}
        return inp
    _L0_xcond_all = _L0_xcond_setup()
    _L0_xcond_in = {k: v for k, v in _L0_xcond_all.items() if k in ('q_mu', 'q_logsig', 'lnkv_g', 'lnkv_b', 'lnq_g', 'lnq_b', 'lnm_g', 'lnm_b', 'lnp_g', 'lnp_b', 'wk', 'bk', 'wv', 'bv', 'wq', 'bq', 'wu', 'bu', 'w1', 'b1', 'w2', 'b2')}
    del _L0_xcond_all

    def _L0_ffn_setup():
        import jax, jax.numpy as jnp
        import numpy as np
        N_EXP = 8
        TOP_K = 2
        CAP_FACTOR = 1.25
        NEG_INF = -1000000000.0

        def _moe_forward(x, w_g, c_fc, c_proj):
            B, T, D = x.shape
            N = B * T
            xf = x.reshape(N, D)
            logits = xf @ w_g
            topv, topi = jax.lax.top_k(logits, TOP_K)
            full = jnp.full_like(logits, NEG_INF)
            full = full.at[jnp.arange(N)[:, None], topi].set(topv)
            probs = jax.nn.softmax(full, axis=-1)
            capacity = int(TOP_K * CAP_FACTOR * N / N_EXP)
            capacity += capacity % 2
            mask = jax.nn.one_hot(jnp.swapaxes(topi, 0, 1), N_EXP, dtype=jnp.int32)
            rank = jnp.cumsum(mask.reshape(TOP_K * N, N_EXP), axis=0).reshape(TOP_K, N, N_EXP) - 1
            mask = mask * (rank < capacity)
            rank_sel = jnp.sum(mask * rank, axis=-1)
            wts = jnp.sum(mask * probs[None], axis=-1)
            cb = jnp.zeros((N, N_EXP, capacity), x.dtype)
            tok = jnp.arange(N)
            for k in range(TOP_K):
                cb = cb.at[tok, topi[:, k], rank_sel[k]].add(wts[k])
            sec_mask = (cb != 0).astype(x.dtype)
            exp_batches = jnp.einsum('nec,nd->ecd', sec_mask, xf)
            h = jax.nn.gelu(jnp.einsum('ecd,edh->ech', exp_batches, c_fc), approximate=False)
            exp_out = jnp.einsum('ech,ehd->ecd', h, c_proj)
            out = jnp.einsum('nec,ecd->nd', cb, exp_out)
            return out.reshape(B, T, D)
        key = jax.random.key(seed)
        k1, k2, k3, k4 = jax.random.split(key, 4)
        B, T, D = (4, 64, 128)
        H = 4 * D
        x = jax.random.normal(k1, (B, T, D), jnp.float32)
        w_g = jax.random.normal(k2, (D, N_EXP), jnp.float32) * 0.02
        c_fc = jax.random.normal(k3, (N_EXP, D, H), jnp.float32) * 0.02
        c_proj = jax.random.normal(k4, (N_EXP, H, D), jnp.float32) * 0.02
        return {'x': x, 'w_g': w_g, 'c_fc': c_fc, 'c_proj': c_proj}
    _L0_ffn_all = _L0_ffn_setup()
    _L0_ffn_in = {k: v for k, v in _L0_ffn_all.items() if k in ('w_g', 'c_fc', 'c_proj')}
    del _L0_ffn_all

    def _L1_xcond_setup():
        import jax, jax.numpy as jnp
        import numpy as np
        NL, D, H, DFF = (6, 128, 16, 512)
        HD = D // H

        def _rope(x):
            L = x.shape[1]
            half = HD // 2
            inv = 1.0 / 10000.0 ** (jnp.arange(half, dtype=jnp.float32) / half)
            ang = jnp.arange(L, dtype=jnp.float32)[:, None] * inv
            cos = jnp.cos(ang)[None, :, None, :]
            sin = jnp.sin(ang)[None, :, None, :]
            x1, x2 = (x[..., :half], x[..., half:])
            return jnp.concatenate([x1 * cos - x2 * sin, x1 * sin + x2 * cos], axis=-1)

        def _ln(x, eps=1e-05):
            m = jnp.mean(x, axis=-1, keepdims=True)
            v = jnp.var(x, axis=-1, keepdims=True)
            return (x - m) * jax.lax.rsqrt(v + eps)

        def _adaln(x, emb, w, b):
            gb = emb[:, 0, :] @ w.T + b
            g, be = jnp.split(gb, 2, axis=-1)
            return _ln(x) * (1.0 + g[:, None, :]) + be[:, None, :]

        def _attn(q, k, v, mask):
            scores = jnp.einsum('bqhd,bkhd->bhqk', q, k) / np.float32(np.sqrt(HD))
            scores = jnp.where(mask[:, None, None, :], jnp.float32(-jnp.inf), scores)
            w = jax.nn.softmax(scores, axis=-1)
            return jnp.einsum('bhqk,bkhd->bqhd', w, v)
        key = jax.random.key(seed)
        ks = jax.random.split(key, 20)
        B, L, LC = (4, 128, 64)
        s = 0.02
        inp = {'x': jax.random.normal(ks[0], (B, L, D), jnp.float32), 'noise_emb': jax.random.normal(ks[1], (B, 1, D), jnp.float32), 'context': jax.random.normal(ks[2], (B, LC, D), jnp.float32), 'src_mask': jnp.zeros((B, L), bool), 'ctx_mask': jnp.zeros((B, LC), bool), 'n1_w': jax.random.normal(ks[3], (NL, 2 * D, D), jnp.float32) * s, 'n1_b': jnp.zeros((NL, 2 * D), jnp.float32), 'n2_w': jax.random.normal(ks[4], (NL, 2 * D, D), jnp.float32) * s, 'n2_b': jnp.zeros((NL, 2 * D), jnp.float32), 'n3_w': jax.random.normal(ks[5], (NL, 2 * D, D), jnp.float32) * s, 'n3_b': jnp.zeros((NL, 2 * D), jnp.float32), 'qkv_w': jax.random.normal(ks[6], (NL, 3 * D, D), jnp.float32) * s, 'so_w': jax.random.normal(ks[7], (NL, D, D), jnp.float32) * s, 'cq_w': jax.random.normal(ks[8], (NL, D, D), jnp.float32) * s, 'ck_w': jax.random.normal(ks[9], (NL, D, D), jnp.float32) * s, 'cv_w': jax.random.normal(ks[10], (NL, D, D), jnp.float32) * s, 'co_w': jax.random.normal(ks[11], (NL, D, D), jnp.float32) * s, 'f1_w': jax.random.normal(ks[12], (NL, DFF, D), jnp.float32) * s, 'f1_b': jnp.zeros((NL, DFF), jnp.float32), 'f2_w': jax.random.normal(ks[13], (NL, D, DFF), jnp.float32) * s, 'f2_b': jnp.zeros((NL, D), jnp.float32)}
        return inp
    _L1_xcond_all = _L1_xcond_setup()
    _L1_xcond_in = {k: v for k, v in _L1_xcond_all.items() if k in ('n1_w', 'n1_b', 'n2_w', 'n2_b', 'n3_w', 'n3_b', 'qkv_w', 'so_w', 'cq_w', 'ck_w', 'cv_w', 'co_w', 'f1_w', 'f1_b', 'f2_w', 'f2_b')}
    del _L1_xcond_all

    def _L1_ffn_setup():
        import jax, jax.numpy as jnp
        import numpy as np
        EPS = 1e-05

        def layernorm(x, w, b):
            mu = jnp.mean(x, axis=-1, keepdims=True)
            var = jnp.mean(jnp.square(x - mu), axis=-1, keepdims=True)
            return (x - mu) * jax.lax.rsqrt(var + EPS) * w + b

        def act_quant_fake(x):
            scale = 127.0 / jnp.clip(jnp.max(jnp.abs(x), axis=-1, keepdims=True), EPS, None)
            return jnp.clip(jnp.round(x * scale), -128.0, 127.0) / scale

        def weight_quant_fake(w):
            scale = 1.0 / jnp.clip(jnp.mean(jnp.abs(w)), EPS, None)
            return jnp.clip(jnp.round(w * scale), -1.0, 1.0) / scale

        def bitlinear(x, w, b):
            dqx = x + jax.lax.stop_gradient(act_quant_fake(x) - x)
            dqw = w + jax.lax.stop_gradient(weight_quant_fake(w) - w)
            return jnp.einsum('btd,hd->bth', dqx, dqw) + b
        key = jax.random.key(seed)
        ks = jax.random.split(key, 5)
        dim, hidden = (128, 512)
        B, T = (8, 256)
        return {'x': jax.random.normal(ks[0], (B, T, dim), dtype=jnp.float32), 'ln1_w': jnp.ones((dim,), jnp.float32), 'ln1_b': jnp.zeros((dim,), jnp.float32), 'w1': jax.random.normal(ks[1], (hidden, dim), jnp.float32) * (1.0 / np.sqrt(dim)), 'b1': jax.random.normal(ks[2], (hidden,), jnp.float32) * 0.01, 'ln2_w': jnp.ones((hidden,), jnp.float32), 'ln2_b': jnp.zeros((hidden,), jnp.float32), 'w2': jax.random.normal(ks[3], (dim, hidden), jnp.float32) * (1.0 / np.sqrt(hidden)), 'b2': jax.random.normal(ks[4], (dim,), jnp.float32) * 0.01}
    _L1_ffn_all = _L1_ffn_setup()
    _L1_ffn_in = {k: v for k, v in _L1_ffn_all.items() if k in ('ln1_w', 'ln1_b', 'w1', 'b1', 'ln2_w', 'ln2_b', 'w2', 'b2')}
    del _L1_ffn_all
    return {'x': x, 'cond_1024': cond_1024, 'ctx_1024': ctx_1024, 'mask_BxS_bf0': mask_BxS_bf0, 'mask_BxS2_bf0': mask_BxS2_bf0, 'L0_xcond_q_mu': _L0_xcond_in['q_mu'], 'L0_xcond_q_logsig': _L0_xcond_in['q_logsig'], 'L0_xcond_lnkv_g': _L0_xcond_in['lnkv_g'], 'L0_xcond_lnkv_b': _L0_xcond_in['lnkv_b'], 'L0_xcond_lnq_g': _L0_xcond_in['lnq_g'], 'L0_xcond_lnq_b': _L0_xcond_in['lnq_b'], 'L0_xcond_lnm_g': _L0_xcond_in['lnm_g'], 'L0_xcond_lnm_b': _L0_xcond_in['lnm_b'], 'L0_xcond_lnp_g': _L0_xcond_in['lnp_g'], 'L0_xcond_lnp_b': _L0_xcond_in['lnp_b'], 'L0_xcond_wk': _L0_xcond_in['wk'], 'L0_xcond_bk': _L0_xcond_in['bk'], 'L0_xcond_wv': _L0_xcond_in['wv'], 'L0_xcond_bv': _L0_xcond_in['bv'], 'L0_xcond_wq': _L0_xcond_in['wq'], 'L0_xcond_bq': _L0_xcond_in['bq'], 'L0_xcond_wu': _L0_xcond_in['wu'], 'L0_xcond_bu': _L0_xcond_in['bu'], 'L0_xcond_w1': _L0_xcond_in['w1'], 'L0_xcond_b1': _L0_xcond_in['b1'], 'L0_xcond_w2': _L0_xcond_in['w2'], 'L0_xcond_b2': _L0_xcond_in['b2'], 'L0_ffn_w_g': _L0_ffn_in['w_g'], 'L0_ffn_c_fc': _L0_ffn_in['c_fc'], 'L0_ffn_c_proj': _L0_ffn_in['c_proj'], 'L1_xcond_n1_w': _L1_xcond_in['n1_w'], 'L1_xcond_n1_b': _L1_xcond_in['n1_b'], 'L1_xcond_n2_w': _L1_xcond_in['n2_w'], 'L1_xcond_n2_b': _L1_xcond_in['n2_b'], 'L1_xcond_n3_w': _L1_xcond_in['n3_w'], 'L1_xcond_n3_b': _L1_xcond_in['n3_b'], 'L1_xcond_qkv_w': _L1_xcond_in['qkv_w'], 'L1_xcond_so_w': _L1_xcond_in['so_w'], 'L1_xcond_cq_w': _L1_xcond_in['cq_w'], 'L1_xcond_ck_w': _L1_xcond_in['ck_w'], 'L1_xcond_cv_w': _L1_xcond_in['cv_w'], 'L1_xcond_co_w': _L1_xcond_in['co_w'], 'L1_xcond_f1_w': _L1_xcond_in['f1_w'], 'L1_xcond_f1_b': _L1_xcond_in['f1_b'], 'L1_xcond_f2_w': _L1_xcond_in['f2_w'], 'L1_xcond_f2_b': _L1_xcond_in['f2_b'], 'L1_ffn_ln1_w': _L1_ffn_in['ln1_w'], 'L1_ffn_ln1_b': _L1_ffn_in['ln1_b'], 'L1_ffn_w1': _L1_ffn_in['w1'], 'L1_ffn_b1': _L1_ffn_in['b1'], 'L1_ffn_ln2_w': _L1_ffn_in['ln2_w'], 'L1_ffn_ln2_b': _L1_ffn_in['ln2_b'], 'L1_ffn_w2': _L1_ffn_in['w2'], 'L1_ffn_b2': _L1_ffn_in['b2']}

def reference(x, cond_1024, ctx_1024, mask_BxS_bf0, mask_BxS2_bf0, L0_xcond_q_mu, L0_xcond_q_logsig, L0_xcond_lnkv_g, L0_xcond_lnkv_b, L0_xcond_lnq_g, L0_xcond_lnq_b, L0_xcond_lnm_g, L0_xcond_lnm_b, L0_xcond_lnp_g, L0_xcond_lnp_b, L0_xcond_wk, L0_xcond_bk, L0_xcond_wv, L0_xcond_bv, L0_xcond_wq, L0_xcond_bq, L0_xcond_wu, L0_xcond_bu, L0_xcond_w1, L0_xcond_b1, L0_xcond_w2, L0_xcond_b2, L0_ffn_w_g, L0_ffn_c_fc, L0_ffn_c_proj, L1_xcond_n1_w, L1_xcond_n1_b, L1_xcond_n2_w, L1_xcond_n2_b, L1_xcond_n3_w, L1_xcond_n3_b, L1_xcond_qkv_w, L1_xcond_so_w, L1_xcond_cq_w, L1_xcond_ck_w, L1_xcond_cv_w, L1_xcond_co_w, L1_xcond_f1_w, L1_xcond_f1_b, L1_xcond_f2_w, L1_xcond_f2_b, L1_ffn_ln1_w, L1_ffn_ln1_b, L1_ffn_w1, L1_ffn_b1, L1_ffn_ln2_w, L1_ffn_ln2_b, L1_ffn_w2, L1_ffn_b2):
    import jax
    import jax.numpy as jnp

    def _L0_xcond_ref(x_cls, x, noise, q_mu, q_logsig, lnkv_g, lnkv_b, lnq_g, lnq_b, lnm_g, lnm_b, lnp_g, lnp_b, wk, bk, wv, bv, wq, bq, wu, bu, w1, b1, w2, b2):
        import jax, jax.numpy as jnp
        import numpy as np
        B, N, K, D, T = (16, 512, 16, 128, 3)
        EPS_ATTN = 1e-08
        LN_EPS = 1e-05

        def _ln(x, g, b):
            mu = jnp.mean(x, axis=-1, keepdims=True)
            var = jnp.mean(jnp.square(x - mu), axis=-1, keepdims=True)
            return (x - mu) * jax.lax.rsqrt(var + LN_EPS) * g + b
        scale = D ** (-0.5)
        x_in = _ln(x, lnkv_g, lnkv_b)
        k = x_in @ wk + bk
        v = x_in @ wv + bv
        slots = q_mu + jnp.exp(q_logsig) * noise
        for _ in range(T):
            prev = slots
            q = _ln(slots, lnq_g, lnq_b) @ wq + bq
            logits = jnp.einsum('bnd,bkd->bnk', k, q) / scale
            attn = jax.nn.softmax(logits, axis=-1) + EPS_ATTN
            attn = attn / jnp.sum(attn, axis=1, keepdims=True)
            upd = jnp.einsum('bnk,bnd->bkd', attn, v)
            slots = upd @ wu + bu + prev
            h = _ln(slots, lnm_g, lnm_b) @ w1 + b1
            slots = jax.nn.gelu(h, approximate=False) @ w2 + b2 + slots
            slots = _ln(slots + x_cls[:, None, :], lnp_g, lnp_b)
        return slots

    def _L0_ffn_ref(x, w_g, c_fc, c_proj):
        import jax, jax.numpy as jnp
        import numpy as np
        N_EXP = 8
        TOP_K = 2
        CAP_FACTOR = 1.25
        NEG_INF = -1000000000.0

        def _moe_forward(x, w_g, c_fc, c_proj):
            B, T, D = x.shape
            N = B * T
            xf = x.reshape(N, D)
            logits = xf @ w_g
            topv, topi = jax.lax.top_k(logits, TOP_K)
            full = jnp.full_like(logits, NEG_INF)
            full = full.at[jnp.arange(N)[:, None], topi].set(topv)
            probs = jax.nn.softmax(full, axis=-1)
            capacity = int(TOP_K * CAP_FACTOR * N / N_EXP)
            capacity += capacity % 2
            mask = jax.nn.one_hot(jnp.swapaxes(topi, 0, 1), N_EXP, dtype=jnp.int32)
            rank = jnp.cumsum(mask.reshape(TOP_K * N, N_EXP), axis=0).reshape(TOP_K, N, N_EXP) - 1
            mask = mask * (rank < capacity)
            rank_sel = jnp.sum(mask * rank, axis=-1)
            wts = jnp.sum(mask * probs[None], axis=-1)
            cb = jnp.zeros((N, N_EXP, capacity), x.dtype)
            tok = jnp.arange(N)
            for k in range(TOP_K):
                cb = cb.at[tok, topi[:, k], rank_sel[k]].add(wts[k])
            sec_mask = (cb != 0).astype(x.dtype)
            exp_batches = jnp.einsum('nec,nd->ecd', sec_mask, xf)
            h = jax.nn.gelu(jnp.einsum('ecd,edh->ech', exp_batches, c_fc), approximate=False)
            exp_out = jnp.einsum('ech,ehd->ecd', h, c_proj)
            out = jnp.einsum('nec,ecd->nd', cb, exp_out)
            return out.reshape(B, T, D)
        return _moe_forward(x, w_g, c_fc, c_proj)

    def _L1_xcond_ref(x, noise_emb, context, src_mask, ctx_mask, n1_w, n1_b, n2_w, n2_b, n3_w, n3_b, qkv_w, so_w, cq_w, ck_w, cv_w, co_w, f1_w, f1_b, f2_w, f2_b):
        import jax, jax.numpy as jnp
        import numpy as np
        NL, D, H, DFF = (6, 128, 16, 512)
        HD = D // H

        def _rope(x):
            L = x.shape[1]
            half = HD // 2
            inv = 1.0 / 10000.0 ** (jnp.arange(half, dtype=jnp.float32) / half)
            ang = jnp.arange(L, dtype=jnp.float32)[:, None] * inv
            cos = jnp.cos(ang)[None, :, None, :]
            sin = jnp.sin(ang)[None, :, None, :]
            x1, x2 = (x[..., :half], x[..., half:])
            return jnp.concatenate([x1 * cos - x2 * sin, x1 * sin + x2 * cos], axis=-1)

        def _ln(x, eps=1e-05):
            m = jnp.mean(x, axis=-1, keepdims=True)
            v = jnp.var(x, axis=-1, keepdims=True)
            return (x - m) * jax.lax.rsqrt(v + eps)

        def _adaln(x, emb, w, b):
            gb = emb[:, 0, :] @ w.T + b
            g, be = jnp.split(gb, 2, axis=-1)
            return _ln(x) * (1.0 + g[:, None, :]) + be[:, None, :]

        def _attn(q, k, v, mask):
            scores = jnp.einsum('bqhd,bkhd->bhqk', q, k) / np.float32(np.sqrt(HD))
            scores = jnp.where(mask[:, None, None, :], jnp.float32(-jnp.inf), scores)
            w = jax.nn.softmax(scores, axis=-1)
            return jnp.einsum('bhqk,bkhd->bqhd', w, v)
        B, L, _ = x.shape
        LC = context.shape[1]
        for i in range(NL):
            xn = _adaln(x, noise_emb, n1_w[i], n1_b[i])
            qkv = xn @ qkv_w[i].T
            q, k, v = jnp.split(qkv, 3, axis=-1)
            q = _rope(q.reshape(B, L, H, HD))
            k = _rope(k.reshape(B, L, H, HD))
            v = v.reshape(B, L, H, HD)
            a = _attn(q, k, v, src_mask).reshape(B, L, D) @ so_w[i].T
            x = x + a
            xn = _adaln(x, noise_emb, n2_w[i], n2_b[i])
            q = _rope((xn @ cq_w[i].T).reshape(B, L, H, HD))
            k = _rope((context @ ck_w[i].T).reshape(B, LC, H, HD))
            v = (context @ cv_w[i].T).reshape(B, LC, H, HD)
            a = _attn(q, k, v, ctx_mask).reshape(B, L, D) @ co_w[i].T
            x = x + a
            xn = _adaln(x, noise_emb, n3_w[i], n3_b[i])
            h = jax.nn.gelu(xn @ f1_w[i].T + f1_b[i], approximate=False)
            x = x + (h @ f2_w[i].T + f2_b[i])
        return x

    def _L1_ffn_ref(x, ln1_w, ln1_b, w1, b1, ln2_w, ln2_b, w2, b2):
        import jax, jax.numpy as jnp
        import numpy as np
        EPS = 1e-05

        def layernorm(x, w, b):
            mu = jnp.mean(x, axis=-1, keepdims=True)
            var = jnp.mean(jnp.square(x - mu), axis=-1, keepdims=True)
            return (x - mu) * jax.lax.rsqrt(var + EPS) * w + b

        def act_quant_fake(x):
            scale = 127.0 / jnp.clip(jnp.max(jnp.abs(x), axis=-1, keepdims=True), EPS, None)
            return jnp.clip(jnp.round(x * scale), -128.0, 127.0) / scale

        def weight_quant_fake(w):
            scale = 1.0 / jnp.clip(jnp.mean(jnp.abs(w)), EPS, None)
            return jnp.clip(jnp.round(w * scale), -1.0, 1.0) / scale

        def bitlinear(x, w, b):
            dqx = x + jax.lax.stop_gradient(act_quant_fake(x) - x)
            dqw = w + jax.lax.stop_gradient(weight_quant_fake(w) - w)
            return jnp.einsum('btd,hd->bth', dqx, dqw) + b
        h = layernorm(x, ln1_w, ln1_b)
        h = bitlinear(h, w1, b1)
        h = jax.nn.gelu(h, approximate=False)
        h = layernorm(h, ln2_w, ln2_b)
        out = bitlinear(h, w2, b2)
        return out
    x = x + _L0_xcond_ref(cond_1024, ctx_1024, _layernorm(x, axis=-1), L0_xcond_q_mu, L0_xcond_q_logsig, L0_xcond_lnkv_g, L0_xcond_lnkv_b, L0_xcond_lnq_g, L0_xcond_lnq_b, L0_xcond_lnm_g, L0_xcond_lnm_b, L0_xcond_lnp_g, L0_xcond_lnp_b, L0_xcond_wk, L0_xcond_bk, L0_xcond_wv, L0_xcond_bv, L0_xcond_wq, L0_xcond_bq, L0_xcond_wu, L0_xcond_bu, L0_xcond_w1, L0_xcond_b1, L0_xcond_w2, L0_xcond_b2)
    x = x + _L0_ffn_ref(_layernorm(x, axis=-1), L0_ffn_w_g, L0_ffn_c_fc, L0_ffn_c_proj)
    x = x + _L1_xcond_ref(_layernorm(x, axis=-1), cond_1024[:, None, :], ctx_1024, mask_BxS_bf0, mask_BxS2_bf0, L1_xcond_n1_w, L1_xcond_n1_b, L1_xcond_n2_w, L1_xcond_n2_b, L1_xcond_n3_w, L1_xcond_n3_b, L1_xcond_qkv_w, L1_xcond_so_w, L1_xcond_cq_w, L1_xcond_ck_w, L1_xcond_cv_w, L1_xcond_co_w, L1_xcond_f1_w, L1_xcond_f1_b, L1_xcond_f2_w, L1_xcond_f2_b)
    x = x + _L1_ffn_ref(_layernorm(x, axis=-1), L1_ffn_ln1_w, L1_ffn_ln1_b, L1_ffn_w1, L1_ffn_b1, L1_ffn_ln2_w, L1_ffn_ln2_b, L1_ffn_w2, L1_ffn_b2)
    return x

_drawn_inputs = setup_inputs


def setup_inputs(seed=0):
    import zlib

    import numpy as np

    out = dict(_drawn_inputs(seed))
    spreads = {'L0_xcond_lnkv_g': (1.0, 0.6),
     'L0_xcond_lnkv_b': (0.0, 2.0),
     'L0_xcond_lnq_g': (1.0, 0.6),
     'L0_xcond_lnq_b': (0.0, 2.0),
     'L0_xcond_lnm_g': (1.0, 0.6),
     'L0_xcond_lnm_b': (0.0, 0.8),
     'L0_xcond_lnp_g': (1.0, 0.2),
     'L0_xcond_lnp_b': (0.0, 0.1),
     'L0_xcond_bk': (0.0, 2.0),
     'L0_xcond_bv': (0.0, 0.602),
     'L0_xcond_bq': (0.0, 2.0),
     'L0_xcond_bu': (0.0, 0.1),
     'L0_xcond_b1': (0.0, 0.8),
     'L0_xcond_b2': (0.0, 0.1),
     'L1_xcond_n1_b': (0.0, 0.8),
     'L1_xcond_n2_b': (0.0, 2.0),
     'L1_xcond_n3_b': (0.0, 0.8),
     'L1_xcond_f1_b': (0.0, 0.352),
     'L1_xcond_f2_b': (0.0, 0.1),
     'L1_ffn_ln1_w': (1.0, 0.2),
     'L1_ffn_ln1_b': (0.0, 0.284),
     'L1_ffn_ln2_w': (1.0, 0.2),
     'L1_ffn_ln2_b': (0.0, 0.318)}
    factors = {'L0_xcond_q_logsig': 8.0,
     'L0_xcond_wk': 200.0,
     'L0_xcond_wq': 200.0,
     'L0_xcond_w1': 3.311,
     'L0_xcond_w2': 3.276,
     'L0_ffn_w_g': 7.462,
     'L1_xcond_n1_w': 3.979,
     'L1_xcond_n2_w': 8.0,
     'L1_xcond_n3_w': 3.399,
     'L1_xcond_cq_w': 8.0,
     'L1_xcond_ck_w': 8.0,
     'L1_ffn_b1': 8.0,
     'L1_ffn_b2': 8.0}
    for name, (base, spread) in spreads.items():
        noise = np.random.default_rng([zlib.crc32(name.encode()), seed]).standard_normal(out[name].shape)
        drawn = base * np.exp(spread * noise) if base else spread * noise
        out[name] = jnp.asarray(drawn.astype(out[name].dtype))
    for name, factor in factors.items():
        out[name] = (out[name] * factor).astype(out[name].dtype)
    return out
```

```python
from contextlib import ExitStack, contextmanager

import numpy as np

import concourse.bass as bass
from concourse import mybir

ALU = mybir.AluOpType
ACT = mybir.ActivationFunctionType
AX = mybir.AxisListType
F32 = mybir.dt.float32
BF16 = mybir.dt.bfloat16
I32 = mybir.dt.int32
U8 = mybir.dt.uint8

P = 128
B, S, D = 4, 512, 128
TB = S // P
T = B * TB
N_CTX = 77
NC_ALL = B * N_CTX
SLOT_STEPS = 3
EXPERTS, HID, TOP_K = 8, 512, 2
CH = HID // P
CAPACITY = int(TOP_K * 1.25 * B * S / EXPERTS)
CAPACITY += CAPACITY % 2
LAYERS, HEADS, HD = 6, 16, 8
PAIRS = HEADS // 2
GROUPS = HEADS // 4
UNITS = B * GROUPS
LN_EPS = 1e-5
ROUND = 1.5 * 2.0 ** 23
MASKED = -1e30
RSQRT_SEED = 0x5F3759DF

PRODUCTS = 6
ROWS_HEAD = HD * PRODUCTS
ROW_MASK = 2 * ROWS_HEAD
ROW_SHIFT = ROW_MASK + 1
ROWS_MAX = ROW_SHIFT
ROWS_ALL = ROW_SHIFT + 6

SECTIONS = (("q", D), ("qr", D), ("k", D), ("kr", D), ("v", D), ("so", GROUPS * D), ("cq", D), ("cqr", D),
            ("ck", D), ("ckr", D), ("cv", D), ("co", GROUPS * D), ("f1", HID), ("f2", HID),
            ("n1", 2 * D), ("n2", 2 * D), ("n3", 2 * D))
COLS, _at = {}, 0
for _name, _width in SECTIONS:
    COLS[_name] = (_at, _at + _width)
    _at += _width
W_COLS = _at


class Memory:
    pass


class Statistics:
    pass


class Chain:

    def __init__(self, engine, sem):
        self.engine, self.sem, self.n = engine, sem, 0

    def link(self, instruction):
        self.n += 1
        instruction.then_inc(self.sem, 1)
        self.engine.wait_ge(self.sem, self.n)


def row_statistics(dve, chain, rows, tiles, width, st):
    n = rows.shape[0]
    for t in range(tiles):
        last = dve.bn_stats(st.bn[:n, t, :], rows[:, t, :])
    chain.link(last)
    for t in range(tiles):
        last = dve.bn_aggr(st.mv[:n, t, :], st.bn[:n, t, :])
    chain.link(last)
    var, a, r = st.var[:n, :tiles], st.tmp[:n, :tiles], st.rstd[:n, :tiles]
    chain.link(dve.tensor_scalar(var, st.mv[:n, :tiles, 1], LN_EPS, None, ALU.add))
    chain.link(dve.tensor_scalar(a.bitcast(I32), var.bitcast(I32), 1, None, ALU.arith_shift_right))
    chain.link(dve.tensor_scalar(r.bitcast(I32), a.bitcast(I32), -1.0, float(RSQRT_SEED), ALU.mult, ALU.add))
    for _ in range(4):
        chain.link(dve.tensor_tensor(a, r, r, ALU.mult))
        chain.link(dve.scalar_tensor_tensor(out=a, in0=a, scalar=-0.5, in1=var, op0=ALU.mult, op1=ALU.mult))
        chain.link(dve.scalar_tensor_tensor(out=r, in0=a, scalar=1.5, in1=r, op0=ALU.add, op1=ALU.mult))


def normalise(dve, out, rows, t, st):
    n = rows.shape[0]
    return dve.tensor_scalar(out[:, t, :], rows[:, t, :], st.mv[:n, t, 0:1], st.rstd[:n, t:t + 1],
                             ALU.subtract, ALU.mult)


@contextmanager
def stage(nc):
    with ExitStack() as ctx:
        sems = []

        def sem(name):
            sems.append(ctx.enter_context(nc.semaphore(name)))
            return sems[-1]

        yield sem
        for s in sems:
            nc.gpsimd.sem_clear(s)
        nc.all_engine_barrier()


def load_and_prepare(nc, a, m, sem):
    x_in, ctx_in, mats, rows_in, consts = sem("x_in"), sem("ctx_in"), sem("mats_in"), sem("rows_in"), sem("consts_in")
    ident, ident0, lnx, lnc, ctx_ps, ctx_sb, kv_ps, kv_sb = (sem(n) for n in (
        "identity", "identity_zero", "noise_ready", "ctx_normal", "ctx_turned", "ctx_copied", "kv_ready", "kv_copied"))
    sig, dch, pch = sem("sigma"), sem("prep_dve"), sem("prep_pool")
    vu_ps, neg, neg_out, shift_out = sem("value_ready"), sem("neg_mask"), sem("neg_mask_out"), sem("shift_rows_out")
    stack0, ones = sem("stack_zero"), sem("stack_one")

    with nc.Block() as block:
        @block.sync
        def _(sp):
            sp.dma_start(m.x[:], a["x"].rearrange("b (t p) d -> p (b t) d", p=P)).then_inc(x_in, 16)
            sp.dma_start(m.ctx[0:N_CTX], a["ctx"].rearrange("b n d -> n b d")).then_inc(ctx_in, 16)
            sp.dma_start(m.rows0[:], a["slot_rows"].partition_broadcast(P)).then_inc(rows_in, 16)
            sp.dma_start(m.cols0[:], a["slot_cols"]).then_inc(mats, 16)
            sp.dma_start(m.mats0[:], a["slot_mats"]).then_inc(mats, 16)
            sp.dma_start(m.cond_rows[:], a["cond"].rearrange("b d -> (b d)").partition_broadcast(P)).then_inc(consts, 16)
            sp.dma_start(m.condT[:], a["condT"]).then_inc(consts, 16)
            sp.dma_start(m.cos[:], a["cos"]).then_inc(consts, 16)
            sp.dma_start(m.sin[:], a["sin"]).then_inc(consts, 16)
            sp.dma_start(m.mask_u8[:], a["mask"]).then_inc(consts, 16)
            sp.dma_start(m.cmask_u8[:], a["cmask"]).then_inc(consts, 16)
            sp.wait_ge(neg, 2)
            sp.dma_start(a["neg_mask"], m.negmask[:]).then_inc(neg_out, 16)
            sp.dma_start(a["neg_cmask"], m.negcmask[:]).then_inc(neg_out, 16)
            sp.wait_ge(neg_out, 32)
            sp.wait_ge(stack0, 3)
            sp.wait_ge(pch, 3)
            for i in range(2):
                sp.dma_start(m.k6[ROW_SHIFT:ROWS_ALL, i], m.shift_rows[:]).then_inc(shift_out, 16)
            for b in range(B):
                sp.dma_start(m.kc6[ROW_SHIFT:ROWS_ALL, b], m.shift_rows[:, :, 0:N_CTX]).then_inc(shift_out, 16)
                sp.dma_start(m.kc6[ROW_MASK:ROW_MASK + 1, b],
                             a["neg_cmask"][b:b + 1, :].unsqueeze(1).to_broadcast([1, HEADS, N_CTX])).then_inc(shift_out, 16)
            sp.wait_ge(shift_out, 16 * (2 + 2 * B))
            sp.wait_ge(consts, 96)

        @block.gpsimd
        def _(pool):
            chain = Chain(pool, pch)
            pool.memset(m.ident[:], 0.0).then_inc(ident0, 1)
            pool.wait_ge(ident0, 1)
            pool.affine_select(out=m.ident[:], in_=m.ident[:], compare_op=ALU.not_equal, fill=1.0, base=0,
                               pattern=[[-1, P]], channel_multiplier=1).then_inc(ident, 1)
            pool.wait_ge(ident, 1)
            pool.tensor_copy(m.ident_bf[:], m.ident[:]).then_inc(ident, 1)
            chain.link(pool.memset(m.shift_rows[:], -1.0))
            by_pair = m.shift_rows[:].rearrange("r (i u) n -> r i u n", u=2)
            chain.link(pool.affine_select(out=by_pair[:, :, 0, :], in_=by_pair[:, :, 0, :], compare_op=ALU.is_ge,
                                          fill=0.0, base=2, pattern=[[0, PAIRS], [0, S]], channel_multiplier=-1))
            chain.link(pool.affine_select(out=by_pair[:, :, 1, :], in_=by_pair[:, :, 1, :], compare_op=ALU.is_ge,
                                          fill=0.0, base=-3, pattern=[[0, PAIRS], [0, S]], channel_multiplier=1))
            chain.link(pool.memset(m.tri[:], 1.0))
            chain.link(pool.affine_select(out=m.tri[:], in_=m.tri[:], compare_op=ALU.is_ge, fill=0.0, base=0,
                                          pattern=[[1, P]], channel_multiplier=-1))
            chain.link(pool.memset(m.spread[:], 0.0))
            quad = m.spread[:].rearrange("p (j r) -> p j r", r=32)
            chain.link(pool.affine_select(out=quad, in_=quad, compare_op=ALU.not_equal, fill=1.0, base=-HD,
                                          pattern=[[-32, 4], [0, 32]], channel_multiplier=1))
            for e in range(EXPERTS):
                last = pool.memset(m.prefer[:, e:e + 1], float(EXPERTS - e))
            chain.link(last)

        @block.scalar
        def _(act):
            act.wait_ge(rows_in, 16)
            nc.scalar.activation(m.sigma[:], m.rows0[:, 1, :], ACT.Exp).then_inc(sig, 1)
            act.wait_ge(mats, 32)
            act.wait_ge(ctx_ps, 1)
            nc.scalar.activation(m.ctxn[:], m.ps[:, 0, 0:NC_ALL], ACT.Identity, bias=m.cols0[:, 1:2],
                                 scale=m.cols0[:, 0:1]).then_inc(ctx_sb, 1)
            act.wait_ge(ctx_ps, 2)
            nc.scalar.copy(m.ctxT[:], m.ps[:, 1, 0:NC_ALL]).then_inc(ctx_sb, 1)
            act.wait_ge(kv_ps, 1)
            nc.scalar.activation(m.slot_k[:], m.ps[:, 2, 0:NC_ALL], ACT.Identity, bias=m.cols0[:, 6:7]).then_inc(kv_sb, 1)
            act.wait_ge(kv_ps, 2)
            nc.scalar.activation(m.slot_vT[:], m.ps[:, 3, 0:NC_ALL], ACT.Identity, bias=m.cols0[:, 7:8]).then_inc(kv_sb, 1)
            act.wait_ge(vu_ps, 1)
            nc.scalar.copy(m.slot_v[0:N_CTX, :, 0:D], m.ps[0:N_CTX, 4, :].rearrange("n (b d) -> n b d", b=B)).then_inc(kv_sb, 1)

        @block.tensor
        def _(pe):
            pe.wait_ge(ident, 2)
            pe.wait_ge(lnc, 1)
            for b in range(B):
                last = nc.tensor.transpose(m.ps[:, 0, b * N_CTX:(b + 1) * N_CTX], m.ctx_hat[0:N_CTX, b, :], m.ident[0:N_CTX, 0:N_CTX])
            last.then_inc(ctx_ps, 1)
            for b in range(B):
                last = nc.tensor.transpose(m.ps[:, 1, b * N_CTX:(b + 1) * N_CTX], m.ctx[0:N_CTX, b, :], m.ident[0:N_CTX, 0:N_CTX])
            last.then_inc(ctx_ps, 1)
            pe.wait_ge(mats, 32)
            pe.wait_ge(ctx_sb, 1)
            nc.tensor.matmul(m.ps[:, 2, 0:NC_ALL], m.mats0[:, 0, :], m.ctxn[:], start=True, stop=True).then_inc(kv_ps, 1)
            nc.tensor.matmul(m.ps[:, 3, 0:NC_ALL], m.mats0[:, 1, :], m.ctxn[:], start=True, stop=True).then_inc(kv_ps, 1)
            pe.wait_ge(kv_sb, 2)
            for b in range(B):
                last = nc.tensor.matmul(m.ps[0:N_CTX, 4, b * D:(b + 1) * D], m.slot_vT[:, b * N_CTX:(b + 1) * N_CTX],
                                        m.mats0[:, 3, :], start=True, stop=True)
            last.then_inc(vu_ps, 1)

        @block.vector
        def _(dve):
            chain = Chain(dve, dch)
            dve.memset(m.k6[:], 0.0).then_inc(stack0, 1)
            dve.memset(m.kc6[:], 0.0).then_inc(stack0, 1)
            dve.memset(m.q6[:], 0.0).then_inc(stack0, 1)
            dve.wait_ge(stack0, 3)
            dve.memset(m.q6[ROW_MASK:ROW_MASK + 1], 1.0)
            dve.memset(m.vaug[:], 0.0)
            dve.memset(m.vcaug[:], 0.0)
            dve.memset(m.slot_v[:, :, D:D + 1], 1.0)
            chain.link(dve.memset(m.ones[:], 1.0))
            dve.memset(m.vaug[:, :, :, :, HD:HD + 1], 1.0)
            chain.link(dve.memset(m.vcaug[:, :, :, HD:HD + 1], 1.0))
            dve.wait_ge(consts, 96)
            dve.tensor_scalar(m.negmask[:], m.mask_u8[:], MASKED, None, ALU.mult).then_inc(neg, 1)
            dve.tensor_scalar(m.negcmask[:], m.cmask_u8[:], MASKED, None, ALU.mult).then_inc(neg, 1)
            dve.wait_ge(ctx_in, 16)
            row_statistics(dve, chain, m.ctx[0:N_CTX], B, D, m.st)
            for b in range(B):
                last = normalise(dve, m.ctx_hat[0:N_CTX], m.ctx[0:N_CTX], b, m.st)
            last.then_inc(lnc, 1)
            dve.wait_ge(lnc, 1)
            dve.wait_ge(x_in, 16)
            row_statistics(dve, chain, m.x[:], T, D, m.st)
            for t in range(T):
                last = normalise(dve, m.hat[:], m.x[:], t, m.st)
            chain.link(last)
            dve.wait_ge(sig, 1)
            chain.link(dve.tensor_tensor(m.hat[:], m.hat[:], m.sigma[:].unsqueeze(1).to_broadcast([P, T, D]), ALU.mult))
            chain.link(dve.tensor_tensor(m.state[:], m.hat[:], m.rows0[:, 0:1, :].to_broadcast([P, T, D]), ALU.add))
            dve.tensor_tensor(m.cond_rows[:], m.cond_rows[:], m.rows0[:, 5:6, :].to_broadcast([P, B, D]), ALU.add).then_inc(lnx, 1)


def slot_step(nc, a, m, sem):
    names = ("sl_dve", "sl_hat", "sl_turned", "sl_qin", "sl_q_ps", "sl_q", "sl_logits", "sl_max", "sl_p", "sl_attn",
             "sl_upd", "sl_new", "sl_biased")
    (dch, hat, turned, qin, q_ps, q_sb, logits, mx, probs, attn, upd, new, biased) = [sem(n) for n in names]
    scale = float(np.float32(1.0) / np.float32(D ** -0.5))
    with nc.Block() as block:
        @block.gpsimd
        def _(pool):
            pool.wait_ge(hat, B)
            nc.gpsimd.tensor_tensor(m.state[:], m.state[:], m.rows0[:, 4:5, :].to_broadcast([P, T, D]), ALU.add).then_inc(biased, 1)

        @block.tensor
        def _(pe):
            for b in range(B):
                pe.wait_ge(hat, b + 1)
                for t in range(TB):
                    last = nc.tensor.transpose(m.ps[:, b % 2, t * P:(t + 1) * P], m.hat[:, b * TB + t, :], m.ident[:])
                last.then_inc(turned, 1)
                pe.wait_ge(qin, b + 1)
                nc.tensor.matmul(m.ps[:, 2 + b % 2, :], m.mats0[:, 2, :], m.xnT[:, b, :], start=True, stop=True).then_inc(q_ps, 1)
                pe.wait_ge(q_sb, b + 1)
                nc.tensor.matmul(m.ps[0:N_CTX, 4 + b % 2, :], m.slot_k[:, b * N_CTX:(b + 1) * N_CTX], m.qT[:, b, :],
                                 start=True, stop=True).then_inc(logits, 1)
            for b in range(B):
                pe.wait_ge(attn, b + 1)
                for t in range(TB):
                    pe_bank = 6 + t % 2
                    if b * TB + t >= 2:
                        pe.wait_ge(new, b * TB + t - 1)
                    nc.tensor.matmul(m.ps[:, pe_bank, 0:D + 1], m.attn[0:N_CTX, b, t * P:(t + 1) * P], m.slot_v[0:N_CTX, b, :],
                                     start=True, stop=True).then_inc(upd, 1)

        @block.scalar
        def _(act):
            for b in range(B):
                act.wait_ge(turned, b + 1)
                nc.scalar.activation(m.xnT[:, b, :], m.ps[:, b % 2, :], ACT.Identity, bias=m.cols0[:, 3:4],
                                     scale=m.cols0[:, 2:3]).then_inc(qin, 1)
                act.wait_ge(q_ps, b + 1)
                nc.scalar.activation(m.qT[:, b, :], m.ps[:, 2 + b % 2, :], ACT.Identity, bias=m.cols0[:, 8:9]).then_inc(q_sb, 1)
                act.wait_ge(mx, b + 1)
                nc.scalar.activation(m.attn[0:N_CTX, b, :], m.ps[0:N_CTX, 4 + b % 2, :], ACT.Exp, bias=m.negmx[0:N_CTX, b:b + 1],
                                     scale=scale, accum_out=m.psum_rows[0:N_CTX, b:b + 1]).then_inc(probs, 1)

        @block.vector
        def _(dve):
            chain = Chain(dve, dch)
            row_statistics(dve, chain, m.state[:], T, D, m.st)
            for b in range(B):
                for t in range(TB):
                    last = normalise(dve, m.hat[:], m.state[:], b * TB + t, m.st)
                last.then_inc(hat, 1)
            for b in range(B):
                dve.wait_ge(logits, b + 1)
                chain.link(nc.vector.reduce_max(m.rowmx[0:N_CTX, b:b + 1], m.ps[0:N_CTX, 4 + b % 2, :], AX.X))
                nc.vector.tensor_scalar(m.negmx[0:N_CTX, b:b + 1], m.rowmx[0:N_CTX, b:b + 1], -scale, None, ALU.mult).then_inc(mx, 1)
                dve.wait_ge(probs, b + 1)
                chain.link(nc.vector.reciprocal(m.rowmx[0:N_CTX, b:b + 1], m.psum_rows[0:N_CTX, b:b + 1]))
                nc.vector.tensor_scalar(m.attn[0:N_CTX, b, :], m.attn[0:N_CTX, b, :], m.rowmx[0:N_CTX, b:b + 1], 1e-8,
                                        ALU.mult, ALU.add).then_inc(attn, 1)
            dve.wait_ge(biased, 1)
            for t in range(T):
                dve.wait_ge(upd, t + 1)
                bank = 6 + t % TB % 2
                chain.link(nc.vector.reciprocal(m.colsum[:, t:t + 1], m.ps[:, bank, D:D + 1]))
                nc.vector.scalar_tensor_tensor(out=m.state[:, t, :], in0=m.ps[:, bank, 0:D], scalar=m.colsum[:, t:t + 1],
                                               in1=m.state[:, t, :], op0=ALU.mult, op1=ALU.add).then_inc(new, 1)

    names = ("sm_dve", "sm_hat", "sm_turned", "sm_in", "sm_h_ps", "sm_h", "sm_out", "sm_added", "sm_normal", "sm_gained")
    (dch, hat, turned, hin, h_ps, h_sb, out_ps, added, normal, gained) = [sem(n) for n in names]
    with nc.Block() as block:
        @block.tensor
        def _(pe):
            for b in range(B):
                pe.wait_ge(hat, b + 1)
                for t in range(TB):
                    last = nc.tensor.transpose(m.ps[:, b % 2, t * P:(t + 1) * P], m.hat[:, b * TB + t, :], m.ident[:])
                last.then_inc(turned, 1)
                pe.wait_ge(hin, b + 1)
                nc.tensor.matmul(m.ps[:, 2 + b % 2, :], m.mats0[:, 4, :], m.xnT[:, b, :], start=True, stop=True).then_inc(h_ps, 1)
                pe.wait_ge(h_sb, b + 1)
                for t in range(TB):
                    last = nc.tensor.matmul(m.ps[:, 4 + b, t * P:(t + 1) * P], m.qT[:, b, t * P:(t + 1) * P], m.mats0[:, 5, :],
                                            start=True, stop=True)
                last.then_inc(out_ps, 1)

        @block.scalar
        def _(act):
            for b in range(B):
                act.wait_ge(turned, b + 1)
                nc.scalar.activation(m.xnT[:, b, :], m.ps[:, b % 2, :], ACT.Identity, bias=m.cols0[:, 5:6],
                                     scale=m.cols0[:, 4:5]).then_inc(hin, 1)
                act.wait_ge(h_ps, b + 1)
                nc.scalar.activation(m.qT[:, b, :], m.ps[:, 2 + b % 2, :], ACT.Gelu, bias=m.cols0[:, 9:10]).then_inc(h_sb, 1)

        @block.gpsimd
        def _(pool):
            pool.wait_ge(hat, B)
            for b in range(B):
                last = nc.gpsimd.tensor_tensor(m.state[:, b * TB:(b + 1) * TB, :], m.state[:, b * TB:(b + 1) * TB, :],
                                               m.cond_rows[:, b:b + 1, :].to_broadcast([P, TB, D]), ALU.add)
            last.then_inc(added, 1)

        @block.vector
        def _(dve):
            chain = Chain(dve, dch)
            row_statistics(dve, chain, m.state[:], T, D, m.st)
            for b in range(B):
                for t in range(TB):
                    last = normalise(dve, m.hat[:], m.state[:], b * TB + t, m.st)
                last.then_inc(hat, 1)
            dve.wait_ge(added, 1)
            for b in range(B):
                dve.wait_ge(out_ps, b + 1)
                last = nc.vector.tensor_tensor(m.state[:, b * TB:(b + 1) * TB, :], m.state[:, b * TB:(b + 1) * TB, :],
                                               m.ps[:, 4 + b, :].rearrange("p (t d) -> p t d", t=TB), ALU.add)
            chain.link(last)
            row_statistics(dve, chain, m.state[:], T, D, m.st)
            for t in range(T):
                last = normalise(dve, m.hat[:], m.state[:], t, m.st)
            chain.link(last)
            chain.link(nc.vector.tensor_tensor(m.hat[:], m.hat[:], m.rows0[:, 2:3, :].to_broadcast([P, T, D]), ALU.mult))
            nc.vector.tensor_tensor(m.state[:], m.hat[:], m.rows0[:, 3:4, :].to_broadcast([P, T, D]), ALU.add).then_inc(normal, 1)


def route_tokens(nc, a, m, sem):
    (dch, hat, turned, xt, logit, first, second, counted, wg_in, gate) = [sem(n) for n in (
        "rt_dve", "rt_hat", "rt_turned", "rt_xT", "rt_logits", "rt_first", "rt_second", "rt_counted", "rt_wg", "rt_gate")]
    expd = sem("rt_exp")
    by_e = [P, T, EXPERTS]
    with nc.Block() as block:
        @block.sync
        def _(sp):
            sp.dma_start(m.wg[:], a["w_g"]).then_inc(wg_in, 16)
            sp.wait_ge(wg_in, 16)

        @block.tensor
        def _(pe):
            pe.wait_ge(wg_in, 16)
            for b in range(B):
                pe.wait_ge(hat, b + 1)
                for t in range(TB):
                    last = nc.tensor.transpose(m.ps[:, b, t * P:(t + 1) * P], m.hat[:, b * TB + t, :], m.ident[:])
                last.then_inc(turned, 1)
            for b in range(B):
                pe.wait_ge(xt, b + 1)
                for t in range(TB):
                    at = (b * TB + t) * EXPERTS
                    last = nc.tensor.matmul(m.ps[:, 4, at:at + EXPERTS], m.xnT[:, b, t * P:(t + 1) * P], m.wg[:], start=True, stop=True)
            last.then_inc(logit, 1)
            for k, chosen in enumerate((first, second)):
                pe.wait_ge(chosen, 1)
                nc.tensor.matmul(m.ps[:, 5 + k, 0:P], m.tri[:], m.onehot_bf[:, k, :, :], start=True, stop=True)
                nc.tensor.matmul(m.ps[:, 5 + k, P:2 * P], m.ones[:], m.onehot_bf[:, k, :, :], start=True, stop=True).then_inc(counted, 1)

        @block.scalar
        def _(act):
            for b in range(B):
                act.wait_ge(turned, b + 1)
                nc.scalar.copy(m.xnT[:, b, :], m.ps[:, b, :]).then_inc(xt, 1)
            act.wait_ge(gate, 1)
            nc.scalar.activation(m.gate[:], m.gate[:], ACT.Exp).then_inc(expd, 1)

        @block.vector
        def _(dve):
            chain = Chain(dve, dch)
            chain.link(nc.vector.tensor_tensor(m.x[:], m.x[:], m.state[:], ALU.add))
            row_statistics(dve, chain, m.x[:], T, D, m.st)
            for b in range(B):
                for t in range(TB):
                    last = normalise(dve, m.hat[:], m.x[:], b * TB + t, m.st)
                last.then_inc(hat, 1)
            dve.wait_ge(logit, 1)
            lg, top, pick, rest = m.logits, m.top, m.pick, m.rest
            chain.link(nc.vector.tensor_copy(lg[:], m.ps[:, 4, 0:T * EXPERTS].rearrange("p (t e) -> p t e", e=EXPERTS)))
            chain.link(nc.vector.tensor_copy(rest[:], lg[:]))
            for k, chosen in enumerate((first, second)):
                chain.link(nc.vector.tensor_reduce(top[:, k, :], rest[:], AX.X, ALU.max))
                chain.link(nc.vector.tensor_tensor(pick[:], rest[:], top[:, k, :].unsqueeze(2).to_broadcast(by_e), ALU.is_equal))
                chain.link(nc.vector.tensor_tensor(pick[:], pick[:], m.prefer[:].unsqueeze(1).to_broadcast(by_e), ALU.mult))
                chain.link(nc.vector.tensor_reduce(m.best[:], pick[:], AX.X, ALU.max))
                chain.link(nc.vector.tensor_tensor(m.onehot[:, k], pick[:], m.best[:].unsqueeze(2).to_broadcast(by_e), ALU.is_equal))
                nc.vector.tensor_copy(m.onehot_bf[:, k], m.onehot[:, k]).then_inc(chosen, 1)
                if k == 0:
                    chain.link(nc.vector.scalar_tensor_tensor(out=rest[:], in0=m.onehot[:, 0], scalar=-3e38, in1=lg[:],
                                                              op0=ALU.mult, op1=ALU.add))
            both = m.pick
            chain.link(nc.vector.tensor_tensor(both[:], m.onehot[:, 0], m.onehot[:, 1], ALU.add))
            chain.link(nc.vector.tensor_tensor(m.gate[:], lg[:], both[:], ALU.mult))
            chain.link(nc.vector.tensor_scalar(rest[:], both[:], 1e9, -1e9, ALU.mult, ALU.add))
            chain.link(nc.vector.tensor_tensor(m.gate[:], m.gate[:], rest[:], ALU.add))
            chain.link(nc.vector.tensor_reduce(m.best[:], m.gate[:], AX.X, ALU.max))
            nc.vector.tensor_tensor(m.gate[:], m.gate[:], m.best[:].unsqueeze(2).to_broadcast(by_e), ALU.subtract).then_inc(gate, 1)
            dve.wait_ge(expd, 1)
            chain.link(nc.vector.tensor_reduce(m.best[:], m.gate[:], AX.X, ALU.add))
            chain.link(nc.vector.reciprocal(m.best[:], m.best[:]))
            chain.link(nc.vector.tensor_tensor(m.gate[:], m.gate[:], m.best[:].unsqueeze(2).to_broadcast(by_e), ALU.mult))
            dve.wait_ge(counted, 2)
            for k in range(TOP_K):
                tot, run = m.rank[:, 0], m.rank[:, 1]
                chain.link(nc.vector.tensor_copy(tot, m.ps[:, 5 + k, P:2 * P].rearrange("p (t e) -> p t e", e=EXPERTS)))
                if k == 0:
                    chain.link(nc.vector.memset(run[:, 0:1, :], 0.0))
                else:
                    chain.link(nc.vector.tensor_copy(run[:, 0:1, :], m.total[:].unsqueeze(1)))
                for t in range(1, T):
                    chain.link(nc.vector.tensor_tensor(run[:, t, :], run[:, t - 1, :], tot[:, t - 1, :], ALU.add))
                chain.link(nc.vector.tensor_tensor(m.total[:], run[:, T - 1, :], tot[:, T - 1, :], ALU.add))
                chain.link(nc.vector.tensor_tensor(run, run, m.ps[:, 5 + k, 0:P].rearrange("p (t e) -> p t e", e=EXPERTS), ALU.add))
                chain.link(nc.vector.scalar_tensor_tensor(out=m.onehot[:, k], in0=run, scalar=float(CAPACITY) + 0.5,
                                                          in1=m.onehot[:, k], op0=ALU.is_lt, op1=ALU.mult))
            chain.link(nc.vector.tensor_tensor(m.onehot[:, 0], m.onehot[:, 0], m.onehot[:, 1], ALU.add))
            nc.vector.tensor_tensor(m.share[:].rearrange("p e t -> p t e"), m.gate[:], m.onehot[:, 0], ALU.mult)
            nc.vector.memset(m.state[:], 0.0)


def expert_pair(nc, a, m, sem, pair):
    (w_in, h_ps, h_sb, o_ps, o_sb, share) = [sem(n) for n in (
        "ex_weights", "ex_h_ready", "ex_h", "ex_out_ready", "ex_added", "ex_share")]
    steps = [(u, b) for u in range(2) for b in range(B)]
    with nc.Block() as block:
        @block.sync
        def _(sp):
            for u in range(2):
                sp.dma_start(m.fc[:, u], a["c_fc"][pair * 2 + u]).then_inc(w_in, 16)
                sp.dma_start(m.proj[:, u], a["c_proj"][pair * 2 + u]).then_inc(w_in, 16)
            sp.wait_ge(w_in, 64)

        @block.tensor
        def _(pe):
            pe.wait_ge(w_in, 64)

            def up(i):
                u, b = steps[i]
                for c in range(CH):
                    n = i * CH + c
                    if n >= 4:
                        pe.wait_ge(h_sb, n - 3)
                    nc.tensor.matmul(m.ps[:, n % 4, :], m.fc[:, u, c * P:(c + 1) * P], m.xnT[:, b, :], start=True, stop=True).then_inc(h_ps, 1)

            def down(i):
                u, b = steps[i]
                pe.wait_ge(h_sb, (i + 1) * CH)
                if i >= 2:
                    pe.wait_ge(o_sb, i - 1)
                for t in range(TB):
                    for c in range(CH):
                        last = nc.tensor.matmul(m.ps[:, 4 + i % 2, t * P:(t + 1) * P], m.hT[:, i % 2, c, t * P:(t + 1) * P],
                                                m.proj[:, u, c, :], start=(c == 0), stop=(c == CH - 1))
                last.then_inc(o_ps, 1)

            for i in range(len(steps) + 1):
                if i < len(steps):
                    up(i)
                if i >= 1:
                    down(i - 1)

        @block.scalar
        def _(act):
            for i in range(len(steps)):
                if i >= 2:
                    act.wait_ge(o_ps, i - 1)
                for c in range(CH):
                    act.wait_ge(h_ps, i * CH + c + 1)
                    nc.scalar.activation(m.hT[:, i % 2, c, :], m.ps[:, (i * CH + c) % 4, :], ACT.Gelu).then_inc(h_sb, 1)

        @block.vector
        def _(dve):
            nc.vector.tensor_copy(m.share2[:], m.share[:, bass.ts(pair, 2), :]).then_inc(share, 1)
            dve.wait_ge(share, 1)
            for i, (u, b) in enumerate(steps):
                dve.wait_ge(o_ps, i + 1)
                if u == 1 and b == 0:
                    dve.wait_ge(o_sb, B)
                for t in range(TB):
                    at = b * TB + t
                    last = nc.vector.scalar_tensor_tensor(out=m.state[:, at, :], in0=m.ps[:, 4 + i % 2, t * P:(t + 1) * P],
                                                          scalar=m.share2[:, u, at:at + 1], in1=m.state[:, at, :],
                                                          op0=ALU.mult, op1=ALU.add)
                last.then_inc(o_sb, 1)


def begin_layers(nc, a, m, sem):
    dch, start = sem("bl_dve"), sem("bl_start")
    with nc.Block() as block:
        @block.vector
        def _(dve):
            chain = Chain(dve, dch)
            chain.link(nc.vector.tensor_tensor(m.x[:], m.x[:], m.state[:], ALU.add))
            row_statistics(dve, chain, m.x[:], T, D, m.st)
            for t in range(T):
                last = normalise(dve, m.state[:], m.x[:], t, m.st)
            last.then_inc(start, 1)


def w_of(m, name):
    lo, hi = COLS[name]
    return m.w[:, lo:hi]


def project(nc, a, m, sem, layer, cross):
    tag = "c" if cross else "s"
    (w_in, ada_ps, ada, dch, hat, turned, xn, q_ps, rot, hi, low, mid, lo, out0, out1, v_ps, v_sb) = [
        sem(f"{tag}p_{n}") for n in ("weights", "ada_ready", "ada", "dve", "hat", "turned", "xn", "qk_ready", "rotated", "high",
                                     "less_high", "middle", "low", "stored0", "stored1", "v_ready", "v")]
    out = (out0, out1)
    norm = "n2" if cross else "n1"
    n_at = 1 if cross else 0
    nt = 1 if cross else 2
    wq, wqr = (w_of(m, "cq"), w_of(m, "cqr")) if cross else (w_of(m, "q"), w_of(m, "qr"))
    rounds = B + 1 if cross else B

    def view(i, tile):
        if cross and i == B:
            return tile[:, 0:1, 0:NC_ALL]
        return tile[:, 0:nt, :]

    with nc.Block() as block:
        @block.sync
        def _(sp):
            if not cross:
                sp.dma_start(m.w[:], a["w"][layer]).then_inc(w_in, 16)
                sp.dma_start(m.cols[:], a["cols"][layer]).then_inc(w_in, 16)
                sp.dma_start(m.f2b[:], a["f2_b"][layer].partition_broadcast(P)).then_inc(w_in, 16)
            for i in range(rounds):
                sp.wait_ge(lo, i + 1)
                if cross and i == B:
                    pk = m.parts[:, i % 2, 0, :, 0:NC_ALL]
                    dst = a["ctx_keys"]
                    sp.dma_start(dst[:, 0:3, :], pk[:, 0:1, :].to_broadcast([P, 3, NC_ALL])).then_inc(out[i % 2], 16)
                    sp.dma_start(dst[:, 3:5, :], pk[:, 1:2, :].to_broadcast([P, 2, NC_ALL])).then_inc(out[i % 2], 16)
                    sp.dma_start(dst[:, 5:6, :], pk[:, 2:3, :]).then_inc(out[i % 2], 16)
                    continue
                pq, dst = m.parts[:, i % 2, 0], a["queries"][i]
                sp.dma_start(dst[:, 0:3, :], pq[:, 0:3, :]).then_inc(out[i % 2], 16)
                sp.dma_start(dst[:, 3:5, :], pq[:, 0:2, :]).then_inc(out[i % 2], 16)
                sp.dma_start(dst[:, 5:6, :], pq[:, 0:1, :]).then_inc(out[i % 2], 16)
                if not cross:
                    pk, dst = m.parts[:, i % 2, 1], a["keys"][i]
                    sp.dma_start(dst[:, 0:3, :], pk[:, 0:1, :].to_broadcast([P, 3, S])).then_inc(out[i % 2], 16)
                    sp.dma_start(dst[:, 3:5, :], pk[:, 1:2, :].to_broadcast([P, 2, S])).then_inc(out[i % 2], 16)
                    sp.dma_start(dst[:, 5:6, :], pk[:, 2:3, :]).then_inc(out[i % 2], 16)
            sp.wait_ge(out0, 48 * nt * (B // 2) + (48 if cross else 0))
            sp.wait_ge(out1, 48 * nt * (B // 2))

        @block.tensor
        def _(pe):
            if not cross:
                pe.wait_ge(w_in, 48)
            lo_c = COLS[norm][0]
            for half in range(2):
                last = nc.tensor.matmul(m.ps[:, 7, half * B:(half + 1) * B], m.w[:, lo_c + half * D:lo_c + (half + 1) * D], m.condT[:],
                                        start=True, stop=True)
            last.then_inc(ada_ps, 1)

            def turn(i):
                pe.wait_ge(hat, i + 1)
                if i >= 2:
                    pe.wait_ge(xn, i - 1)
                for t in range(TB):
                    last = nc.tensor.transpose(m.ps[:, 5 + i % 2, t * P:(t + 1) * P], m.hat[:, i * TB + t, :], m.ident[:])
                last.then_inc(turned, 1)

            if cross:
                pe.wait_ge(ada, 1)
                for b in range(B):
                    last = nc.tensor.matmul(m.ps[0:N_CTX, 4, b * D:(b + 1) * D], m.ctxT[:, b * N_CTX:(b + 1) * N_CTX], w_of(m, "cv"),
                                            start=True, stop=True)
                last.then_inc(v_ps, 1)
            turn(0)
            for i in range(rounds):
                if i + 1 < B:
                    turn(i + 1)
                if i >= 1:
                    pe.wait_ge(rot, i)
                if cross and i == B:
                    nc.tensor.matmul(m.ps[:, 0, 0:NC_ALL], w_of(m, "ck"), m.ctxT[:], start=True, stop=True)
                    nc.tensor.matmul(m.ps[:, 2, 0:NC_ALL], w_of(m, "ckr"), m.ctxT[:], start=True, stop=True).then_inc(q_ps, 1)
                    continue
                pe.wait_ge(xn, i + 1)
                rhs = m.xnT[:, i, :]
                nc.tensor.matmul(m.ps[:, 0, :], wq, rhs, start=True, stop=True)
                last = nc.tensor.matmul(m.ps[:, 2, :], wqr, rhs, start=True, stop=True)
                if not cross:
                    nc.tensor.matmul(m.ps[:, 1, :], w_of(m, "k"), rhs, start=True, stop=True)
                    last = nc.tensor.matmul(m.ps[:, 3, :], w_of(m, "kr"), rhs, start=True, stop=True)
                last.then_inc(q_ps, 1)
                if not cross:
                    if i >= 1:
                        pe.wait_ge(v_sb, i)
                    for t in range(TB):
                        last = nc.tensor.matmul(m.ps[:, 4, t * P:(t + 1) * P], m.xnT[:, i, t * P:(t + 1) * P], w_of(m, "v"),
                                                start=True, stop=True)
                    last.then_inc(v_ps, 1)

        @block.scalar
        def _(act):
            if cross:
                act.wait_ge(v_ps, 1)
                nc.scalar.copy(m.vcaug[0:N_CTX, :, :, 0:HD],
                               m.ps[0:N_CTX, 4, :].rearrange("n (b h d) -> n b h d", b=B, d=HD)).then_inc(v_sb, 1)

            def scale_shift(i):
                act.wait_ge(turned, i + 1)
                if i == 0:
                    act.wait_ge(ada, 1)
                nc.scalar.activation(m.xnT[:, i, :], m.ps[:, 5 + i % 2, :], ACT.Identity, bias=m.ada[:, B + i:B + i + 1],
                                     scale=m.ada[:, i:i + 1]).then_inc(xn, 1)

            scale_shift(0)
            for i in range(rounds):
                if i + 1 < B:
                    scale_shift(i + 1)
                if not cross:
                    act.wait_ge(v_ps, i + 1)
                    nc.scalar.copy(m.vaug[:, i, :, :, 0:HD], m.ps[:, 4, :].rearrange("p (t h d) -> p t h d", t=TB, d=HD)).then_inc(v_sb, 1)
                act.wait_ge(rot, i + 1)
                if i >= 2:
                    act.wait_ge(out[i % 2], 48 * nt * (i // 2))
                parts, r = view(i, m.parts[:, i % 2, :, 0, :]), view(i, m.rot[:, i % 2])
                nc.scalar.copy(parts, r).then_inc(hi, 1)
                act.wait_ge(low, i + 1)
                nc.scalar.copy(view(i, m.parts[:, i % 2, :, 1, :]), view(i, m.left[:, i % 2])).then_inc(mid, 1)

        @block.gpsimd
        def _(pool):
            for i in range(rounds):
                pool.wait_ge(hi, i + 1)
                nc.gpsimd.tensor_tensor(view(i, m.left[:, i % 2]), view(i, m.rot[:, i % 2]), view(i, m.parts[:, i % 2, :, 0, :]),
                                        ALU.subtract).then_inc(low, 1)
                pool.wait_ge(mid, i + 1)
                nc.gpsimd.tensor_tensor(view(i, m.parts[:, i % 2, :, 2, :]), view(i, m.left[:, i % 2]), view(i, m.parts[:, i % 2, :, 1, :]),
                                        ALU.subtract).then_inc(lo, 1)

        @block.vector
        def _(dve):
            chain = Chain(dve, dch)
            if not cross:
                dve.wait_ge(w_in, 48)
            dve.wait_ge(ada_ps, 1)
            nc.vector.tensor_scalar(m.ada[:, 0:B], m.ps[:, 7, 0:B], m.cols[:, 2 * n_at:2 * n_at + 1], 1.0, ALU.add, ALU.add)
            nc.vector.tensor_scalar(m.ada[:, B:2 * B], m.ps[:, 7, B:2 * B], m.cols[:, 2 * n_at + 1:2 * n_at + 2], None, ALU.add).then_inc(ada, 1)
            row_statistics(dve, chain, m.state[:], T, D, m.st)
            for b in range(B):
                for t in range(TB):
                    last = normalise(dve, m.hat[:], m.state[:], b * TB + t, m.st)
                last.then_inc(hat, 1)
            for i in range(rounds):
                dve.wait_ge(q_ps, i + 1)
                if i >= 2:
                    dve.wait_ge(lo, i - 1)
                if cross and i == B:
                    shape = [P, B, N_CTX]
                    by_b = lambda ap: ap.rearrange("p (b n) -> p b n", b=B)
                    cos, sin = (t[:, 0:N_CTX].unsqueeze(1).to_broadcast(shape) for t in (m.cos, m.sin))
                    src, srcr = by_b(m.ps[:, 0, 0:NC_ALL]), by_b(m.ps[:, 2, 0:NC_ALL])
                    turned_, r = by_b(m.swap[:, 0, 0:NC_ALL]), by_b(m.rot[:, i % 2, 0, 0:NC_ALL])
                else:
                    shape = [P, nt, S]
                    cos, sin = (t[:].unsqueeze(1).to_broadcast(shape) for t in (m.cos, m.sin))
                    src, srcr = m.ps[:, 0:nt, :], m.ps[:, 2:2 + nt, :]
                    turned_, r = m.swap[:, 0:nt, :], m.rot[:, i % 2, 0:nt, :]
                nc.vector.tensor_tensor(r, src, cos, ALU.mult)
                chain.link(nc.vector.tensor_tensor(turned_, srcr, sin, ALU.mult))
                nc.vector.tensor_tensor(r, r, turned_, ALU.add).then_inc(rot, 1)
                dve.wait_ge(rot, i + 1)


def attend(nc, a, m, sem, cross):
    tag = "c" if cross else "s"
    (kq0, kq1, s_ready, s_read, maxima, mt_ps, mt_sb, m_rows, st_ready, probs, pv, sums_ready, u_sb, recip, on, o_ps, added, dch) = [
        sem(f"{tag}a_{n}") for n in ("stacked0", "stacked1", "max_scores", "max_read", "maxima", "shift_turned", "shift_copied",
                                     "shift_rows", "scores", "probs", "weighted", "sums_spread", "unit_copied",
                                     "sums_inverted", "unit_done", "projected", "added", "dve")]
    kq = (kq0, kq1)
    keys = N_CTX if cross else S
    kts = 1 if cross else TB
    kw = N_CTX if cross else P
    steps = 2 * kts
    pieces = TB if cross else 4 * TB
    per_step = pieces // steps
    loads = 1 if cross else 4
    wo = w_of(m, "co" if cross else "so")
    scale = float(np.float32(1.0) / np.float32(np.sqrt(HD)))
    st_bank, s_bank, pv_bank, aux = 0, 4, 6, 7
    total = UNITS * steps

    def k_of(b, h, lo, n):
        return m.kc6[:, b, h, lo:lo + n] if cross else m.k6[:, b % 2, h, lo:lo + n]

    def v_of(b, kt, h):
        return m.vcaug[0:kw, b, h, :] if cross else m.vaug[:, b, kt, h, :]

    with nc.Block() as block:
        @block.sync
        def _(sp):
            def load(b):
                if b >= 2:
                    sp.wait_ge(st_ready, (b - 1) * GROUPS * steps)
                sp.dma_start(m.q6[0:ROW_MASK, b % 2], a["queries"][b].rearrange("(i r) c n -> (r c) i n", i=PAIRS)).then_inc(kq[b % 2], 16)
                if cross:
                    return
                src = a["keys"][b].rearrange("(i u r) c n -> u (r c) i n", u=2, r=HD)
                for u in range(2):
                    dst = m.k6[u * ROWS_HEAD:(u + 1) * ROWS_HEAD, b % 2].rearrange("r (i u) n -> r u i n", u=2)[:, u]
                    sp.dma_start(dst, src[u]).then_inc(kq[b % 2], 16)
                sp.dma_start(m.k6[ROW_MASK:ROW_MASK + 1, b % 2],
                             a["neg_mask"][b:b + 1, :].unsqueeze(1).to_broadcast([1, HEADS, S])).then_inc(kq[b % 2], 16)

            load(0)
            load(1)
            for n in range(UNITS):
                sp.wait_ge(mt_sb, n + 1)
                b, g = n // GROUPS, n % GROUPS
                for i in range(2):
                    sp.dma_start(m.q6[ROW_SHIFT:ROWS_ALL, b % 2, 2 * g + i, :], m.mt[6 * i:6 * i + 6, n % 2, :]).then_inc(m_rows, 16)
                if g == GROUPS - 1 and b + 2 < B:
                    load(b + 2)

        @block.tensor
        def _(pe):
            def max_scores(n, piece):
                b, g = n // GROUPS, n % GROUPS
                at = n * pieces + piece
                if n % GROUPS == 0 and piece == 0:
                    pe.wait_ge(kq[b % 2], 16 * loads * (b // 2 + 1))
                if at >= 2:
                    pe.wait_ge(s_read, at - 1)
                if cross:
                    for h in range(4):
                        last = nc.tensor.matmul(m.ps[:, s_bank + at % 2, h * N_CTX:(h + 1) * N_CTX],
                                                m.q6[0:ROWS_MAX, b % 2, 2 * g + h // 2, piece * P:(piece + 1) * P],
                                                k_of(b, 4 * g + h, 0, keys)[0:ROWS_MAX], start=True, stop=True)
                else:
                    qt, h = piece // 4, piece % 4
                    last = nc.tensor.matmul(m.ps[:, s_bank + at % 2, :], m.q6[0:ROWS_MAX, b % 2, 2 * g + h // 2, qt * P:(qt + 1) * P],
                                            k_of(b, 4 * g + h, 0, keys)[0:ROWS_MAX], start=True, stop=True)
                last.then_inc(s_ready, 1)

            def turn_maxima(n):
                pe.wait_ge(maxima, n + 1)
                if n >= 3:
                    pe.wait_ge(recip, n - 2)
                if n >= GROUPS + 2 and (n - 2) % GROUPS == 0:
                    pe.wait_ge(added, (n - 2) // GROUPS)
                for t in range(TB):
                    last = nc.tensor.transpose(m.ps[0:12, aux, :].bitcast(BF16)[:, t * P:(t + 1) * P],
                                               m.mparts[:, n % 2, t, :, :].rearrange("p h c -> p (h c)"), m.ident_bf[:])
                last.then_inc(mt_ps, 1)

            def shifted_scores(gs):
                n, s = gs // steps, gs % steps
                b, g = n // GROUPS, n % GROUPS
                kt, i = s // 2, s % 2
                if s == 0:
                    pe.wait_ge(m_rows, 32 * (n + 1))
                if gs >= 2:
                    pe.wait_ge(probs, gs - 1)
                for u in range(2):
                    last = nc.tensor.matmul(m.ps[0:kw, st_bank + 2 * (gs % 2) + u, :],
                                            k_of(b, 4 * g + 2 * i + u, kt * kw, kw)[0:ROWS_ALL],
                                            m.q6[0:ROWS_ALL, b % 2, 2 * g + i, :], start=True, stop=True)
                last.then_inc(st_ready, 1)

            def weigh_values(gs):
                n, s = gs // steps, gs % steps
                b, g = n // GROUPS, n % GROUPS
                kt, i = s // 2, s % 2
                pe.wait_ge(probs, gs + 1)
                if s == 0 and n >= 1:
                    pe.wait_ge(u_sb, n)
                for u in range(2):
                    j = 2 * i + u
                    last = nc.tensor.matmul(m.ps[32 * j:32 * j + 32, pv_bank, :], v_of(b, kt, 4 * g + j), m.probs[0:kw, gs % 4, u, :],
                                            start=(kt == 0), stop=(kt == kts - 1))
                last.then_inc(pv, 1)

            def spread_sums(n):
                pe.wait_ge(u_sb, n + 1)
                if n >= 1:
                    pe.wait_ge(recip, n)
                pe.wait_ge(mt_sb, min(n + 3, UNITS))
                if n % GROUPS == 0 and n >= GROUPS:
                    pe.wait_ge(added, n // GROUPS)
                nc.tensor.matmul(m.ps[:, aux, :], m.spread[:], m.unit[:, n % 2, :], start=True, stop=True).then_inc(sums_ready, 1)

            def project_out(b):
                pe.wait_ge(on, GROUPS * (b + 1))
                pe.wait_ge(recip, GROUPS * (b + 1))
                for t in range(TB):
                    for g in range(GROUPS):
                        last = nc.tensor.matmul(m.ps[:, aux, t * P:(t + 1) * P], m.on[:, g, t * P:(t + 1) * P], wo[:, g * D:(g + 1) * D],
                                                start=(g == 0), stop=(g == GROUPS - 1))
                last.then_inc(o_ps, 1)

            for n in range(2):
                for piece in range(pieces):
                    max_scores(n, piece)
            turn_maxima(0)
            for gs in range(total + 1):
                n, s = gs // steps, gs % steps
                if gs < total:
                    shifted_scores(gs)
                    if n + 2 < UNITS:
                        for piece in range(s * per_step, (s + 1) * per_step):
                            max_scores(n + 2, piece)
                if gs >= 1:
                    weigh_values(gs - 1)
                if gs < total and s == 0:
                    if n + 1 < UNITS:
                        turn_maxima(n + 1)
                    if n >= 1:
                        spread_sums(n - 1)
                if gs < total and s == 1 and n >= GROUPS and n % GROUPS == 0:
                    project_out(n // GROUPS - 1)
            spread_sums(UNITS - 1)
            project_out(B - 1)

        @block.scalar
        def _(act):
            def copy_maxima(n):
                act.wait_ge(mt_ps, n + 1)
                if n >= 2:
                    act.wait_ge(m_rows, 32 * (n - 1))
                nc.scalar.copy(m.mt[0:12, n % 2, :], m.ps[0:12, aux, :].bitcast(BF16)[:, 0:S]).then_inc(mt_sb, 1)

            copy_maxima(0)
            for gs in range(total):
                n, s = gs // steps, gs % steps
                act.wait_ge(st_ready, gs + 1)
                if gs >= 4:
                    act.wait_ge(pv, gs - 3)
                nc.scalar.activation(m.probs[0:kw, gs % 4], m.ps[0:kw, st_bank + 2 * (gs % 2):st_bank + 2 * (gs % 2) + 2, :],
                                     ACT.Exp, scale=scale).then_inc(probs, 1)
                if s == 0:
                    if n >= 1:
                        act.wait_ge(pv, gs)
                        if n >= 3:
                            act.wait_ge(on, n - 2)
                        nc.scalar.copy(m.unit[:, (n - 1) % 2, :], m.ps[:, pv_bank, :]).then_inc(u_sb, 1)
                    if n + 1 < UNITS:
                        copy_maxima(n + 1)
            act.wait_ge(pv, total)
            act.wait_ge(on, UNITS - 2)
            nc.scalar.copy(m.unit[:, (UNITS - 1) % 2, :], m.ps[:, pv_bank, :]).then_inc(u_sb, 1)

        @block.gpsimd
        def _(pool):
            for n in range(UNITS):
                pool.wait_ge(recip, n + 1)
                if n % GROUPS == 0 and n >= GROUPS:
                    pool.wait_ge(o_ps, n // GROUPS)
                nc.gpsimd.tensor_tensor(m.on[:, n % GROUPS, :], m.unit[:, n % 2, :], m.inverse[:, n % 2, :], ALU.mult).then_inc(on, 1)

        @block.vector
        def _(dve):
            chain = Chain(dve, dch)

            def row_maxima(n, piece):
                at = n * pieces + piece
                dve.wait_ge(s_ready, at + 1)
                if cross:
                    nc.vector.tensor_reduce(m.maxima[:, piece, :], m.ps[:, s_bank + at % 2, 0:4 * N_CTX].rearrange("p (h n) -> p h n", h=4),
                                            AX.X, ALU.max).then_inc(s_read, 1)
                else:
                    qt, h = piece // 4, piece % 4
                    nc.vector.reduce_max(m.maxima[:, qt, h:h + 1], m.ps[:, s_bank + at % 2, :], AX.X).then_inc(s_read, 1)

            def split_maxima(n):
                dve.wait_ge(s_read, (n + 1) * pieces)
                if n >= 2:
                    dve.wait_ge(mt_ps, n - 1)
                parts = m.mparts[:, n % 2]
                chain.link(nc.vector.tensor_copy(parts[:, :, :, 0], m.maxima[:]))
                chain.link(nc.vector.tensor_tensor(m.maxima[:], m.maxima[:], parts[:, :, :, 0], ALU.subtract))
                chain.link(nc.vector.tensor_copy(parts[:, :, :, 1], m.maxima[:]))
                nc.vector.tensor_tensor(parts[:, :, :, 2], m.maxima[:], parts[:, :, :, 1], ALU.subtract).then_inc(maxima, 1)
                dve.wait_ge(maxima, n + 1)

            def invert_sums(n):
                dve.wait_ge(sums_ready, n + 1)
                if n >= 2:
                    dve.wait_ge(on, n - 1)
                nc.vector.reciprocal(m.inverse[:, n % 2, :], m.ps[:, aux, :]).then_inc(recip, 1)

            def add_to_state(b):
                dve.wait_ge(o_ps, b + 1)
                nc.vector.tensor_tensor(m.state[:, b * TB:(b + 1) * TB, :], m.state[:, b * TB:(b + 1) * TB, :],
                                        m.ps[:, aux, :].rearrange("p (t d) -> p t d", t=TB), ALU.add).then_inc(added, 1)

            for n in range(2):
                for piece in range(pieces):
                    row_maxima(n, piece)
                split_maxima(n)
            for gs in range(total):
                n, s = gs // steps, gs % steps
                if n + 2 < UNITS:
                    for piece in range(s * per_step, (s + 1) * per_step):
                        row_maxima(n + 2, piece)
                if s == 0 and n >= 1:
                    invert_sums(n - 1)
                if s == 1 and n >= GROUPS and n % GROUPS == 0:
                    add_to_state(n // GROUPS - 1)
                if s == steps - 1 and n + 2 < UNITS:
                    split_maxima(n + 2)
            invert_sums(UNITS - 1)
            add_to_state(B - 1)


def stack_context_keys(nc, a, m, sem):
    got = sem("ctx_stacked")
    with nc.Block() as block:
        @block.sync
        def _(sp):
            src = a["ctx_keys"].rearrange("(i u r) c (b n) -> u b (r c) i n", u=2, r=HD, b=B)
            for b in range(B):
                for u in range(2):
                    dst = m.kc6[u * ROWS_HEAD:(u + 1) * ROWS_HEAD, b].rearrange("r (i u) n -> r u i n", u=2)[:, u]
                    sp.dma_start(dst, src[u, b]).then_inc(got, 16)
            sp.wait_ge(got, 16 * 2 * B)


def feed_forward(nc, a, m, sem):
    (ada_ps, ada, dch, hat, turned, xn, h_ps, h_sb, o_ps, biased, added) = [sem(f"ff_{n}") for n in (
        "ada_ready", "ada", "dve", "hat", "turned", "xn", "h_ready", "h", "out_ready", "biased", "added")]
    w1, w2 = w_of(m, "f1"), w_of(m, "f2")
    with nc.Block() as block:
        @block.tensor
        def _(pe):
            lo_c = COLS["n3"][0]
            for half in range(2):
                last = nc.tensor.matmul(m.ps[:, 7, half * B:(half + 1) * B], m.w[:, lo_c + half * D:lo_c + (half + 1) * D], m.condT[:],
                                        start=True, stop=True)
            last.then_inc(ada_ps, 1)

            def turn(b):
                pe.wait_ge(hat, b + 1)
                pe.wait_ge(ada, 1)
                for t in range(TB):
                    last = nc.tensor.transpose(m.ps[:, 6 + b % 2, t * P:(t + 1) * P], m.hat[:, b * TB + t, :], m.ident[:])
                last.then_inc(turned, 1)

            def up(b):
                pe.wait_ge(xn, b + 1)
                for c in range(CH):
                    n = b * CH + c
                    if n >= 4:
                        pe.wait_ge(h_sb, n - 3)
                    nc.tensor.matmul(m.ps[:, n % 4, :], w1[:, c * P:(c + 1) * P], m.xnT[:, b, :], start=True, stop=True).then_inc(h_ps, 1)

            def down(b):
                pe.wait_ge(h_sb, (b + 1) * CH)
                if b >= 2:
                    pe.wait_ge(added, b - 1)
                for t in range(TB):
                    for c in range(CH):
                        last = nc.tensor.matmul(m.ps[:, 4 + b % 2, t * P:(t + 1) * P], m.hT[:, b % 2, c, t * P:(t + 1) * P],
                                                w2[:, c * P:(c + 1) * P], start=(c == 0), stop=(c == CH - 1))
                last.then_inc(o_ps, 1)

            turn(0)
            turn(1)
            for b in range(B + 1):
                if b < B:
                    up(b)
                if b + 2 < B:
                    turn(b + 2)
                if b >= 1:
                    down(b - 1)

        @block.scalar
        def _(act):
            act.wait_ge(ada, 1)

            def scale_shift(b):
                act.wait_ge(turned, b + 1)
                nc.scalar.activation(m.xnT[:, b, :], m.ps[:, 6 + b % 2, :], ACT.Identity, bias=m.ada[:, B + b:B + b + 1],
                                     scale=m.ada[:, b:b + 1]).then_inc(xn, 1)

            scale_shift(0)
            scale_shift(1)
            for b in range(B):
                if b >= 2:
                    act.wait_ge(o_ps, b - 1)
                for c in range(CH):
                    act.wait_ge(h_ps, b * CH + c + 1)
                    nc.scalar.activation(m.hT[:, b % 2, c, :], m.ps[:, (b * CH + c) % 4, :], ACT.Gelu,
                                         bias=m.cols[:, 6 + c:7 + c]).then_inc(h_sb, 1)
                if b + 2 < B:
                    scale_shift(b + 2)

        @block.gpsimd
        def _(pool):
            pool.wait_ge(hat, B)
            nc.gpsimd.tensor_tensor(m.state[:], m.state[:], m.f2b[:].unsqueeze(1).to_broadcast([P, T, D]), ALU.add).then_inc(biased, 1)

        @block.vector
        def _(dve):
            chain = Chain(dve, dch)
            dve.wait_ge(ada_ps, 1)
            nc.vector.tensor_scalar(m.ada[:, 0:B], m.ps[:, 7, 0:B], m.cols[:, 4:5], 1.0, ALU.add, ALU.add)
            nc.vector.tensor_scalar(m.ada[:, B:2 * B], m.ps[:, 7, B:2 * B], m.cols[:, 5:6], None, ALU.add).then_inc(ada, 1)
            row_statistics(dve, chain, m.state[:], T, D, m.st)
            for b in range(B):
                for t in range(TB):
                    last = normalise(dve, m.hat[:], m.state[:], b * TB + t, m.st)
                last.then_inc(hat, 1)
            dve.wait_ge(biased, 1)
            for b in range(B):
                dve.wait_ge(o_ps, b + 1)
                nc.vector.tensor_tensor(m.state[:, b * TB:(b + 1) * TB, :], m.state[:, b * TB:(b + 1) * TB, :],
                                        m.ps[:, 4 + b % 2, :].rearrange("p (t d) -> p t d", t=TB), ALU.add).then_inc(added, 1)


def quantised_block(nc, a, m, sem):
    (w_in, dch, wabs, wsum, wq, q1, q1_ps, q1T, h_ps, h_in, h_sb, q2, q2_ps, q2T, o_ps, done, out, rows_in, pch, gain) = [
        sem(f"qb_{n}") for n in ("weights", "dve", "abs", "abs_sum", "ternary", "q1", "q1_turned", "q1T", "h_ready", "h_in", "h",
                                 "q2", "q2_turned", "q2T", "out_ready", "done", "stored", "rows", "pool", "gain")]
    w_n = float(D * HID)
    hid = m.hid

    def quantise(dve, chain, rows, width, t0, t1, out_bf):
        big = m.absmax[:, t0:t1]
        chain.link(nc.vector.tensor_reduce(big, rows[:, t0:t1, :], AX.X, ALU.max, apply_absolute_value=True))
        chain.link(nc.vector.tensor_scalar(big, big, LN_EPS, None, ALU.max))
        chain.link(nc.vector.reciprocal(m.qscale[:, t0:t1], big))
        chain.link(nc.vector.tensor_scalar(m.qscale[:, t0:t1], m.qscale[:, t0:t1], 127.0, None, ALU.mult))
        chain.link(nc.vector.reciprocal(m.step[:, t0:t1], m.qscale[:, t0:t1]))
        for t in range(t0, t1):
            last = nc.vector.tensor_scalar(rows[:, t, :], rows[:, t, :], m.qscale[:, t:t + 1], ROUND, ALU.mult, ALU.add)
        chain.link(last)
        chain.link(nc.vector.tensor_scalar(rows[:, t0:t1, :], rows[:, t0:t1, :], ROUND, 127.0, ALU.subtract, ALU.min))
        return nc.vector.tensor_scalar(out_bf[:, t0:t1, :], rows[:, t0:t1, :], -128.0, None, ALU.max)

    with nc.Block() as block:
        @block.sync
        def _(sp):
            sp.dma_start(m.tw[:, 0, :], a["ffn_w1"]).then_inc(w_in, 16)
            sp.dma_start(m.tw[:, 1, :], a["ffn_w2"]).then_inc(w_in, 16)
            sp.dma_start(m.frow[:], a["ffn_rows"].partition_broadcast(P)).then_inc(rows_in, 16)
            for b in range(B):
                sp.wait_ge(done, b + 1)
                sp.dma_start(a["out"][b].rearrange("(t p) d -> p t d", p=P), m.x[:, b * TB:(b + 1) * TB, :]).then_inc(out, 16)
            sp.wait_ge(out, 16 * B)

        @block.tensor
        def _(pe):
            pe.wait_ge(wabs, 1)
            nc.tensor.matmul(m.ps[:, 7, 0:2], m.ones32[:], m.wabs[:], start=True, stop=True).then_inc(wsum, 1)

            def turn1(b):
                pe.wait_ge(q1, b + 1)
                for t in range(TB):
                    last = nc.tensor.transpose(m.ps[:, b % 2, :].bitcast(BF16)[:, t * P:(t + 1) * P], m.qrow[:, b * TB + t, :], m.ident_bf[:])
                last.then_inc(q1_ps, 1)

            pe.wait_ge(wq, 1)
            for b in range(B):
                if b >= 2:
                    pe.wait_ge(q1T, b - 1)
                turn1(b)
                pe.wait_ge(q1T, b + 1)
                for t in range(TB):
                    n = b * TB + t
                    if n >= 4:
                        pe.wait_ge(h_in, n - 3)
                    nc.tensor.matmul(m.ps[:, 2 + n % 4, :], m.qT_bf[:, b % 2, t * P:(t + 1) * P], m.tern[:, 0, :], start=True, stop=True).then_inc(h_ps, 1)
            for n in range(T):
                pe.wait_ge(q2, n // TB + 1)
                if n >= 2:
                    pe.wait_ge(q2T, n - 1)
                if n < 2:
                    pe.wait_ge(q1T, B)
                for c in range(CH):
                    last = nc.tensor.transpose(m.ps[:, n % 2, :].bitcast(BF16)[:, c * P:(c + 1) * P],
                                               m.qhid[:, n, c * P:(c + 1) * P], m.ident_bf[:])
                last.then_inc(q2_ps, 1)
                pe.wait_ge(q2T, n + 1)
                b, t = n // TB, n % TB
                if t == 0:
                    pe.wait_ge(h_in, T)
                    if b >= 2:
                        pe.wait_ge(done, b - 1)
                for c in range(CH):
                    last = nc.tensor.matmul(m.ps[:, 4 + b % 2, t * P:(t + 1) * P], m.qT_bf[:, n % 2, c * P:(c + 1) * P],
                                            m.tern[:, 1, c * P:(c + 1) * P], start=(c == 0), stop=(c == CH - 1))
                last.then_inc(o_ps, 1)

        @block.scalar
        def _(act):
            for b in range(B):
                act.wait_ge(q1_ps, b + 1)
                if b >= 2:
                    act.wait_ge(h_ps, TB * (b - 1))
                nc.scalar.copy(m.qT_bf[:, b % 2, :], m.ps[:, b % 2, :].bitcast(BF16)[:, 0:S]).then_inc(q1T, 1)
                for t in range(TB):
                    n = b * TB + t
                    act.wait_ge(h_in, n + 1)
                    nc.scalar.activation(hid[:, n, :], hid[:, n, :], ACT.Gelu).then_inc(h_sb, 1)
            for n in range(T):
                act.wait_ge(q2_ps, n + 1)
                if n >= 2:
                    act.wait_ge(o_ps, n - 1)
                nc.scalar.copy(m.qT_bf[:, n % 2, :], m.ps[:, n % 2, :].bitcast(BF16)[:, 0:HID]).then_inc(q2T, 1)

        @block.gpsimd
        def _(pool):
            chain = Chain(pool, pch)
            chain.link(nc.gpsimd.memset(m.ones32[:], 1.0))

        @block.vector
        def _(dve):
            chain = Chain(dve, dch)
            dve.wait_ge(w_in, 32)
            for i in range(2):
                last = nc.vector.tensor_reduce(m.wabs[:, i:i + 1], m.tw[:, i, :], AX.X, ALU.add, apply_absolute_value=True)
            dve.wait_ge(pch, 1)
            chain.link(last)
            nc.vector.tensor_copy(m.wmean[:], m.wabs[:]).then_inc(wabs, 1)
            dve.wait_ge(wsum, 1)
            chain.link(nc.vector.tensor_scalar(m.wmean[:], m.ps[:, 7, 0:2], 1.0 / w_n, LN_EPS, ALU.mult, ALU.max))
            chain.link(nc.vector.reciprocal(m.wscale[:], m.wmean[:]))
            chain.link(nc.vector.reciprocal(m.wmean[:], m.wscale[:]))
            for i in range(2):
                last = nc.vector.tensor_scalar(m.tw[:, i, :], m.tw[:, i, :], m.wscale[:, i:i + 1], ROUND, ALU.mult, ALU.add)
            chain.link(last)
            chain.link(nc.vector.tensor_scalar(m.tw[:], m.tw[:], ROUND, 1.0, ALU.subtract, ALU.min))
            nc.vector.tensor_scalar(m.tern[:], m.tw[:], -1.0, None, ALU.max).then_inc(wq, 1)
            chain.link(nc.vector.tensor_tensor(m.x[:], m.x[:], m.state[:], ALU.add))
            row_statistics(dve, chain, m.x[:], T, D, m.st)
            for t in range(T):
                last = normalise(dve, m.state[:], m.x[:], t, m.st)
            chain.link(last)
            row_statistics(dve, chain, m.state[:], T, D, m.st)
            for t in range(T):
                last = normalise(dve, m.hat[:], m.state[:], t, m.st)
            chain.link(last)
            dve.wait_ge(rows_in, 16)
            chain.link(nc.vector.tensor_tensor(m.hat[:], m.hat[:], m.frow[:, 0:D].unsqueeze(1).to_broadcast([P, T, D]), ALU.mult))
            chain.link(nc.vector.tensor_tensor(m.hat[:], m.hat[:], m.frow[:, D:2 * D].unsqueeze(1).to_broadcast([P, T, D]), ALU.add))
            for b in range(B):
                quantise(dve, chain, m.hat[:], D, b * TB, (b + 1) * TB, m.qrow).then_inc(q1, 1)
            chain.link(nc.vector.tensor_scalar(m.step[:], m.step[:], m.wmean[:, 0:1], None, ALU.mult))
            at = 2 * D
            for n in range(T):
                dve.wait_ge(h_ps, n + 1)
                nc.vector.scalar_tensor_tensor(out=hid[:, n, :], in0=m.ps[:, 2 + n % 4, :], scalar=m.step[:, n:n + 1],
                                               in1=m.frow[:, at:at + HID], op0=ALU.mult, op1=ALU.add).then_inc(h_in, 1)
            dve.wait_ge(h_sb, T)
            row_statistics(dve, chain, hid[:], T, HID, m.st)
            for t in range(T):
                last = normalise(dve, hid[:], hid[:], t, m.st)
            chain.link(last)
            for b in range(B):
                rows = hid[:, b * TB:(b + 1) * TB, :]
                chain.link(nc.vector.tensor_tensor(rows, rows, m.frow[:, at + HID:at + 2 * HID].unsqueeze(1).to_broadcast([P, TB, HID]), ALU.mult))
                chain.link(nc.vector.tensor_tensor(rows, rows, m.frow[:, at + 2 * HID:at + 3 * HID].unsqueeze(1).to_broadcast([P, TB, HID]), ALU.add))
                quantise(dve, chain, hid[:], HID, b * TB, (b + 1) * TB, m.qhid).then_inc(q2, 1)
            chain.link(nc.vector.tensor_scalar(m.step[:], m.step[:], m.wmean[:, 1:2], None, ALU.mult))
            chain.link(nc.vector.tensor_tensor(m.x[:], m.x[:], m.frow[:, at + 3 * HID:at + 3 * HID + D].unsqueeze(1).to_broadcast([P, T, D]), ALU.add))
            for n in range(T):
                b, t = n // TB, n % TB
                dve.wait_ge(o_ps, (b + 1) * TB)
                last = nc.vector.scalar_tensor_tensor(out=m.x[:, n, :], in0=m.ps[:, 4 + b % 2, t * P:(t + 1) * P], scalar=m.step[:, n:n + 1],
                                                      in1=m.x[:, n, :], op0=ALU.mult, op1=ALU.add)
                if t == TB - 1:
                    last.then_inc(done, 1)


def build(nc, a):
    with ExitStack() as ctx:
        def sb(name, shape, dt=F32):
            return ctx.enter_context(nc.sbuf_tensor(name, shape, dt))

        big = sb("big", [P, T * HID])
        k6 = sb("k6", [P, 2, HEADS, S], BF16)
        w = sb("w", [P, W_COLS])
        vaug = sb("vaug", [P, B, TB, HEADS, 32])
        def early(lo, *shape):
            names = [f"d{i}" for i in range(len(shape))]
            flat = w[:, lo:lo + int(np.prod(shape))]
            return flat.rearrange(f"p ({' '.join(names)}) -> p {' '.join(names)}", **dict(zip(names, shape)))

        m = Memory()
        m.ps = ctx.enter_context(nc.psum_tensor("ps", [P, 8, 512], F32))
        m.x = sb("x", [P, T, D])
        m.state = sb("state", [P, T, D])
        m.hat = sb("hat", [P, T, D])
        m.xnT = sb("xnT", [P, B, S])
        m.ident = sb("ident", [P, P])
        m.ident_bf = sb("ident_bf", [P, P], BF16)
        m.st = Statistics()
        m.st.bn = sb("bn", [P, T, 6])
        m.st.mv = sb("mv", [P, T, 2])
        m.st.var = sb("var", [P, T])
        m.st.tmp = sb("tmp", [P, T])
        m.st.rstd = sb("rstd", [P, T])
        m.ctx = sb("ctx", [P, B, D])
        m.ctx_hat = early(1536, B, D)
        m.ctxn = early(2048, NC_ALL)
        m.ctxT = sb("ctxT", [P, NC_ALL])
        m.rows0 = early(0, 6, D)
        m.cols0 = sb("cols0", [P, 10])
        m.mats0 = early(768, 6, D)
        m.sigma = early(3620, D)
        m.cond_rows = sb("cond_rows", [P, B, D])
        m.condT = sb("condT", [P, B])
        m.cos = sb("cos", [P, S])
        m.sin = sb("sin", [P, S])
        m.mask_u8 = sb("mask_u8", [B, S], U8)
        m.cmask_u8 = sb("cmask_u8", [B, N_CTX], U8)
        m.negmask = sb("negmask", [B, S], BF16)
        m.negcmask = sb("negcmask", [B, N_CTX], BF16)
        m.shift_rows = big[0:6, 0:HEADS * S // 2].bitcast(BF16).rearrange("r (h n) -> r h n", h=HEADS)
        m.tri = sb("tri", [P, P], BF16)
        m.ones = sb("ones", [P, P], BF16)
        m.spread = sb("spread", [P, P])
        m.prefer = sb("prefer", [P, EXPERTS])
        m.slot_k = early(2400, NC_ALL)
        m.slot_vT = early(2750, NC_ALL)
        m.slot_v = early(3100, B, D + 1)
        m.qT = big[:, 0:B * S].rearrange("p (b n) -> p b n", b=B)
        m.attn = big[:, B * S:2 * B * S].rearrange("p (b n) -> p b n", b=B)
        m.rowmx = sb("rowmx", [P, B])
        m.negmx = sb("negmx", [P, B])
        m.psum_rows = sb("psum_rows", [P, B])
        m.colsum = sb("colsum", [P, T])
        m.wg = sb("wg", [P, EXPERTS])
        m.logits = sb("logits", [P, T, EXPERTS])
        m.rest = sb("rest", [P, T, EXPERTS])
        m.pick = sb("pick", [P, T, EXPERTS])
        m.gate = sb("gate", [P, T, EXPERTS])
        m.top = sb("top", [P, TOP_K, T])
        m.best = sb("best", [P, T])
        m.onehot = sb("onehot", [P, TOP_K, T, EXPERTS])
        m.onehot_bf = sb("onehot_bf", [P, TOP_K, T, EXPERTS], BF16)
        m.rank = sb("rank", [P, 2, T, EXPERTS])
        m.total = sb("total", [P, EXPERTS])
        m.share = sb("share", [P, EXPERTS, T])
        m.share2 = sb("share2", [P, 2, T])
        m.hT = big[:, 0:2 * CH * S].rearrange("p (i c n) -> p i c n", i=2, c=CH)
        m.fc = big[:, 4096:4096 + 2 * HID].rearrange("p (u n) -> p u n", u=2)
        m.proj = big[:, 5120:5120 + 2 * HID].rearrange("p (u c n) -> p u c n", u=2, c=CH)
        m.w = w
        m.cols = sb("cols", [P, 10])
        m.f2b = sb("f2b", [P, D])
        m.ada = sb("ada", [P, 2 * B])
        m.k6 = k6
        m.kc6 = sb("kc6", [P, B, HEADS, N_CTX], BF16)
        m.q6 = sb("q6", [P, 2, PAIRS, S], BF16)
        m.vaug = vaug
        m.vcaug = sb("vcaug", [P, B, HEADS, 32])
        m.rot = big[:, 0:4 * S].rearrange("p (i t n) -> p i t n", i=2, t=2)
        m.left = big[:, 4 * S:8 * S].rearrange("p (i t n) -> p i t n", i=2, t=2)
        m.swap = big[:, 8 * S:10 * S].rearrange("p (t n) -> p t n", t=2)
        m.parts = big[:, 10 * S:16 * S].bitcast(BF16).rearrange("p (i t c n) -> p i t c n", i=2, t=2, c=3)
        m.probs = big[:, 0:8 * S].rearrange("p (i u n) -> p i u n", i=4, u=2)
        m.unit = big[:, 8 * S:10 * S].rearrange("p (i n) -> p i n", i=2)
        m.inverse = big[:, 10 * S:12 * S].rearrange("p (i n) -> p i n", i=2)
        m.on = big[:, 12 * S:16 * S].rearrange("p (g n) -> p g n", g=GROUPS)
        m.maxima = sb("maxima", [P, TB, 4])
        m.mparts = sb("mparts", [P, 2, TB, 4, 3], BF16)
        m.mt = sb("mt", [12, 2, S], BF16)
        m.hid = big[:].rearrange("p (t n) -> p t n", t=T)
        m.tw = w[:, 0:2 * HID].rearrange("p (i n) -> p i n", i=2)
        m.tern = sb("tern", [P, 2, HID], BF16)
        m.frow = w[:, 2 * HID:5 * HID + 3 * D]
        m.wabs = sb("wabs", [P, 2])
        m.wmean = sb("wmean", [P, 2])
        m.wscale = sb("wscale", [P, 2])
        m.ones32 = sb("ones32", [P, P])
        m.absmax = sb("absmax", [P, T])
        m.qscale = sb("qscale", [P, T])
        m.step = sb("step", [P, T])
        m.qrow = vaug[:, 0, 0:2].rearrange("p t h n -> p (t h n)").bitcast(BF16).rearrange("p (t d) -> p t d", t=T)
        m.qT_bf = sb("qT_bf", [P, 2, S], BF16)
        m.qhid = k6[:, 0].rearrange("p h n -> p (h n)")[:, 0:T * HID].rearrange("p (t n) -> p t n", t=T)
        with stage(nc) as sem:
            load_and_prepare(nc, a, m, sem)
        with nc.Fori(0, SLOT_STEPS), stage(nc) as sem:
            slot_step(nc, a, m, sem)
        with stage(nc) as sem:
            route_tokens(nc, a, m, sem)
        with nc.Fori(0, EXPERTS // 2) as pair, stage(nc) as sem:
            expert_pair(nc, a, m, sem, pair)
        with stage(nc) as sem:
            begin_layers(nc, a, m, sem)
        with nc.Fori(0, LAYERS) as layer, stage(nc) as sem:
            project(nc, a, m, sem, layer, False)
            attend(nc, a, m, sem, False)
            project(nc, a, m, sem, layer, True)
            stack_context_keys(nc, a, m, sem)
            attend(nc, a, m, sem, True)
            feed_forward(nc, a, m, sem)
        with stage(nc) as sem:
            quantised_block(nc, a, m, sem)


def rotary_tables():
    half = HD // 2
    inv = np.float32(1.0) / np.power(np.float32(10000.0), np.arange(half, dtype=np.float32) / np.float32(half))
    ang = np.arange(S, dtype=np.float32)[:, None] * inv
    cos, sin = np.cos(ang).T.astype(np.float32), np.sin(ang).T.astype(np.float32)
    return np.tile(np.concatenate([cos, cos]), (HEADS, 1)), np.tile(np.concatenate([-sin, sin]), (HEADS, 1))


def lay_out(i):
    swap = np.arange(D).reshape(HEADS, 2, HD // 2)[:, ::-1].reshape(D)
    i = {k: np.asarray(v) for k, v in i.items()}
    L0, L1, F = "L0_xcond_", "L1_xcond_", "L1_ffn_"

    def out_rows(w):
        r = np.zeros((4, 32, GROUPS, D), np.float32)
        r[:, 0:HD] = w.T.reshape(GROUPS, 4, HD, D).transpose(1, 2, 0, 3)
        return r.reshape(P, GROUPS * D)

    def layer(n):
        qkv = i[L1 + "qkv_w"][n]
        q, k, v = qkv[0:D], qkv[D:2 * D], qkv[2 * D:]
        cq, ck = i[L1 + "cq_w"][n], i[L1 + "ck_w"][n]
        f2 = i[L1 + "f2_w"][n].T.reshape(CH, P, D).transpose(1, 0, 2).reshape(P, HID)
        return np.concatenate([q.T, q[swap].T, k.T, k[swap].T, v.T, out_rows(i[L1 + "so_w"][n]), cq.T, cq[swap].T, ck.T, ck[swap].T,
                               i[L1 + "cv_w"][n].T, out_rows(i[L1 + "co_w"][n]), i[L1 + "f1_w"][n].T, f2,
                               i[L1 + "n1_w"][n].T, i[L1 + "n2_w"][n].T, i[L1 + "n3_w"][n].T], axis=1)

    def layer_cols(n):
        vecs = [i[L1 + k][n].reshape(-1, P) for k in ("n1_b", "n2_b", "n3_b", "f1_b")]
        return np.concatenate(vecs).T

    cos, sin = rotary_tables()
    got = {
        "x": i["x"], "ctx": i["ctx_1024"], "cond": i["cond_1024"], "condT": i["cond_1024"].T,
        "mask": i["mask_BxS_bf0"], "cmask": i["mask_BxS2_bf0"], "cos": cos, "sin": sin,
        "slot_mats": np.stack([i[L0 + k] for k in ("wk", "wv", "wq", "wu", "w1", "w2")], axis=1),
        "slot_cols": np.stack([i[L0 + k] for k in ("lnkv_g", "lnkv_b", "lnq_g", "lnq_b", "lnm_g", "lnm_b", "bk", "bv", "bq", "b1")], axis=1),
        "slot_rows": np.stack([i[L0 + k].reshape(D) for k in ("q_mu", "q_logsig", "lnp_g", "lnp_b", "bu", "b2")]),
        "w_g": i["L0_ffn_w_g"], "c_fc": i["L0_ffn_c_fc"],
        "c_proj": i["L0_ffn_c_proj"].reshape(EXPERTS, CH, P, D).transpose(0, 2, 1, 3),
        "w": np.stack([layer(n) for n in range(LAYERS)]), "cols": np.stack([layer_cols(n) for n in range(LAYERS)]),
        "f2_b": i[L1 + "f2_b"],
        "ffn_w1": i[F + "w1"].T, "ffn_w2": i[F + "w2"].T.reshape(CH, P, D).transpose(1, 0, 2).reshape(P, HID),
        "ffn_rows": np.concatenate([i[F + k] for k in ("ln1_w", "ln1_b", "b1", "ln2_w", "ln2_b", "b2")]),
    }
    return {k: np.ascontiguousarray(v) for k, v in got.items()}


SCRATCH = {"neg_mask": ((B, S), BF16), "neg_cmask": ((B, N_CTX), BF16), "queries": ((B, P, PRODUCTS, S), BF16),
           "keys": ((B, P, PRODUCTS, S), BF16), "ctx_keys": ((P, PRODUCTS, NC_ALL), BF16)}


def kernel(**inputs):
    import concourse.bacc as bacc
    from concourse.bass_utils import run_bass_kernel_spmd

    nc = bacc.Bacc("TRN2", target_bir_lowering=False, num_devices=1)
    arrays = lay_out(inputs)
    a = {k: nc.dram_tensor(f"in_{k}", v.shape, mybir.dt.from_np(v.dtype), kind="ExternalInput").ap() for k, v in arrays.items()}
    a |= {k: nc.dram_tensor(f"scratch_{k}", shape, dt, kind="Internal").ap() for k, (shape, dt) in SCRATCH.items()}
    a["out"] = nc.dram_tensor("out", (B, S, D), F32, kind="ExternalOutput").ap()
    build(nc, a)
    r = run_bass_kernel_spmd(nc, [{f"in_{k}": v for k, v in arrays.items()}], core_ids=[0])
    return r.results[0]["out"]
```

```python
from contextlib import ExitStack, contextmanager

import numpy as np

import concourse.bass as bass
from concourse import mybir

ALU = mybir.AluOpType
ACT = mybir.ActivationFunctionType
AX = mybir.AxisListType
F32 = mybir.dt.float32
BF16 = mybir.dt.bfloat16
I32 = mybir.dt.int32
U8 = mybir.dt.uint8

P = 128
B, S, D = 4, 512, 128
TB = S // P
T = B * TB
N_CTX = 77
NC_ALL = B * N_CTX
SLOT_STEPS = 3
EXPERTS, HID, TOP_K = 8, 512, 2
CH = HID // P
CAPACITY = int(TOP_K * 1.25 * B * S / EXPERTS)
CAPACITY += CAPACITY % 2
LAYERS, HEADS, HD = 6, 16, 8
PAIRS = HEADS // 2
GROUPS = HEADS // 4
UNITS = B * GROUPS
LN_EPS = 1e-5
ROUND = 1.5 * 2.0 ** 23
MASKED = -1e30
RSQRT_SEED = 0x5F3759DF

PRODUCTS = 6
ROWS_HEAD = HD * PRODUCTS
ROW_MASK = 2 * ROWS_HEAD
ROW_SHIFT = ROW_MASK + 1
ROWS_MAX = ROW_SHIFT
ROWS_ALL = ROW_SHIFT + 6

SECTIONS = (("n1", 2 * D), ("q", D), ("qr", D), ("k", D), ("kr", D), ("v", D), ("so", GROUPS * D), ("n2", 2 * D), ("cq", D), ("cqr", D),
            ("ck", D), ("ckr", D), ("cv", D), ("co", GROUPS * D), ("n3", 2 * D), ("f1", HID), ("f2", HID))
COLS, _at = {}, 0
for _name, _width in SECTIONS:
    COLS[_name] = (_at, _at + _width)
    _at += _width
W_COLS = _at
W_FIRST = COLS["so"][0]


class Memory:
    pass


class Statistics:
    pass


class Chain:

    def __init__(self, engine, sem):
        self.engine, self.sem, self.n = engine, sem, 0

    def link(self, instruction):
        self.n += 1
        instruction.then_inc(self.sem, 1)
        self.engine.wait_ge(self.sem, self.n)


def row_statistics(dve, chain, rows, tiles, width, st):
    n = rows.shape[0]
    for t in range(tiles):
        last = dve.bn_stats(st.bn[:n, t, :], rows[:, t, :])
    chain.link(last)
    for t in range(tiles):
        last = dve.bn_aggr(st.mv[:n, t, :], st.bn[:n, t, :])
    chain.link(last)
    var, a, r = st.var[:n, :tiles], st.tmp[:n, :tiles], st.rstd[:n, :tiles]
    chain.link(dve.tensor_scalar(var, st.mv[:n, :tiles, 1], LN_EPS, None, ALU.add))
    chain.link(dve.tensor_scalar(a.bitcast(I32), var.bitcast(I32), 1, None, ALU.arith_shift_right))
    chain.link(dve.tensor_scalar(r.bitcast(I32), a.bitcast(I32), -1.0, float(RSQRT_SEED), ALU.mult, ALU.add))
    for _ in range(3):
        chain.link(dve.tensor_tensor(a, r, r, ALU.mult))
        chain.link(dve.scalar_tensor_tensor(out=a, in0=a, scalar=-0.5, in1=var, op0=ALU.mult, op1=ALU.mult))
        chain.link(dve.scalar_tensor_tensor(out=r, in0=a, scalar=1.5, in1=r, op0=ALU.add, op1=ALU.mult))


def normalise(dve, out, rows, t, st):
    n = rows.shape[0]
    return dve.tensor_scalar(out[:, t, :], rows[:, t, :], st.mv[:n, t, 0:1], st.rstd[:n, t:t + 1],
                             ALU.subtract, ALU.mult)


@contextmanager
def stage(nc):
    with ExitStack() as ctx:
        sems = []

        def sem(name):
            sems.append(ctx.enter_context(nc.semaphore(name)))
            return sems[-1]

        yield sem
        for s in sems:
            nc.gpsimd.sem_clear(s)
        nc.all_engine_barrier()


def load_and_prepare(nc, a, m, sem):
    x_in, ctx_in, mats, rows_in, consts = sem("x_in"), sem("ctx_in"), sem("mats_in"), sem("rows_in"), sem("consts_in")
    ident, ident0, lnx, lnc, ctx_ps, ctx_sb, kv_ps, kv_sb = (sem(n) for n in (
        "identity", "identity_zero", "noise_ready", "ctx_normal", "ctx_turned", "ctx_copied", "kv_ready", "kv_copied"))
    sig, dch, pch = sem("sigma"), sem("prep_dve"), sem("prep_pool")
    vu_ps, neg, neg_out, shift_out = sem("value_ready"), sem("neg_mask"), sem("neg_mask_out"), sem("shift_rows_out")
    stack0, ones = sem("stack_zero"), sem("stack_one")

    with nc.Block() as block:
        @block.sync
        def _(sp):
            sp.dma_start(m.x[:], a["x"].rearrange("b (t p) d -> p (b t) d", p=P)).then_inc(x_in, 16)
            sp.dma_start(m.ctx[0:N_CTX], a["ctx"].rearrange("b n d -> n b d")).then_inc(ctx_in, 16)
            sp.dma_start(m.rows0[:], a["slot_rows"].partition_broadcast(P)).then_inc(rows_in, 16)
            sp.dma_start(m.cols0[:], a["slot_cols"]).then_inc(mats, 16)
            sp.dma_start(m.mats0[:], a["slot_mats"]).then_inc(mats, 16)
            sp.dma_start(m.cond_rows[:], a["cond"].rearrange("b d -> (b d)").partition_broadcast(P)).then_inc(consts, 16)
            sp.dma_start(m.condT[:], a["condT"]).then_inc(consts, 16)
            sp.dma_start(m.cos[:], a["cos"]).then_inc(consts, 16)
            sp.dma_start(m.sin[:], a["sin"]).then_inc(consts, 16)
            sp.dma_start(m.mask_u8[:], a["mask"]).then_inc(consts, 16)
            sp.dma_start(m.cmask_u8[:], a["cmask"]).then_inc(consts, 16)
            sp.wait_ge(neg, 2)
            sp.dma_start(a["neg_mask"], m.negmask[:]).then_inc(neg_out, 16)
            sp.dma_start(a["neg_cmask"], m.negcmask[:]).then_inc(neg_out, 16)
            sp.wait_ge(neg_out, 32)
            sp.wait_ge(stack0, 3)
            sp.wait_ge(pch, 3)
            for i in range(2):
                sp.dma_start(m.k6[ROW_SHIFT:ROWS_ALL, i], m.shift_rows[:]).then_inc(shift_out, 16)
            for b in range(B):
                sp.dma_start(m.kc6[ROW_SHIFT:ROWS_ALL, b, :, 0:N_CTX], m.shift_rows[:, :, 0:N_CTX]).then_inc(shift_out, 16)
                sp.dma_start(m.kc6[ROW_MASK:ROW_MASK + 1, b, :, 0:N_CTX],
                             a["neg_cmask"][b:b + 1, :].unsqueeze(1).to_broadcast([1, HEADS, N_CTX])).then_inc(shift_out, 16)
            sp.wait_ge(shift_out, 16 * (2 + 2 * B))
            sp.wait_ge(consts, 96)

        @block.gpsimd
        def _(pool):
            chain = Chain(pool, pch)
            pool.memset(m.ident[:], 0.0).then_inc(ident0, 1)
            pool.wait_ge(ident0, 1)
            pool.affine_select(out=m.ident[:], in_=m.ident[:], compare_op=ALU.not_equal, fill=1.0, base=0,
                               pattern=[[-1, P]], channel_multiplier=1).then_inc(ident, 1)
            pool.wait_ge(ident, 1)
            pool.tensor_copy(m.ident_bf[:], m.ident[:]).then_inc(ident, 1)
            chain.link(pool.memset(m.shift_rows[:], -1.0))
            by_pair = m.shift_rows[:].rearrange("r (i u) n -> r i u n", u=2)
            chain.link(pool.affine_select(out=by_pair[:, :, 0, :], in_=by_pair[:, :, 0, :], compare_op=ALU.is_ge,
                                          fill=0.0, base=2, pattern=[[0, PAIRS], [0, S]], channel_multiplier=-1))
            chain.link(pool.affine_select(out=by_pair[:, :, 1, :], in_=by_pair[:, :, 1, :], compare_op=ALU.is_ge,
                                          fill=0.0, base=-3, pattern=[[0, PAIRS], [0, S]], channel_multiplier=1))
            chain.link(pool.memset(m.tri[:], 1.0))
            chain.link(pool.affine_select(out=m.tri[:], in_=m.tri[:], compare_op=ALU.is_ge, fill=0.0, base=0,
                                          pattern=[[1, P]], channel_multiplier=-1))
            for e in range(EXPERTS):
                last = pool.memset(m.prefer[:, e:e + 1], float(EXPERTS - e))
            chain.link(last)

        @block.scalar
        def _(act):
            act.wait_ge(rows_in, 16)
            nc.scalar.activation(m.sigma[:], m.rows0[:, 1, :], ACT.Exp).then_inc(sig, 1)
            act.wait_ge(mats, 32)
            act.wait_ge(ctx_ps, 1)
            nc.scalar.activation(m.ctxn[:], m.ps[:, 0, 0:NC_ALL], ACT.Identity, bias=m.cols0[:, 1:2],
                                 scale=m.cols0[:, 0:1]).then_inc(ctx_sb, 1)
            act.wait_ge(ctx_ps, 2)
            nc.scalar.copy(m.ctxT[:], m.ps[:, 1, 0:NC_ALL]).then_inc(ctx_sb, 1)
            act.wait_ge(kv_ps, 1)
            nc.scalar.activation(m.slot_k[:], m.ps[:, 2, 0:NC_ALL], ACT.Identity, bias=m.cols0[:, 6:7]).then_inc(kv_sb, 1)
            act.wait_ge(kv_ps, 2)
            nc.scalar.activation(m.slot_vT[:], m.ps[:, 3, 0:NC_ALL], ACT.Identity, bias=m.cols0[:, 7:8]).then_inc(kv_sb, 1)
            act.wait_ge(vu_ps, 1)
            nc.scalar.copy(m.slot_v[0:N_CTX, :, 0:D], m.ps[0:N_CTX, 4, :].rearrange("n (b d) -> n b d", b=B)).then_inc(kv_sb, 1)

        @block.tensor
        def _(pe):
            pe.wait_ge(ident, 2)
            pe.wait_ge(lnc, 1)
            for b in range(B):
                last = nc.tensor.transpose(m.ps[:, 0, b * N_CTX:(b + 1) * N_CTX], m.ctx_hat[0:N_CTX, b, :], m.ident[0:N_CTX, 0:N_CTX])
            last.then_inc(ctx_ps, 1)
            for b in range(B):
                last = nc.tensor.transpose(m.ps[:, 1, b * N_CTX:(b + 1) * N_CTX], m.ctx[0:N_CTX, b, :], m.ident[0:N_CTX, 0:N_CTX])
            last.then_inc(ctx_ps, 1)
            pe.wait_ge(mats, 32)
            pe.wait_ge(ctx_sb, 1)
            nc.tensor.matmul(m.ps[:, 2, 0:NC_ALL], m.mats0[:, 0, :], m.ctxn[:], start=True, stop=True).then_inc(kv_ps, 1)
            nc.tensor.matmul(m.ps[:, 3, 0:NC_ALL], m.mats0[:, 1, :], m.ctxn[:], start=True, stop=True).then_inc(kv_ps, 1)
            pe.wait_ge(kv_sb, 2)
            for b in range(B):
                last = nc.tensor.matmul(m.ps[0:N_CTX, 4, b * D:(b + 1) * D], m.slot_vT[:, b * N_CTX:(b + 1) * N_CTX],
                                        m.mats0[:, 3, :], start=True, stop=True)
            last.then_inc(vu_ps, 1)

        @block.vector
        def _(dve):
            chain = Chain(dve, dch)
            dve.memset(m.k6[:], 0.0).then_inc(stack0, 1)
            dve.memset(m.kc6[:], 0.0).then_inc(stack0, 1)
            dve.memset(m.q6[:], 0.0).then_inc(stack0, 1)
            dve.wait_ge(stack0, 3)
            dve.memset(m.q6[ROW_MASK:ROW_MASK + 1], 1.0)
            dve.memset(m.vaug[:], 0.0)
            dve.memset(m.vcaug[:], 0.0)
            dve.memset(m.slot_v[:, :, D:D + 1], 1.0)
            chain.link(dve.memset(m.ones[:], 1.0))
            dve.memset(m.vaug[:, :, :, :, HD:HD + 1], 1.0)
            chain.link(dve.memset(m.vcaug[0:N_CTX, :, :, HD:HD + 1], 1.0))
            dve.wait_ge(consts, 96)
            dve.tensor_scalar(m.negmask[:], m.mask_u8[:], MASKED, None, ALU.mult).then_inc(neg, 1)
            dve.tensor_scalar(m.negcmask[:], m.cmask_u8[:], MASKED, None, ALU.mult).then_inc(neg, 1)
            dve.wait_ge(ctx_in, 16)
            row_statistics(dve, chain, m.ctx[0:N_CTX], B, D, m.st)
            for b in range(B):
                last = normalise(dve, m.ctx_hat[0:N_CTX], m.ctx[0:N_CTX], b, m.st)
            last.then_inc(lnc, 1)
            dve.wait_ge(lnc, 1)
            dve.wait_ge(x_in, 16)
            row_statistics(dve, chain, m.x[:], T, D, m.st)
            for t in range(T):
                last = normalise(dve, m.hat[:], m.x[:], t, m.st)
            chain.link(last)
            dve.wait_ge(sig, 1)
            chain.link(dve.tensor_tensor(m.hat[:], m.hat[:], m.sigma[:].unsqueeze(1).to_broadcast([P, T, D]), ALU.mult))
            chain.link(dve.tensor_tensor(m.state[:], m.hat[:], m.rows0[:, 0:1, :].to_broadcast([P, T, D]), ALU.add))
            dve.tensor_tensor(m.cond_rows[:], m.cond_rows[:], m.rows0[:, 5:6, :].to_broadcast([P, B, D]), ALU.add).then_inc(lnx, 1)


def slot_step(nc, a, m, sem):
    names = ("sl_dve", "sl_hat", "sl_turned", "sl_qin", "sl_q_ps", "sl_q", "sl_logits", "sl_max", "sl_p", "sl_attn",
             "sl_upd", "sl_new", "sl_biased")
    (dch, hat, turned, qin, q_ps, q_sb, logits, mx, probs, attn, upd, new, biased) = [sem(n) for n in names]
    scale = float(np.float32(1.0) / np.float32(D ** -0.5))
    with nc.Block() as block:
        @block.gpsimd
        def _(pool):
            pool.wait_ge(hat, B)
            nc.gpsimd.tensor_tensor(m.state[:], m.state[:], m.rows0[:, 4:5, :].to_broadcast([P, T, D]), ALU.add).then_inc(biased, 1)

        @block.tensor
        def _(pe):
            for b in range(B):
                pe.wait_ge(hat, b + 1)
                for t in range(TB):
                    last = nc.tensor.transpose(m.ps[:, b % 2, t * P:(t + 1) * P], m.hat[:, b * TB + t, :], m.ident[:])
                last.then_inc(turned, 1)
                pe.wait_ge(qin, b + 1)
                nc.tensor.matmul(m.ps[:, 2 + b % 2, :], m.mats0[:, 2, :], m.xnT[:, b, :], start=True, stop=True).then_inc(q_ps, 1)
                pe.wait_ge(q_sb, b + 1)
                nc.tensor.matmul(m.ps[0:N_CTX, 4 + b % 2, :], m.slot_k[:, b * N_CTX:(b + 1) * N_CTX], m.qT[:, b, :],
                                 start=True, stop=True).then_inc(logits, 1)
            for b in range(B):
                pe.wait_ge(attn, b + 1)
                for t in range(TB):
                    pe_bank = 6 + t % 2
                    if b * TB + t >= 2:
                        pe.wait_ge(new, b * TB + t - 1)
                    nc.tensor.matmul(m.ps[:, pe_bank, 0:D + 1], m.attn[0:N_CTX, b, t * P:(t + 1) * P], m.slot_v[0:N_CTX, b, :],
                                     start=True, stop=True).then_inc(upd, 1)

        @block.scalar
        def _(act):
            for b in range(B):
                act.wait_ge(turned, b + 1)
                nc.scalar.activation(m.xnT[:, b, :], m.ps[:, b % 2, :], ACT.Identity, bias=m.cols0[:, 3:4],
                                     scale=m.cols0[:, 2:3]).then_inc(qin, 1)
                act.wait_ge(q_ps, b + 1)
                nc.scalar.activation(m.qT[:, b, :], m.ps[:, 2 + b % 2, :], ACT.Identity, bias=m.cols0[:, 8:9]).then_inc(q_sb, 1)
                act.wait_ge(mx, b + 1)
                nc.scalar.activation(m.attn[0:N_CTX, b, :], m.ps[0:N_CTX, 4 + b % 2, :], ACT.Exp, bias=m.negmx[0:N_CTX, b:b + 1],
                                     scale=scale, accum_out=m.psum_rows[0:N_CTX, b:b + 1]).then_inc(probs, 1)

        @block.vector
        def _(dve):
            chain = Chain(dve, dch)
            row_statistics(dve, chain, m.state[:], T, D, m.st)
            for b in range(B):
                for t in range(TB):
                    last = normalise(dve, m.hat[:], m.state[:], b * TB + t, m.st)
                last.then_inc(hat, 1)
            for b in range(B):
                dve.wait_ge(logits, b + 1)
                chain.link(nc.vector.reduce_max(m.rowmx[0:N_CTX, b:b + 1], m.ps[0:N_CTX, 4 + b % 2, :], AX.X))
                nc.vector.tensor_scalar(m.negmx[0:N_CTX, b:b + 1], m.rowmx[0:N_CTX, b:b + 1], -scale, None, ALU.mult).then_inc(mx, 1)
                dve.wait_ge(probs, b + 1)
                chain.link(nc.vector.reciprocal(m.rowmx[0:N_CTX, b:b + 1], m.psum_rows[0:N_CTX, b:b + 1]))
                nc.vector.tensor_scalar(m.attn[0:N_CTX, b, :], m.attn[0:N_CTX, b, :], m.rowmx[0:N_CTX, b:b + 1], 1e-8,
                                        ALU.mult, ALU.add).then_inc(attn, 1)
            dve.wait_ge(biased, 1)
            for t in range(T):
                dve.wait_ge(upd, t + 1)
                bank = 6 + t % TB % 2
                chain.link(nc.vector.reciprocal(m.colsum[:, t:t + 1], m.ps[:, bank, D:D + 1]))
                nc.vector.scalar_tensor_tensor(out=m.state[:, t, :], in0=m.ps[:, bank, 0:D], scalar=m.colsum[:, t:t + 1],
                                               in1=m.state[:, t, :], op0=ALU.mult, op1=ALU.add).then_inc(new, 1)

    names = ("sm_dve", "sm_hat", "sm_turned", "sm_in", "sm_h_ps", "sm_h", "sm_out", "sm_added", "sm_normal", "sm_gained")
    (dch, hat, turned, hin, h_ps, h_sb, out_ps, added, normal, gained) = [sem(n) for n in names]
    with nc.Block() as block:
        @block.tensor
        def _(pe):
            for b in range(B):
                pe.wait_ge(hat, b + 1)
                for t in range(TB):
                    last = nc.tensor.transpose(m.ps[:, b % 2, t * P:(t + 1) * P], m.hat[:, b * TB + t, :], m.ident[:])
                last.then_inc(turned, 1)
                pe.wait_ge(hin, b + 1)
                nc.tensor.matmul(m.ps[:, 2 + b % 2, :], m.mats0[:, 4, :], m.xnT[:, b, :], start=True, stop=True).then_inc(h_ps, 1)
                pe.wait_ge(h_sb, b + 1)
                for t in range(TB):
                    last = nc.tensor.matmul(m.ps[:, 4 + b, t * P:(t + 1) * P], m.qT[:, b, t * P:(t + 1) * P], m.mats0[:, 5, :],
                                            start=True, stop=True)
                last.then_inc(out_ps, 1)

        @block.scalar
        def _(act):
            for b in range(B):
                act.wait_ge(turned, b + 1)
                nc.scalar.activation(m.xnT[:, b, :], m.ps[:, b % 2, :], ACT.Identity, bias=m.cols0[:, 5:6],
                                     scale=m.cols0[:, 4:5]).then_inc(hin, 1)
                act.wait_ge(h_ps, b + 1)
                nc.scalar.activation(m.qT[:, b, :], m.ps[:, 2 + b % 2, :], ACT.Gelu, bias=m.cols0[:, 9:10]).then_inc(h_sb, 1)

        @block.gpsimd
        def _(pool):
            pool.wait_ge(hat, B)
            for b in range(B):
                last = nc.gpsimd.tensor_tensor(m.state[:, b * TB:(b + 1) * TB, :], m.state[:, b * TB:(b + 1) * TB, :],
                                               m.cond_rows[:, b:b + 1, :].to_broadcast([P, TB, D]), ALU.add)
            last.then_inc(added, 1)

        @block.vector
        def _(dve):
            chain = Chain(dve, dch)
            row_statistics(dve, chain, m.state[:], T, D, m.st)
            for b in range(B):
                for t in range(TB):
                    last = normalise(dve, m.hat[:], m.state[:], b * TB + t, m.st)
                last.then_inc(hat, 1)
            dve.wait_ge(added, 1)
            for b in range(B):
                dve.wait_ge(out_ps, b + 1)
                last = nc.vector.tensor_tensor(m.state[:, b * TB:(b + 1) * TB, :], m.state[:, b * TB:(b + 1) * TB, :],
                                               m.ps[:, 4 + b, :].rearrange("p (t d) -> p t d", t=TB), ALU.add)
            chain.link(last)
            row_statistics(dve, chain, m.state[:], T, D, m.st)
            for t in range(T):
                last = normalise(dve, m.hat[:], m.state[:], t, m.st)
            chain.link(last)
            chain.link(nc.vector.tensor_tensor(m.hat[:], m.hat[:], m.rows0[:, 2:3, :].to_broadcast([P, T, D]), ALU.mult))
            nc.vector.tensor_tensor(m.state[:], m.hat[:], m.rows0[:, 3:4, :].to_broadcast([P, T, D]), ALU.add).then_inc(normal, 1)


def route_tokens(nc, a, m, sem):
    (dch, hat, turned, xt, logit, first, second, counted, wg_in, gate) = [sem(n) for n in (
        "rt_dve", "rt_hat", "rt_turned", "rt_xT", "rt_logits", "rt_first", "rt_second", "rt_counted", "rt_wg", "rt_gate")]
    expd = sem("rt_exp")
    by_e = [P, T, EXPERTS]
    with nc.Block() as block:
        @block.sync
        def _(sp):
            sp.dma_start(m.wg[:], a["w_g"]).then_inc(wg_in, 16)
            sp.wait_ge(wg_in, 16)

        @block.tensor
        def _(pe):
            pe.wait_ge(wg_in, 16)
            for b in range(B):
                pe.wait_ge(hat, b + 1)
                for t in range(TB):
                    last = nc.tensor.transpose(m.ps[:, b, t * P:(t + 1) * P], m.hat[:, b * TB + t, :], m.ident[:])
                last.then_inc(turned, 1)
            for b in range(B):
                pe.wait_ge(xt, b + 1)
                for t in range(TB):
                    at = (b * TB + t) * EXPERTS
                    last = nc.tensor.matmul(m.ps[:, 4, at:at + EXPERTS], m.xnT[:, b, t * P:(t + 1) * P], m.wg[:], start=True, stop=True)
            last.then_inc(logit, 1)
            for k, chosen in enumerate((first, second)):
                pe.wait_ge(chosen, 1)
                nc.tensor.matmul(m.ps[:, 5 + k, 0:P], m.tri[:], m.onehot_bf[:, k, :, :], start=True, stop=True)
                nc.tensor.matmul(m.ps[:, 5 + k, P:2 * P], m.ones[:], m.onehot_bf[:, k, :, :], start=True, stop=True).then_inc(counted, 1)

        @block.scalar
        def _(act):
            for b in range(B):
                act.wait_ge(turned, b + 1)
                nc.scalar.copy(m.xnT[:, b, :], m.ps[:, b, :]).then_inc(xt, 1)
            act.wait_ge(gate, 1)
            nc.scalar.activation(m.gate[:], m.gate[:], ACT.Exp).then_inc(expd, 1)

        @block.vector
        def _(dve):
            chain = Chain(dve, dch)
            chain.link(nc.vector.tensor_tensor(m.x[:], m.x[:], m.state[:], ALU.add))
            row_statistics(dve, chain, m.x[:], T, D, m.st)
            for b in range(B):
                for t in range(TB):
                    last = normalise(dve, m.hat[:], m.x[:], b * TB + t, m.st)
                last.then_inc(hat, 1)
            dve.wait_ge(logit, 1)
            lg, top, pick, rest = m.logits, m.top, m.pick, m.rest
            chain.link(nc.vector.tensor_copy(lg[:], m.ps[:, 4, 0:T * EXPERTS].rearrange("p (t e) -> p t e", e=EXPERTS)))
            chain.link(nc.vector.tensor_copy(rest[:], lg[:]))
            for k, chosen in enumerate((first, second)):
                chain.link(nc.vector.tensor_reduce(top[:, k, :], rest[:], AX.X, ALU.max))
                chain.link(nc.vector.tensor_tensor(pick[:], rest[:], top[:, k, :].unsqueeze(2).to_broadcast(by_e), ALU.is_equal))
                chain.link(nc.vector.tensor_tensor(pick[:], pick[:], m.prefer[:].unsqueeze(1).to_broadcast(by_e), ALU.mult))
                chain.link(nc.vector.tensor_reduce(m.best[:], pick[:], AX.X, ALU.max))
                chain.link(nc.vector.tensor_tensor(m.onehot[:, k], pick[:], m.best[:].unsqueeze(2).to_broadcast(by_e), ALU.is_equal))
                nc.vector.tensor_copy(m.onehot_bf[:, k], m.onehot[:, k]).then_inc(chosen, 1)
                if k == 0:
                    chain.link(nc.vector.scalar_tensor_tensor(out=rest[:], in0=m.onehot[:, 0], scalar=-3e38, in1=lg[:],
                                                              op0=ALU.mult, op1=ALU.add))
            both = m.pick
            chain.link(nc.vector.tensor_tensor(both[:], m.onehot[:, 0], m.onehot[:, 1], ALU.add))
            chain.link(nc.vector.tensor_tensor(m.gate[:], lg[:], both[:], ALU.mult))
            chain.link(nc.vector.tensor_scalar(rest[:], both[:], 1e9, -1e9, ALU.mult, ALU.add))
            chain.link(nc.vector.tensor_tensor(m.gate[:], m.gate[:], rest[:], ALU.add))
            chain.link(nc.vector.tensor_reduce(m.best[:], m.gate[:], AX.X, ALU.max))
            nc.vector.tensor_tensor(m.gate[:], m.gate[:], m.best[:].unsqueeze(2).to_broadcast(by_e), ALU.subtract).then_inc(gate, 1)
            dve.wait_ge(expd, 1)
            chain.link(nc.vector.tensor_reduce(m.best[:], m.gate[:], AX.X, ALU.add))
            chain.link(nc.vector.reciprocal(m.best[:], m.best[:]))
            chain.link(nc.vector.tensor_tensor(m.gate[:], m.gate[:], m.best[:].unsqueeze(2).to_broadcast(by_e), ALU.mult))
            dve.wait_ge(counted, 2)
            for k in range(TOP_K):
                tot, run = m.rank[:, 0], m.rank[:, 1]
                chain.link(nc.vector.tensor_copy(tot, m.ps[:, 5 + k, P:2 * P].rearrange("p (t e) -> p t e", e=EXPERTS)))
                if k == 0:
                    chain.link(nc.vector.memset(run[:, 0:1, :], 0.0))
                else:
                    chain.link(nc.vector.tensor_copy(run[:, 0:1, :], m.total[:].unsqueeze(1)))
                for t in range(1, T):
                    chain.link(nc.vector.tensor_tensor(run[:, t, :], run[:, t - 1, :], tot[:, t - 1, :], ALU.add))
                chain.link(nc.vector.tensor_tensor(m.total[:], run[:, T - 1, :], tot[:, T - 1, :], ALU.add))
                chain.link(nc.vector.tensor_tensor(run, run, m.ps[:, 5 + k, 0:P].rearrange("p (t e) -> p t e", e=EXPERTS), ALU.add))
                chain.link(nc.vector.scalar_tensor_tensor(out=m.onehot[:, k], in0=run, scalar=float(CAPACITY) + 0.5,
                                                          in1=m.onehot[:, k], op0=ALU.is_lt, op1=ALU.mult))
            chain.link(nc.vector.tensor_tensor(m.onehot[:, 0], m.onehot[:, 0], m.onehot[:, 1], ALU.add))
            nc.vector.tensor_tensor(m.share[:].rearrange("p e t -> p t e"), m.gate[:], m.onehot[:, 0], ALU.mult)
            nc.vector.memset(m.state[:], 0.0)


def expert_pair(nc, a, m, sem, pair):
    (w_in, h_ps, h_sb, o_ps, o_sb, share) = [sem(n) for n in (
        "ex_weights", "ex_h_ready", "ex_h", "ex_out_ready", "ex_added", "ex_share")]
    steps = [(u, b) for u in range(2) for b in range(B)]
    with nc.Block() as block:
        @block.sync
        def _(sp):
            for u in range(2):
                sp.dma_start(m.fc[:, u], a["c_fc"][pair * 2 + u]).then_inc(w_in, 16)
                sp.dma_start(m.proj[:, u], a["c_proj"][pair * 2 + u]).then_inc(w_in, 16)
            sp.wait_ge(w_in, 64)

        @block.tensor
        def _(pe):
            pe.wait_ge(w_in, 64)

            def up(i):
                u, b = steps[i]
                for c in range(CH):
                    n = i * CH + c
                    if n >= 4:
                        pe.wait_ge(h_sb, n - 3)
                    nc.tensor.matmul(m.ps[:, n % 4, :], m.fc[:, u, c * P:(c + 1) * P], m.xnT[:, b, :], start=True, stop=True).then_inc(h_ps, 1)

            def down(i):
                u, b = steps[i]
                pe.wait_ge(h_sb, (i + 1) * CH)
                if i >= 2:
                    pe.wait_ge(o_sb, i - 1)
                for t in range(TB):
                    for c in range(CH):
                        last = nc.tensor.matmul(m.ps[:, 4 + i % 2, t * P:(t + 1) * P], m.hT[:, i % 2, c, t * P:(t + 1) * P],
                                                m.proj[:, u, c, :], start=(c == 0), stop=(c == CH - 1))
                last.then_inc(o_ps, 1)

            for i in range(len(steps) + 1):
                if i < len(steps):
                    up(i)
                if i >= 1:
                    down(i - 1)

        @block.scalar
        def _(act):
            for i in range(len(steps)):
                if i >= 2:
                    act.wait_ge(o_ps, i - 1)
                for c in range(CH):
                    act.wait_ge(h_ps, i * CH + c + 1)
                    nc.scalar.activation(m.hT[:, i % 2, c, :], m.ps[:, (i * CH + c) % 4, :], ACT.Gelu).then_inc(h_sb, 1)

        @block.vector
        def _(dve):
            nc.vector.tensor_copy(m.share2[:], m.share[:, bass.ts(pair, 2), :]).then_inc(share, 1)
            dve.wait_ge(share, 1)
            for i, (u, b) in enumerate(steps):
                dve.wait_ge(o_ps, i + 1)
                if u == 1 and b == 0:
                    dve.wait_ge(o_sb, B)
                for t in range(TB):
                    at = b * TB + t
                    last = nc.vector.scalar_tensor_tensor(out=m.state[:, at, :], in0=m.ps[:, 4 + i % 2, t * P:(t + 1) * P],
                                                          scalar=m.share2[:, u, at:at + 1], in1=m.state[:, at, :],
                                                          op0=ALU.mult, op1=ALU.add)
                last.then_inc(o_sb, 1)


def begin_layers(nc, a, m, sem):
    dch, start = sem("bl_dve"), sem("bl_start")
    with nc.Block() as block:
        @block.vector
        def _(dve):
            chain = Chain(dve, dch)
            chain.link(nc.vector.tensor_tensor(m.x[:], m.x[:], m.state[:], ALU.add))
            row_statistics(dve, chain, m.x[:], T, D, m.st)
            for t in range(T):
                last = normalise(dve, m.state[:], m.x[:], t, m.st)
            last.then_inc(start, 1)


def w_of(m, name):
    lo, hi = COLS[name]
    return m.w[:, lo:hi]


def project(nc, a, m, sem, layer, cross):
    tag = "c" if cross else "s"
    (w_in, w_rest, ada_ps, ada, dch, hat, turned, xn, q_ps, read, rot, hi, low, mid, lo, v_ps, v_sb) = [
        sem(f"{tag}p_{n}") for n in ("weights", "weights_rest", "ada_ready", "ada", "dve", "hat", "turned", "xn", "qk_ready", "qk_read",
                                     "rotated", "high", "less_high", "middle", "low", "v_ready", "v")]
    out = [sem(f"{tag}p_stored{i}") for i in range(4)]
    stacked = sem(f"{tag}p_stacked")
    n_at = 1 if cross else 0
    norm = COLS["n2" if cross else "n1"][0]
    if cross:
        rounds = [("ck", "ckr", None)] + [("cq", "cqr", b) for b in range(B)]
    else:
        rounds = [(w, w + "r", b) for b in range(B) for w in "qk"]

    early = 1 if cross else 0

    def width(i):
        return S if rounds[i][2] is not None else NC_ALL

    with nc.Block() as block:
        @block.sync
        def _(sp):
            if not cross:
                sp.dma_start(m.w[:, 0:W_FIRST], a["w"][layer][:, 0:W_FIRST]).then_inc(w_in, 16)
                sp.dma_start(m.cols[:], a["cols"][layer]).then_inc(w_in, 16)
                sp.dma_start(m.w[:, W_FIRST:W_COLS], a["w"][layer][:, W_FIRST:W_COLS]).then_inc(w_rest, 16)
                sp.dma_start(m.f2b[:], a["f2_b"][layer].partition_broadcast(P)).then_inc(w_rest, 16)
            for i, (name, _, b) in enumerate(rounds):
                parts = m.parts[:, i % 4, :, 0:width(i)]
                sp.wait_ge(lo, i + 1)
                if name in ("q", "cq"):
                    dst = a["queries"][b]
                    sp.dma_start(dst[:, 0:3, :], parts[:, 0:3, :]).then_inc(out[i % 4], 16)
                    sp.dma_start(dst[:, 3:5, :], parts[:, 0:2, :]).then_inc(out[i % 4], 16)
                    sp.dma_start(dst[:, 5:6, :], parts[:, 0:1, :]).then_inc(out[i % 4], 16)
                else:
                    dst = a["keys"][b] if name == "k" else a["ctx_keys"]
                    sp.dma_start(dst[:, 0:3, :], parts[:, 0:1, :].to_broadcast([P, 3, width(i)])).then_inc(out[i % 4], 16)
                    sp.dma_start(dst[:, 3:5, :], parts[:, 1:2, :].to_broadcast([P, 2, width(i)])).then_inc(out[i % 4], 16)
                    sp.dma_start(dst[:, 5:6, :], parts[:, 2:3, :]).then_inc(out[i % 4], 16)
                if name == "ck":
                    sp.wait_ge(out[0], 48)
                    src = a["ctx_keys"].rearrange("(i u r) c (b n) -> u b (r c) i n", u=2, r=HD, b=B)
                    for b in range(B):
                        for u in range(2):
                            dst = m.kc6[u * ROWS_HEAD:(u + 1) * ROWS_HEAD, b, :, 0:N_CTX].rearrange("r (i u) n -> r u i n", u=2)[:, u]
                            sp.dma_start(dst, src[u, b]).then_inc(stacked, 16)
            if cross:
                sp.wait_ge(stacked, 16 * 2 * B)
            for j in range(4):
                sp.wait_ge(out[j], 48 * len(range(j, len(rounds), 4)))
            if not cross:
                sp.wait_ge(w_rest, 32)

        @block.tensor
        def _(pe):
            if not cross:
                pe.wait_ge(w_in, 32)
            for half in range(2):
                last = nc.tensor.matmul(m.ps[:, 7, half * B:(half + 1) * B], m.w[:, norm + half * D:norm + (half + 1) * D], m.condT[:],
                                        start=True, stop=True)
            last.then_inc(ada_ps, 1)
            if cross:
                for b in range(B):
                    last = nc.tensor.matmul(m.ps[0:N_CTX, 4, b * D:(b + 1) * D], m.ctxT[:, b * N_CTX:(b + 1) * N_CTX], w_of(m, "cv"),
                                            start=True, stop=True)
                last.then_inc(v_ps, 1)

            def turn():
                for b in range(B):
                    pe.wait_ge(hat, b + 1)
                    if b >= 2:
                        pe.wait_ge(xn, b - 1)
                    for t in range(TB):
                        last = nc.tensor.transpose(m.ps[:, 5 + b % 2, t * P:(t + 1) * P], m.hat[:, b * TB + t, :], m.ident[:])
                    last.then_inc(turned, 1)

            def products(i):
                name, swapped, b = rounds[i]
                bank, n = 2 * (i % 2), width(i)
                if i >= 2:
                    pe.wait_ge(read, i - 1)
                if b is None:
                    rhs = m.ctxT[:]
                else:
                    pe.wait_ge(xn, b + 1)
                    rhs = m.xnT[:, b, :]
                nc.tensor.matmul(m.ps[:, bank, 0:n], w_of(m, name), rhs, start=True, stop=True)
                nc.tensor.matmul(m.ps[:, bank + 1, 0:n], w_of(m, swapped), rhs, start=True, stop=True).then_inc(q_ps, 1)
                if name == "k":
                    if b >= 1:
                        pe.wait_ge(v_sb, b)
                    for t in range(TB):
                        last = nc.tensor.matmul(m.ps[:, 4, t * P:(t + 1) * P], m.xnT[:, b, t * P:(t + 1) * P], w_of(m, "v"),
                                                start=True, stop=True)
                    last.then_inc(v_ps, 1)

            for i in range(early):
                products(i)
            turn()
            for i in range(early, len(rounds)):
                products(i)

        @block.scalar
        def _(act):
            if cross:
                act.wait_ge(v_ps, 1)
                nc.scalar.copy(m.vcaug[0:N_CTX, :, :, 0:HD],
                               m.ps[0:N_CTX, 4, :].rearrange("n (b h d) -> n b h d", b=B, d=HD)).then_inc(v_sb, 1)

            def first_part(i):
                act.wait_ge(rot, i + 1)
                if i >= 4:
                    act.wait_ge(out[i % 4], 48 * (i // 4))
                nc.scalar.copy(m.parts[:, i % 4, 0, 0:width(i)], m.rot[:, i % 2, 0:width(i)]).then_inc(hi, 1)

            def second_part(i):
                act.wait_ge(low, i + 1)
                nc.scalar.copy(m.parts[:, i % 4, 1, 0:width(i)], m.left[:, i % 2, 0:width(i)]).then_inc(mid, 1)

            for i in range(early):
                first_part(i)
                second_part(i)
            act.wait_ge(ada, 1)
            for b in range(B):
                act.wait_ge(turned, b + 1)
                nc.scalar.activation(m.xnT[:, b, :], m.ps[:, 5 + b % 2, :], ACT.Identity, bias=m.ada[:, B + b:B + b + 1],
                                     scale=m.ada[:, b:b + 1]).then_inc(xn, 1)
            for i in range(early, len(rounds) + 1):
                if i < len(rounds):
                    first_part(i)
                if i < len(rounds) and rounds[i][0] == "k":
                    b = rounds[i][2]
                    act.wait_ge(v_ps, b + 1)
                    nc.scalar.copy(m.vaug[:, b, :, :, 0:HD], m.ps[:, 4, :].rearrange("p (t h d) -> p t h d", t=TB, d=HD)).then_inc(v_sb, 1)
                if i > early:
                    second_part(i - 1)

        @block.gpsimd
        def _(pool):
            def less_first(i):
                pool.wait_ge(hi, i + 1)
                if i >= 2:
                    pool.wait_ge(lo, i - 1)
                nc.gpsimd.tensor_tensor(m.left[:, i % 2, 0:width(i)], m.rot[:, i % 2, 0:width(i)], m.parts[:, i % 4, 0, 0:width(i)],
                                        ALU.subtract).then_inc(low, 1)

            def third_part(i):
                pool.wait_ge(mid, i + 1)
                nc.gpsimd.tensor_tensor(m.parts[:, i % 4, 2, 0:width(i)], m.left[:, i % 2, 0:width(i)], m.parts[:, i % 4, 1, 0:width(i)],
                                        ALU.subtract).then_inc(lo, 1)

            for i in range(early):
                less_first(i)
                third_part(i)
            for i in range(early, len(rounds) + 1):
                if i < len(rounds):
                    less_first(i)
                if i > early:
                    third_part(i - 1)

        @block.vector
        def _(dve):
            chain = Chain(dve, dch)
            def rotate(i):
                b = rounds[i][2]
                bank, n = 2 * (i % 2), width(i)
                x, y, r, t = m.ps[:, bank, 0:n], m.ps[:, bank + 1, 0:n], m.rot[:, i % 2, 0:n], m.swap[:, i % 2, 0:n]
                cos, sin = m.cos[:], m.sin[:]
                if b is None:
                    x, y, r, t = (v.rearrange("p (b n) -> p b n", b=B) for v in (x, y, r, t))
                    cos, sin = (v[:, 0:N_CTX].unsqueeze(1).to_broadcast([P, B, N_CTX]) for v in (m.cos, m.sin))
                dve.wait_ge(q_ps, i + 1)
                if i >= 2:
                    dve.wait_ge(low, i - 1)
                nc.vector.tensor_tensor(r, x, cos, ALU.mult)
                nc.vector.tensor_tensor(t, y, sin, ALU.mult).then_inc(read, 1)
                dve.wait_ge(read, i + 1)
                nc.vector.tensor_tensor(r, r, t, ALU.add).then_inc(rot, 1)

            for i in range(early):
                rotate(i)
            row_statistics(dve, chain, m.state[:], T, D, m.st)
            for b in range(B):
                for t in range(TB):
                    last = normalise(dve, m.hat[:], m.state[:], b * TB + t, m.st)
                last.then_inc(hat, 1)
                if b == 0:
                    if not cross:
                        dve.wait_ge(w_in, 32)
                    dve.wait_ge(ada_ps, 1)
                    nc.vector.tensor_scalar(m.ada[:, 0:B], m.ps[:, 7, 0:B], m.cols[:, 2 * n_at:2 * n_at + 1], 1.0, ALU.add, ALU.add)
                    nc.vector.tensor_scalar(m.ada[:, B:2 * B], m.ps[:, 7, B:2 * B], m.cols[:, 2 * n_at + 1:2 * n_at + 2], None,
                                            ALU.add).then_inc(ada, 1)
            for i in range(early, len(rounds)):
                rotate(i)


def attend(nc, a, m, sem):
    (kq0, kq1, s_ready, s_read, maxima, mt_ps, mt_sb, m_rows, st_ready, probs, pv, sums_ready, inverted, widened, u_sb, spread, on,
     o_ps, added, dch) = [sem(f"sa_{n}") for n in (
        "stacked0", "stacked1", "max_scores", "max_read", "maxima", "shift_turned", "shift_copied", "shift_rows", "scores", "probs",
        "weighted", "sums", "sums_inverted", "inverse_widened", "unit_copied", "inverse_spread", "unit_done", "projected", "added", "dve")]
    kq = (kq0, kq1)
    wo = w_of(m, "so")
    scale = float(np.float32(1.0) / np.float32(np.sqrt(HD)))
    st_bank, s_bank, pv_bank, aux = 0, 3, 6, 7
    steps = 4 * TB
    total = UNITS * steps
    ahead = 28
    turn_at, gather_at, spread_at, project_at = 6, 9, 12, 15

    with nc.Block() as block:
        @block.sync
        def _(sp):
            def load(b):
                if b >= 2:
                    sp.wait_ge(st_ready, (b - 1) * GROUPS * steps)
                sp.dma_start(m.q6[0:ROW_MASK, b % 2], a["queries"][b].rearrange("(i r) c n -> (r c) i n", i=PAIRS)).then_inc(kq[b % 2], 16)
                src = a["keys"][b].rearrange("(i u r) c n -> u (r c) i n", u=2, r=HD)
                for u in range(2):
                    dst = m.k6[u * ROWS_HEAD:(u + 1) * ROWS_HEAD, b % 2].rearrange("r (i u) n -> r u i n", u=2)[:, u]
                    sp.dma_start(dst, src[u]).then_inc(kq[b % 2], 16)
                sp.dma_start(m.k6[ROW_MASK:ROW_MASK + 1, b % 2],
                             a["neg_mask"][b:b + 1, :].unsqueeze(1).to_broadcast([1, HEADS, S])).then_inc(kq[b % 2], 16)

            load(0)
            load(1)
            for n in range(UNITS):
                sp.wait_ge(mt_sb, n + 1)
                b, g = n // GROUPS, n % GROUPS
                sp.dma_start(m.q6[ROW_SHIFT:ROWS_ALL, b % 2, 2 * g:2 * g + 2, :], m.mt[:, n % 2, :]).then_inc(m_rows, 16)
                if g == 0 and 1 <= b < B - 1:
                    load(b + 1)

        @block.tensor
        def _(pe):
            def max_scores(at):
                n, qt, h = at // steps, at % steps // 4, at % 4
                b, g = n // GROUPS, n % GROUPS
                if at % (GROUPS * steps) == 0:
                    pe.wait_ge(kq[b % 2], 64 * (b // 2 + 1))
                if at >= 3:
                    pe.wait_ge(s_read, at - 2)
                nc.tensor.matmul(m.ps[:, s_bank + at % 3, :], m.q6[0:ROWS_MAX, b % 2, 2 * g + h // 2, qt * P:(qt + 1) * P],
                                 m.k6[0:ROWS_MAX, b % 2, 4 * g + h, :], start=True, stop=True).then_inc(s_ready, 1)

            reader = [None]

            def take_aux(next_reader, count):
                if reader[0] is not None:
                    pe.wait_ge(*reader[0])
                reader[0] = (next_reader, count)

            def turn_maxima(n):
                pe.wait_ge(maxima, n + 1)
                take_aux(mt_sb, n + 1)
                for t in range(TB):
                    last = nc.tensor.transpose(m.ps[0:12, aux, :].bitcast(BF16)[:, t * P:(t + 1) * P],
                                               m.mparts[:, n % 2, t].rearrange("p u c i -> p (u c i)"), m.ident_bf[:])
                last.then_inc(mt_ps, 1)

            def shifted_scores(at):
                n, kt, j = at // steps, at % steps // 4, at % 4
                b, g = n // GROUPS, n % GROUPS
                if at % steps == 0:
                    pe.wait_ge(m_rows, 16 * (n + 1))
                if at >= 3:
                    pe.wait_ge(probs, at - 2)
                nc.tensor.matmul(m.ps[:, st_bank + at % 3, :], m.k6[:, b % 2, 4 * g + j, kt * P:(kt + 1) * P],
                                 m.q6[:, b % 2, 2 * g + j // 2, :], start=True, stop=True).then_inc(st_ready, 1)

            def weigh_values(quad):
                n, kt = quad // TB, quad % TB
                b, g = n // GROUPS, n % GROUPS
                pe.wait_ge(probs, 4 * (quad + 1))
                if kt == 0 and n >= 1:
                    pe.wait_ge(u_sb, n)
                for j in range(4):
                    last = nc.tensor.matmul(m.ps[32 * j:32 * j + 32, pv_bank, :], m.vaug[:, b, kt, 4 * g + j, :], m.probs[:, quad % 2, j, :],
                                            start=(kt == 0), stop=(kt == TB - 1))
                last.then_inc(pv, 1)

            def gather_sums(n):
                pe.wait_ge(u_sb, n + 1)
                take_aux(inverted, n + 1)
                for t in range(TB):
                    last = nc.tensor.transpose(m.ps[:, aux, t * P:(t + 1) * P], m.unit[:, n % 2, t * P:(t + 1) * P], m.ident[:])
                last.then_inc(sums_ready, 1)

            def spread_inverse(n):
                pe.wait_ge(widened, n + 1)
                take_aux(on, n + 1)
                for t in range(TB):
                    last = nc.tensor.transpose(m.ps[:, aux, t * P:(t + 1) * P], m.inverse[:, n % 2, t, :, :].rearrange("p h r -> p (h r)"),
                                               m.ident[:])
                last.then_inc(spread, 1)

            def project_out(b):
                pe.wait_ge(on, GROUPS * (b + 1))
                take_aux(added, b + 1)
                for t in range(TB):
                    for g in range(GROUPS):
                        last = nc.tensor.matmul(m.ps[:, aux, t * P:(t + 1) * P], m.on[:, g, t * P:(t + 1) * P], wo[:, g * D:(g + 1) * D],
                                                start=(g == 0), stop=(g == GROUPS - 1))
                last.then_inc(o_ps, 1)

            for at in range(ahead):
                max_scores(at)
                if at == steps + 2:
                    turn_maxima(0)
            for at in range(total + steps):
                n, s = at // steps, at % steps
                if at < total:
                    shifted_scores(at)
                if at + ahead < total:
                    max_scores(at + ahead)
                if s % 4 == 3 and 0 <= at // 4 - 1 < total // 4:
                    weigh_values(at // 4 - 1)
                if s == turn_at and n + 1 < UNITS:
                    turn_maxima(n + 1)
                if s == gather_at and n >= 1:
                    gather_sums(n - 1)
                if s == spread_at and n >= 1:
                    spread_inverse(n - 1)
                if s == project_at and n >= 1 and n % GROUPS == 0:
                    project_out(n // GROUPS - 1)

        @block.scalar
        def _(act):
            def copy_maxima(n):
                act.wait_ge(mt_ps, n + 1)
                if n >= 2:
                    act.wait_ge(m_rows, 16 * (n - 1))
                nc.scalar.copy(m.mt[0:12, n % 2, :], m.ps[0:12, aux, :].bitcast(BF16)[:, 0:S]).then_inc(mt_sb, 1)

            def copy_unit(n):
                act.wait_ge(pv, TB * (n + 1))
                if n >= 2:
                    act.wait_ge(on, n - 1)
                nc.scalar.copy(m.unit[:, n % 2, :], m.ps[:, pv_bank, :]).then_inc(u_sb, 1)

            copy_maxima(0)
            for at in range(total):
                n, s = at // steps, at % steps
                act.wait_ge(st_ready, at + 1)
                if s % 4 == 0 and at >= 8:
                    act.wait_ge(pv, at // 4 - 1)
                nc.scalar.activation(m.probs[:, at // 4 % 2, at % 4, :], m.ps[:, st_bank + at % 3, :], ACT.Exp, scale=scale).then_inc(probs, 1)
                if s == 4 and n >= 1:
                    copy_unit(n - 1)
                if s == turn_at + 1 and n + 1 < UNITS:
                    copy_maxima(n + 1)
            copy_unit(UNITS - 1)

        @block.gpsimd
        def _(pool):
            for n in range(UNITS):
                pool.wait_ge(inverted, n + 1)
                if n >= 2:
                    pool.wait_ge(spread, n - 1)
                nc.gpsimd.tensor_copy(m.inverse[:, n % 2].rearrange("p t h r -> p (t h) r"),
                                      m.invsum[:, 0].rearrange("p t h -> p (t h)").unsqueeze(2).to_broadcast([P, 4 * TB, 32])).then_inc(widened, 1)

        @block.vector
        def _(dve):
            chain = Chain(dve, dch)

            def row_maxima(at):
                dve.wait_ge(s_ready, at + 1)
                qt, h = at % steps // 4, at % 4
                nc.vector.reduce_max(m.maxima[:, qt, h:h + 1], m.ps[:, s_bank + at % 3, :], AX.X).then_inc(s_read, 1)

            def split_maxima(n):
                dve.wait_ge(s_read, (n + 1) * steps)
                if n >= 2:
                    dve.wait_ge(mt_ps, n - 1)
                parts, left = m.mparts[:, n % 2], m.maxima[:, :, 0:4].rearrange("p t (i u) -> p t u i", u=2)
                chain.link(nc.vector.tensor_copy(parts[:, :, :, 0], left))
                chain.link(nc.vector.tensor_tensor(left, left, parts[:, :, :, 0], ALU.subtract))
                chain.link(nc.vector.tensor_copy(parts[:, :, :, 1], left))
                nc.vector.tensor_tensor(parts[:, :, :, 2], left, parts[:, :, :, 1], ALU.subtract).then_inc(maxima, 1)
                dve.wait_ge(maxima, n + 1)

            def invert_sums(n):
                dve.wait_ge(sums_ready, n + 1)
                if n >= 1:
                    dve.wait_ge(widened, n)
                nc.vector.reciprocal(m.invsum[:, 0], m.ps[:, aux, :].rearrange("p (t h r) -> p t h r", t=TB, h=4)[:, :, :, HD]).then_inc(inverted, 1)

            def divide_unit(n):
                dve.wait_ge(spread, n + 1)
                if n % GROUPS == 0 and n >= GROUPS:
                    dve.wait_ge(o_ps, n // GROUPS)
                nc.vector.tensor_tensor(m.on[:, n % GROUPS, :], m.unit[:, n % 2, :], m.ps[:, aux, :], ALU.mult).then_inc(on, 1)

            def add_to_state(b):
                dve.wait_ge(o_ps, b + 1)
                nc.vector.tensor_tensor(m.state[:, b * TB:(b + 1) * TB, :], m.state[:, b * TB:(b + 1) * TB, :],
                                        m.ps[:, aux, :].rearrange("p (t d) -> p t d", t=TB), ALU.add).then_inc(added, 1)

            def reduce_scores(at):
                row_maxima(at)
                if at % steps == steps - 1:
                    split_maxima(at // steps)

            for at in range(ahead):
                reduce_scores(at)
            for at in range(total + steps):
                n, s = at // steps, at % steps
                if at + ahead < total:
                    reduce_scores(at + ahead)
                if s == gather_at and n >= 1:
                    invert_sums(n - 1)
                if s == spread_at and n >= 1:
                    divide_unit(n - 1)
                if s == project_at and n >= 1 and n % GROUPS == 0:
                    add_to_state(n // GROUPS - 1)


def attend_context(nc, a, m, sem):
    (kq0, kq1, s_ready, s_read, maxima, mt_ps, mt_sb, m_rows, st_ready, probs, pv, sums_ready, inverted, widened, u_sb, spread, on,
     o_ps, added, dch, kq2, row_ones) = [sem(f"ca_{n}") for n in (
        "stacked0", "stacked1", "max_scores", "max_read", "maxima", "shift_turned", "shift_copied", "shift_rows", "scores", "probs",
        "weighted", "sums", "sums_inverted", "inverse_widened", "unit_copied", "inverse_spread", "unit_done", "projected", "added", "dve",
        "stacked2", "mask_row")]
    kq = (kq0, kq1, kq2)
    q6 = (m.q6[:, 0], m.q6[:, 1], m.q6_third)
    wo = w_of(m, "co")
    scale = float(np.float32(1.0) / np.float32(np.sqrt(HD)))
    st_bank, s_bank, pv_bank, aux0, aux1 = 0, 3, 5, 6, 7
    steps = HEADS
    total = B * steps
    ahead = 26
    turn_at = 7
    weigh_at, copy_at, gather_at, spread_at, project_at = 6, 7, 9, 13, 28

    def group_at(at, lag):
        quad, rest = (at - lag) // 4, (at - lag) % 4
        return quad if rest == 0 and 0 <= quad < total // 4 else None

    with nc.Block() as block:
        @block.sync
        def _(sp):
            def load(b):
                if b >= 3:
                    sp.wait_ge(st_ready, (b - 2) * steps)
                sp.dma_start(q6[b % 3][0:ROW_MASK], a["queries"][b].rearrange("(i r) c n -> (r c) i n", i=PAIRS)).then_inc(kq[b % 3], 16)

            for b in range(3):
                load(b)
            for b in range(B):
                sp.wait_ge(mt_sb, b + 1)
                if b == 2:
                    sp.wait_ge(row_ones, 2)
                sp.dma_start(q6[b % 3][ROW_SHIFT:ROWS_ALL], m.mct[:, b % 2, :]).then_inc(m_rows, 16)
                if b == 1:
                    load(3)

        @block.tensor
        def _(pe):
            def max_scores(at):
                b, qt, g = at // steps, at % steps // GROUPS, at % GROUPS
                if at % steps == 0:
                    pe.wait_ge(kq[b % 3], 16 * (b // 3 + 1))
                if at == 2 * steps:
                    pe.wait_ge(row_ones, 2)
                if at >= 2:
                    pe.wait_ge(s_read, at - 1)
                for h in range(4):
                    last = nc.tensor.matmul(m.ps[:, s_bank + at % 2, h * N_CTX:(h + 1) * N_CTX],
                                            q6[b % 3][0:ROWS_MAX, 2 * g + h // 2, qt * P:(qt + 1) * P],
                                            m.kc6[0:ROWS_MAX, b, 4 * g + h, 0:N_CTX], start=True, stop=True)
                last.then_inc(s_ready, 1)

            reader = {}

            def take_aux(bank, next_reader, count):
                if bank in reader:
                    pe.wait_ge(*reader[bank])
                reader[bank] = (next_reader, count)

            def turn_maxima(b):
                pe.wait_ge(maxima, b + 1)
                take_aux(aux1, mt_sb, b + 1)
                for t in range(TB):
                    last = nc.tensor.transpose(m.ps[0:3 * HEADS, aux1, :].bitcast(BF16)[:, t * P:(t + 1) * P],
                                               m.mcparts[:, t].rearrange("p u c i -> p (u c i)"), m.ident_bf[:])
                last.then_inc(mt_ps, 1)

            def shifted_scores(at):
                b, h = at // steps, at % steps
                if h == 0:
                    pe.wait_ge(m_rows, 16 * (b + 1))
                if at >= 3:
                    pe.wait_ge(probs, at - 2)
                nc.tensor.matmul(m.ps[:, st_bank + at % 3, :], m.kc6[:, b, h, :], q6[b % 3][:, h // 2, :],
                                 start=True, stop=True).then_inc(st_ready, 1)

            def weigh_values(quad):
                b, g = quad // GROUPS, quad % GROUPS
                pe.wait_ge(probs, 4 * (quad + 1))
                if quad >= 1:
                    pe.wait_ge(u_sb, quad)
                for j in range(4):
                    last = nc.tensor.matmul(m.ps[32 * j:32 * j + 32, pv_bank, :], m.vcaug[:, b, 4 * g + j, :],
                                            m.cprobs[quad % 2][:, j, :], start=True, stop=True)
                last.then_inc(pv, 1)

            def gather_sums(quad):
                pe.wait_ge(u_sb, quad + 1)
                take_aux(aux0, inverted, quad + 1)
                for t in range(TB):
                    last = nc.tensor.transpose(m.ps[:, aux0, t * P:(t + 1) * P],
                                               m.units[:, quad // GROUPS % 2, quad % GROUPS, t * P:(t + 1) * P], m.ident[:])
                last.then_inc(sums_ready, 1)

            def spread_inverse(quad):
                pe.wait_ge(widened, quad + 1)
                take_aux(aux1, on, quad + 1)
                for t in range(TB):
                    last = nc.tensor.transpose(m.ps[:, aux1, t * P:(t + 1) * P],
                                               m.inverses[:, quad % GROUPS, 4 * t:4 * t + 4, :].rearrange("p h r -> p (h r)"), m.ident[:])
                last.then_inc(spread, 1)

            def project_out(b):
                pe.wait_ge(on, GROUPS * (b + 1))
                take_aux(aux0, added, b + 1)
                for t in range(TB):
                    for g in range(GROUPS):
                        last = nc.tensor.matmul(m.ps[:, aux0, t * P:(t + 1) * P], m.units[:, b % 2, g, t * P:(t + 1) * P],
                                                wo[:, g * D:(g + 1) * D], start=(g == 0), stop=(g == GROUPS - 1))
                last.then_inc(o_ps, 1)

            for at in range(ahead):
                max_scores(at)
                if at == steps + 2:
                    turn_maxima(0)
            for at in range(total + steps):
                b, s = at // steps, at % steps
                if at < total:
                    shifted_scores(at)
                if at + ahead < total:
                    max_scores(at + ahead)
                if group_at(at, weigh_at) is not None:
                    weigh_values(group_at(at, weigh_at))
                if s == turn_at and b + 1 < B:
                    turn_maxima(b + 1)
                if group_at(at, gather_at) is not None:
                    gather_sums(group_at(at, gather_at))
                if group_at(at, spread_at) is not None:
                    spread_inverse(group_at(at, spread_at))
                if at >= project_at and (at - project_at) % steps == 0:
                    project_out((at - project_at) // steps)

        @block.scalar
        def _(act):
            def copy_maxima(b):
                act.wait_ge(mt_ps, b + 1)
                if b >= 2:
                    act.wait_ge(m_rows, 16 * (b - 1))
                nc.scalar.copy(m.mct[:, b % 2, :], m.ps[0:3 * HEADS, aux1, :].bitcast(BF16)[:, 0:S]).then_inc(mt_sb, 1)

            def copy_unit(quad):
                b, g = quad // GROUPS, quad % GROUPS
                act.wait_ge(pv, quad + 1)
                if g == 0 and b >= 2:
                    act.wait_ge(o_ps, b - 1)
                nc.scalar.copy(m.units[:, b % 2, g, :], m.ps[:, pv_bank, :]).then_inc(u_sb, 1)

            copy_maxima(0)
            for at in range(total):
                b, s = at // steps, at % steps
                act.wait_ge(st_ready, at + 1)
                if at % 4 == 0 and at >= 8:
                    act.wait_ge(pv, at // 4 - 1)
                nc.scalar.activation(m.cprobs[at // 4 % 2][:, at % 4, :], m.ps[:, st_bank + at % 3, :], ACT.Exp,
                                     scale=scale).then_inc(probs, 1)
                if group_at(at, copy_at) is not None:
                    copy_unit(group_at(at, copy_at))
                if s == turn_at + 1 and b + 1 < B:
                    copy_maxima(b + 1)
            for quad in range((total - 1 - copy_at) // 4 + 1, total // 4):
                copy_unit(quad)

        @block.gpsimd
        def _(pool):
            pool.memset(m.q6_third[ROW_MASK:P], 0.0).then_inc(row_ones, 1)
            pool.wait_ge(row_ones, 1)
            pool.memset(m.q6_third[ROW_MASK:ROW_MASK + 1], 1.0).then_inc(row_ones, 1)
            for quad in range(total // 4):
                pool.wait_ge(inverted, quad + 1)
                if quad >= GROUPS:
                    pool.wait_ge(spread, quad - GROUPS + 1)
                g = quad % GROUPS
                nc.gpsimd.tensor_copy(m.inverses[:, g], m.invsum[:, g].rearrange("p t h -> p (t h)").unsqueeze(2)
                                      .to_broadcast([P, 4 * TB, 32])).then_inc(widened, 1)

        @block.vector
        def _(dve):
            chain = Chain(dve, dch)

            def row_maxima(at):
                dve.wait_ge(s_ready, at + 1)
                qt, g = at % steps // GROUPS, at % GROUPS
                nc.vector.tensor_reduce(m.maxima[:, qt, 4 * g:4 * g + 4],
                                        m.ps[:, s_bank + at % 2, 0:4 * N_CTX].rearrange("p (h n) -> p h n", h=4),
                                        AX.X, ALU.max).then_inc(s_read, 1)

            def split_maxima(b):
                dve.wait_ge(s_read, (b + 1) * steps)
                if b >= 1:
                    dve.wait_ge(mt_ps, b)
                parts, left = m.mcparts, m.maxima[:].rearrange("p t (i u) -> p t u i", u=2)
                chain.link(nc.vector.tensor_copy(parts[:, :, :, 0], left))
                chain.link(nc.vector.tensor_tensor(left, left, parts[:, :, :, 0], ALU.subtract))
                chain.link(nc.vector.tensor_copy(parts[:, :, :, 1], left))
                nc.vector.tensor_tensor(parts[:, :, :, 2], left, parts[:, :, :, 1], ALU.subtract).then_inc(maxima, 1)
                dve.wait_ge(maxima, b + 1)

            def invert_sums(quad):
                dve.wait_ge(sums_ready, quad + 1)
                if quad >= GROUPS:
                    dve.wait_ge(widened, quad - GROUPS + 1)
                nc.vector.reciprocal(m.invsum[:, quad % GROUPS],
                                     m.ps[:, aux0, :].rearrange("p (t h r) -> p t h r", t=TB, h=4)[:, :, :, HD]).then_inc(inverted, 1)

            def divide_group(quad):
                dve.wait_ge(spread, quad + 1)
                rows = m.units[:, quad // GROUPS % 2, quad % GROUPS, :]
                nc.vector.tensor_tensor(rows, rows, m.ps[:, aux1, :], ALU.mult).then_inc(on, 1)

            def add_to_state(b):
                dve.wait_ge(o_ps, b + 1)
                nc.vector.tensor_tensor(m.state[:, b * TB:(b + 1) * TB, :], m.state[:, b * TB:(b + 1) * TB, :],
                                        m.ps[:, aux0, :].rearrange("p (t d) -> p t d", t=TB), ALU.add).then_inc(added, 1)

            def reduce_scores(at):
                row_maxima(at)
                if at % steps == steps - 1:
                    split_maxima(at // steps)

            for at in range(ahead):
                reduce_scores(at)
            for at in range(total + steps):
                b, s = at // steps, at % steps
                if at + ahead < total:
                    reduce_scores(at + ahead)
                if group_at(at, gather_at) is not None:
                    invert_sums(group_at(at, gather_at))
                if group_at(at, spread_at) is not None:
                    divide_group(group_at(at, spread_at))
                if at >= project_at and (at - project_at) % steps == 0:
                    add_to_state((at - project_at) // steps)


def feed_forward(nc, a, m, sem):
    (ada_ps, ada, dch, hat, turned, xn, h_ps, h_sb, o_ps, biased, added) = [sem(f"ff_{n}") for n in (
        "ada_ready", "ada", "dve", "hat", "turned", "xn", "h_ready", "h", "out_ready", "biased", "added")]
    w1, w2 = w_of(m, "f1"), w_of(m, "f2")
    with nc.Block() as block:
        @block.tensor
        def _(pe):
            lo_c = COLS["n3"][0]
            for half in range(2):
                last = nc.tensor.matmul(m.ps[:, 7, half * B:(half + 1) * B], m.w[:, lo_c + half * D:lo_c + (half + 1) * D], m.condT[:],
                                        start=True, stop=True)
            last.then_inc(ada_ps, 1)

            def turn(b):
                pe.wait_ge(hat, b + 1)
                pe.wait_ge(ada, 1)
                for t in range(TB):
                    last = nc.tensor.transpose(m.ps[:, 6 + b % 2, t * P:(t + 1) * P], m.hat[:, b * TB + t, :], m.ident[:])
                last.then_inc(turned, 1)

            def up(b):
                pe.wait_ge(xn, b + 1)
                for c in range(CH):
                    n = b * CH + c
                    if n >= 4:
                        pe.wait_ge(h_sb, n - 3)
                    nc.tensor.matmul(m.ps[:, n % 4, :], w1[:, c * P:(c + 1) * P], m.xnT[:, b, :], start=True, stop=True).then_inc(h_ps, 1)

            def down(b):
                pe.wait_ge(h_sb, (b + 1) * CH)
                if b >= 2:
                    pe.wait_ge(added, b - 1)
                for t in range(TB):
                    for c in range(CH):
                        last = nc.tensor.matmul(m.ps[:, 4 + b % 2, t * P:(t + 1) * P], m.hT[:, b % 2, c, t * P:(t + 1) * P],
                                                w2[:, c * P:(c + 1) * P], start=(c == 0), stop=(c == CH - 1))
                last.then_inc(o_ps, 1)

            turn(0)
            turn(1)
            for b in range(B + 1):
                if b < B:
                    up(b)
                if b + 2 < B:
                    turn(b + 2)
                if b >= 1:
                    down(b - 1)

        @block.scalar
        def _(act):
            act.wait_ge(ada, 1)

            def scale_shift(b):
                act.wait_ge(turned, b + 1)
                nc.scalar.activation(m.xnT[:, b, :], m.ps[:, 6 + b % 2, :], ACT.Identity, bias=m.ada[:, B + b:B + b + 1],
                                     scale=m.ada[:, b:b + 1]).then_inc(xn, 1)

            scale_shift(0)
            scale_shift(1)
            for b in range(B):
                if b >= 2:
                    act.wait_ge(o_ps, b - 1)
                for c in range(CH):
                    act.wait_ge(h_ps, b * CH + c + 1)
                    nc.scalar.activation(m.hT[:, b % 2, c, :], m.ps[:, (b * CH + c) % 4, :], ACT.Gelu,
                                         bias=m.cols[:, 6 + c:7 + c]).then_inc(h_sb, 1)
                if b + 2 < B:
                    scale_shift(b + 2)

        @block.gpsimd
        def _(pool):
            pool.wait_ge(hat, B)
            nc.gpsimd.tensor_tensor(m.state[:], m.state[:], m.f2b[:].unsqueeze(1).to_broadcast([P, T, D]), ALU.add).then_inc(biased, 1)

        @block.vector
        def _(dve):
            chain = Chain(dve, dch)
            dve.wait_ge(ada_ps, 1)
            nc.vector.tensor_scalar(m.ada[:, 0:B], m.ps[:, 7, 0:B], m.cols[:, 4:5], 1.0, ALU.add, ALU.add)
            nc.vector.tensor_scalar(m.ada[:, B:2 * B], m.ps[:, 7, B:2 * B], m.cols[:, 5:6], None, ALU.add).then_inc(ada, 1)
            row_statistics(dve, chain, m.state[:], T, D, m.st)
            for b in range(B):
                for t in range(TB):
                    last = normalise(dve, m.hat[:], m.state[:], b * TB + t, m.st)
                last.then_inc(hat, 1)
            dve.wait_ge(biased, 1)
            for b in range(B):
                dve.wait_ge(o_ps, b + 1)
                nc.vector.tensor_tensor(m.state[:, b * TB:(b + 1) * TB, :], m.state[:, b * TB:(b + 1) * TB, :],
                                        m.ps[:, 4 + b % 2, :].rearrange("p (t d) -> p t d", t=TB), ALU.add).then_inc(added, 1)


def quantised_block(nc, a, m, sem):
    (w_in, dch, wabs, wsum, wq, q1, q1_ps, q1T, h_ps, h_in, h_sb, q2, q2_ps, q2T, o_ps, done, out, rows_in, pch, gain) = [
        sem(f"qb_{n}") for n in ("weights", "dve", "abs", "abs_sum", "ternary", "q1", "q1_turned", "q1T", "h_ready", "h_in", "h",
                                 "q2", "q2_turned", "q2T", "out_ready", "done", "stored", "rows", "pool", "gain")]
    w_n = float(D * HID)
    hid = m.hid

    def quantise(dve, chain, rows, width, t0, t1, out_bf):
        big = m.absmax[:, t0:t1]
        chain.link(nc.vector.tensor_reduce(big, rows[:, t0:t1, :], AX.X, ALU.max, apply_absolute_value=True))
        chain.link(nc.vector.tensor_scalar(big, big, LN_EPS, None, ALU.max))
        chain.link(nc.vector.reciprocal(m.qscale[:, t0:t1], big))
        chain.link(nc.vector.tensor_scalar(m.qscale[:, t0:t1], m.qscale[:, t0:t1], 127.0, None, ALU.mult))
        chain.link(nc.vector.reciprocal(m.step[:, t0:t1], m.qscale[:, t0:t1]))
        for t in range(t0, t1):
            last = nc.vector.tensor_scalar(rows[:, t, :], rows[:, t, :], m.qscale[:, t:t + 1], ROUND, ALU.mult, ALU.add)
        chain.link(last)
        chain.link(nc.vector.tensor_scalar(rows[:, t0:t1, :], rows[:, t0:t1, :], ROUND, 127.0, ALU.subtract, ALU.min))
        return nc.vector.tensor_scalar(out_bf[:, t0:t1, :], rows[:, t0:t1, :], -128.0, None, ALU.max)

    with nc.Block() as block:
        @block.sync
        def _(sp):
            sp.dma_start(m.tw[:, 0, :], a["ffn_w1"]).then_inc(w_in, 16)
            sp.dma_start(m.tw[:, 1, :], a["ffn_w2"]).then_inc(w_in, 16)
            sp.dma_start(m.frow[:], a["ffn_rows"].partition_broadcast(P)).then_inc(rows_in, 16)
            for b in range(B):
                sp.wait_ge(done, b + 1)
                sp.dma_start(a["out"][b].rearrange("(t p) d -> p t d", p=P), m.x[:, b * TB:(b + 1) * TB, :]).then_inc(out, 16)
            sp.wait_ge(out, 16 * B)

        @block.tensor
        def _(pe):
            pe.wait_ge(wabs, 1)
            nc.tensor.matmul(m.ps[:, 7, 0:2], m.ones32[:], m.wabs[:], start=True, stop=True).then_inc(wsum, 1)

            def turn1(b):
                pe.wait_ge(q1, b + 1)
                for t in range(TB):
                    last = nc.tensor.transpose(m.ps[:, b % 2, :].bitcast(BF16)[:, t * P:(t + 1) * P], m.qrow[:, b * TB + t, :], m.ident_bf[:])
                last.then_inc(q1_ps, 1)

            pe.wait_ge(wq, 1)
            for b in range(B):
                if b >= 2:
                    pe.wait_ge(q1T, b - 1)
                turn1(b)
                pe.wait_ge(q1T, b + 1)
                for t in range(TB):
                    n = b * TB + t
                    if n >= 4:
                        pe.wait_ge(h_in, n - 3)
                    nc.tensor.matmul(m.ps[:, 2 + n % 4, :], m.qT_bf[:, b % 2, t * P:(t + 1) * P], m.tern[:, 0, :], start=True, stop=True).then_inc(h_ps, 1)
            for n in range(T):
                pe.wait_ge(q2, n // TB + 1)
                if n >= 2:
                    pe.wait_ge(q2T, n - 1)
                if n < 2:
                    pe.wait_ge(q1T, B)
                for c in range(CH):
                    last = nc.tensor.transpose(m.ps[:, n % 2, :].bitcast(BF16)[:, c * P:(c + 1) * P],
                                               m.qhid[:, n, c * P:(c + 1) * P], m.ident_bf[:])
                last.then_inc(q2_ps, 1)
                pe.wait_ge(q2T, n + 1)
                b, t = n // TB, n % TB
                if t == 0:
                    pe.wait_ge(h_in, T)
                    if b >= 2:
                        pe.wait_ge(done, b - 1)
                for c in range(CH):
                    last = nc.tensor.matmul(m.ps[:, 4 + b % 2, t * P:(t + 1) * P], m.qT_bf[:, n % 2, c * P:(c + 1) * P],
                                            m.tern[:, 1, c * P:(c + 1) * P], start=(c == 0), stop=(c == CH - 1))
                last.then_inc(o_ps, 1)

        @block.scalar
        def _(act):
            for b in range(B):
                act.wait_ge(q1_ps, b + 1)
                if b >= 2:
                    act.wait_ge(h_ps, TB * (b - 1))
                nc.scalar.copy(m.qT_bf[:, b % 2, :], m.ps[:, b % 2, :].bitcast(BF16)[:, 0:S]).then_inc(q1T, 1)
                for t in range(TB):
                    n = b * TB + t
                    act.wait_ge(h_in, n + 1)
                    nc.scalar.activation(hid[:, n, :], hid[:, n, :], ACT.Gelu).then_inc(h_sb, 1)
            for n in range(T):
                act.wait_ge(q2_ps, n + 1)
                if n >= 2:
                    act.wait_ge(o_ps, n - 1)
                nc.scalar.copy(m.qT_bf[:, n % 2, :], m.ps[:, n % 2, :].bitcast(BF16)[:, 0:HID]).then_inc(q2T, 1)

        @block.gpsimd
        def _(pool):
            chain = Chain(pool, pch)
            chain.link(nc.gpsimd.memset(m.ones32[:], 1.0))

        @block.vector
        def _(dve):
            chain = Chain(dve, dch)
            dve.wait_ge(w_in, 32)
            for i in range(2):
                last = nc.vector.tensor_reduce(m.wabs[:, i:i + 1], m.tw[:, i, :], AX.X, ALU.add, apply_absolute_value=True)
            dve.wait_ge(pch, 1)
            chain.link(last)
            nc.vector.tensor_copy(m.wmean[:], m.wabs[:]).then_inc(wabs, 1)
            dve.wait_ge(wsum, 1)
            chain.link(nc.vector.tensor_scalar(m.wmean[:], m.ps[:, 7, 0:2], 1.0 / w_n, LN_EPS, ALU.mult, ALU.max))
            chain.link(nc.vector.reciprocal(m.wscale[:], m.wmean[:]))
            chain.link(nc.vector.reciprocal(m.wmean[:], m.wscale[:]))
            for i in range(2):
                last = nc.vector.tensor_scalar(m.tw[:, i, :], m.tw[:, i, :], m.wscale[:, i:i + 1], ROUND, ALU.mult, ALU.add)
            chain.link(last)
            chain.link(nc.vector.tensor_scalar(m.tw[:], m.tw[:], ROUND, 1.0, ALU.subtract, ALU.min))
            nc.vector.tensor_scalar(m.tern[:], m.tw[:], -1.0, None, ALU.max).then_inc(wq, 1)
            chain.link(nc.vector.tensor_tensor(m.x[:], m.x[:], m.state[:], ALU.add))
            row_statistics(dve, chain, m.x[:], T, D, m.st)
            for t in range(T):
                last = normalise(dve, m.state[:], m.x[:], t, m.st)
            chain.link(last)
            row_statistics(dve, chain, m.state[:], T, D, m.st)
            for t in range(T):
                last = normalise(dve, m.hat[:], m.state[:], t, m.st)
            chain.link(last)
            dve.wait_ge(rows_in, 16)
            chain.link(nc.vector.tensor_tensor(m.hat[:], m.hat[:], m.frow[:, 0:D].unsqueeze(1).to_broadcast([P, T, D]), ALU.mult))
            chain.link(nc.vector.tensor_tensor(m.hat[:], m.hat[:], m.frow[:, D:2 * D].unsqueeze(1).to_broadcast([P, T, D]), ALU.add))
            for b in range(B):
                quantise(dve, chain, m.hat[:], D, b * TB, (b + 1) * TB, m.qrow).then_inc(q1, 1)
            chain.link(nc.vector.tensor_scalar(m.step[:], m.step[:], m.wmean[:, 0:1], None, ALU.mult))
            at = 2 * D
            for n in range(T):
                dve.wait_ge(h_ps, n + 1)
                nc.vector.scalar_tensor_tensor(out=hid[:, n, :], in0=m.ps[:, 2 + n % 4, :], scalar=m.step[:, n:n + 1],
                                               in1=m.frow[:, at:at + HID], op0=ALU.mult, op1=ALU.add).then_inc(h_in, 1)
            dve.wait_ge(h_sb, T)
            row_statistics(dve, chain, hid[:], T, HID, m.st)
            for t in range(T):
                last = normalise(dve, hid[:], hid[:], t, m.st)
            chain.link(last)
            for b in range(B):
                rows = hid[:, b * TB:(b + 1) * TB, :]
                chain.link(nc.vector.tensor_tensor(rows, rows, m.frow[:, at + HID:at + 2 * HID].unsqueeze(1).to_broadcast([P, TB, HID]), ALU.mult))
                chain.link(nc.vector.tensor_tensor(rows, rows, m.frow[:, at + 2 * HID:at + 3 * HID].unsqueeze(1).to_broadcast([P, TB, HID]), ALU.add))
                quantise(dve, chain, hid[:], HID, b * TB, (b + 1) * TB, m.qhid).then_inc(q2, 1)
            chain.link(nc.vector.tensor_scalar(m.step[:], m.step[:], m.wmean[:, 1:2], None, ALU.mult))
            chain.link(nc.vector.tensor_tensor(m.x[:], m.x[:], m.frow[:, at + 3 * HID:at + 3 * HID + D].unsqueeze(1).to_broadcast([P, T, D]), ALU.add))
            for n in range(T):
                b, t = n // TB, n % TB
                dve.wait_ge(o_ps, (b + 1) * TB)
                last = nc.vector.scalar_tensor_tensor(out=m.x[:, n, :], in0=m.ps[:, 4 + b % 2, t * P:(t + 1) * P], scalar=m.step[:, n:n + 1],
                                                      in1=m.x[:, n, :], op0=ALU.mult, op1=ALU.add)
                if t == TB - 1:
                    last.then_inc(done, 1)


def build(nc, a):
    with ExitStack() as ctx:
        def sb(name, shape, dt=F32):
            return ctx.enter_context(nc.sbuf_tensor(name, shape, dt))

        big = sb("big", [P, T * HID])
        k6 = sb("k6", [P, 2, HEADS, S], BF16)
        w = sb("w", [P, W_COLS])
        vaug = sb("vaug", [P, B, TB, HEADS, 32])
        def early(lo, *shape):
            names = [f"d{i}" for i in range(len(shape))]
            flat = w[:, lo:lo + int(np.prod(shape))]
            return flat.rearrange(f"p ({' '.join(names)}) -> p {' '.join(names)}", **dict(zip(names, shape)))

        m = Memory()
        m.ps = ctx.enter_context(nc.psum_tensor("ps", [P, 8, 512], F32))
        m.x = sb("x", [P, T, D])
        m.state = sb("state", [P, T, D])
        m.hat = sb("hat", [P, T, D])
        m.xnT = sb("xnT", [P, B, S])
        m.ident = sb("ident", [P, P])
        m.ident_bf = sb("ident_bf", [P, P], BF16)
        m.st = Statistics()
        m.st.bn = sb("bn", [P, T, 6])
        m.st.mv = sb("mv", [P, T, 2])
        m.st.var = sb("var", [P, T])
        m.st.tmp = sb("tmp", [P, T])
        m.st.rstd = sb("rstd", [P, T])
        m.ctx = sb("ctx", [P, B, D])
        m.ctx_hat = early(1536, B, D)
        m.ctxn = early(2048, NC_ALL)
        m.ctxT = sb("ctxT", [P, NC_ALL])
        m.rows0 = early(0, 6, D)
        m.cols0 = sb("cols0", [P, 10])
        m.mats0 = early(768, 6, D)
        m.sigma = early(3620, D)
        m.cond_rows = sb("cond_rows", [P, B, D])
        m.condT = sb("condT", [P, B])
        m.cos = sb("cos", [P, S])
        m.sin = sb("sin", [P, S])
        m.mask_u8 = sb("mask_u8", [B, S], U8)
        m.cmask_u8 = sb("cmask_u8", [B, N_CTX], U8)
        m.negmask = sb("negmask", [B, S], BF16)
        m.negcmask = sb("negcmask", [B, N_CTX], BF16)
        m.shift_rows = big[0:6, 0:HEADS * S // 2].bitcast(BF16).rearrange("r (h n) -> r h n", h=HEADS)
        m.tri = sb("tri", [P, P], BF16)
        m.ones = sb("ones", [P, P], BF16)
        m.invsum = sb("invsum", [P, GROUPS, TB, 4])
        m.prefer = sb("prefer", [P, EXPERTS])
        m.slot_k = early(2400, NC_ALL)
        m.slot_vT = early(2750, NC_ALL)
        m.slot_v = early(3100, B, D + 1)
        m.qT = big[:, 0:B * S].rearrange("p (b n) -> p b n", b=B)
        m.attn = big[:, B * S:2 * B * S].rearrange("p (b n) -> p b n", b=B)
        m.rowmx = sb("rowmx", [P, B])
        m.negmx = sb("negmx", [P, B])
        m.psum_rows = sb("psum_rows", [P, B])
        m.colsum = sb("colsum", [P, T])
        m.wg = sb("wg", [P, EXPERTS])
        m.logits = sb("logits", [P, T, EXPERTS])
        m.rest = sb("rest", [P, T, EXPERTS])
        m.pick = sb("pick", [P, T, EXPERTS])
        m.gate = sb("gate", [P, T, EXPERTS])
        m.top = sb("top", [P, TOP_K, T])
        m.best = sb("best", [P, T])
        m.onehot = sb("onehot", [P, TOP_K, T, EXPERTS])
        m.onehot_bf = sb("onehot_bf", [P, TOP_K, T, EXPERTS], BF16)
        m.rank = sb("rank", [P, 2, T, EXPERTS])
        m.total = sb("total", [P, EXPERTS])
        m.share = sb("share", [P, EXPERTS, T])
        m.share2 = sb("share2", [P, 2, T])
        m.hT = big[:, 0:2 * CH * S].rearrange("p (i c n) -> p i c n", i=2, c=CH)
        m.fc = big[:, 4096:4096 + 2 * HID].rearrange("p (u n) -> p u n", u=2)
        m.proj = big[:, 5120:5120 + 2 * HID].rearrange("p (u c n) -> p u c n", u=2, c=CH)
        m.w = w
        m.cols = sb("cols", [P, 10])
        m.f2b = sb("f2b", [P, D])
        m.ada = sb("ada", [P, 2 * B])
        m.k6 = k6
        m.kc6 = sb("kc6", [P, B, HEADS, P], BF16)
        m.q6 = sb("q6", [P, 2, PAIRS, S], BF16)
        m.vaug = vaug
        m.vcaug = sb("vcaug", [P, B, HEADS, 32])
        m.rot = big[:, 0:2 * S].rearrange("p (i n) -> p i n", i=2)
        m.left = big[:, 4 * S:6 * S].rearrange("p (i n) -> p i n", i=2)
        m.swap = big[:, 8 * S:10 * S].rearrange("p (i n) -> p i n", i=2)
        m.parts = big[:, 10 * S:16 * S].bitcast(BF16).rearrange("p (i c n) -> p i c n", i=4, c=3)
        m.probs = big[:, 0:8 * S].rearrange("p (i u n) -> p i u n", i=2, u=4)
        m.unit = big[:, 8 * S:10 * S].rearrange("p (i n) -> p i n", i=2)
        m.inverse = big[:, 10 * S:12 * S].rearrange("p (i t h r) -> p i t h r", i=2, t=TB, h=4)
        m.on = big[:, 12 * S:16 * S].rearrange("p (g n) -> p g n", g=GROUPS)
        m.units = big[:, 0:8 * S].rearrange("p (i g n) -> p i g n", i=2, g=GROUPS)
        m.inverses = big[:, 8 * S:12 * S].rearrange("p (g t r) -> p g t r", g=GROUPS, r=32)
        m.q6_third = big[:, 12 * S:16 * S].bitcast(BF16).rearrange("p (i n) -> p i n", i=PAIRS)
        m.cprobs = (m.xnT, m.hat[:].rearrange("p t d -> p (t d)").rearrange("p (j n) -> p j n", j=4))
        m.maxima = sb("maxima", [P, TB, HEADS])
        m.mcparts = sb("mcparts", [P, TB, 2, 3, PAIRS], BF16)
        m.mct = sb("mct", [3 * HEADS, 2, S], BF16)
        m.mparts = sb("mparts", [P, 2, TB, 2, 3, 2], BF16)
        m.mt = m.mct[0:12]
        m.hid = big[:].rearrange("p (t n) -> p t n", t=T)
        m.tw = w[:, 0:2 * HID].rearrange("p (i n) -> p i n", i=2)
        m.tern = vaug[:, 1, 0].rearrange("p h n -> p (h n)").bitcast(BF16).rearrange("p (i n) -> p i n", i=2)
        m.frow = w[:, 2 * HID:5 * HID + 3 * D]
        m.wabs = sb("wabs", [P, 2])
        m.wmean = sb("wmean", [P, 2])
        m.wscale = sb("wscale", [P, 2])
        m.ones32 = sb("ones32", [P, P])
        m.absmax = sb("absmax", [P, T])
        m.qscale = sb("qscale", [P, T])
        m.step = sb("step", [P, T])
        m.qrow = vaug[:, 0, 0:2].rearrange("p t h n -> p (t h n)").bitcast(BF16).rearrange("p (t d) -> p t d", t=T)
        m.qT_bf = vaug[:, 1, 1].rearrange("p h n -> p (h n)").bitcast(BF16).rearrange("p (i n) -> p i n", i=2)
        m.qhid = k6[:, 0].rearrange("p h n -> p (h n)")[:, 0:T * HID].rearrange("p (t n) -> p t n", t=T)
        with stage(nc) as sem:
            load_and_prepare(nc, a, m, sem)
        with nc.Fori(0, SLOT_STEPS), stage(nc) as sem:
            slot_step(nc, a, m, sem)
        with stage(nc) as sem:
            route_tokens(nc, a, m, sem)
        with nc.Fori(0, EXPERTS // 2) as pair, stage(nc) as sem:
            expert_pair(nc, a, m, sem, pair)
        with stage(nc) as sem:
            begin_layers(nc, a, m, sem)
        with nc.Fori(0, LAYERS) as layer, stage(nc) as sem:
            project(nc, a, m, sem, layer, False)
            attend(nc, a, m, sem)
            project(nc, a, m, sem, layer, True)
            attend_context(nc, a, m, sem)
            feed_forward(nc, a, m, sem)
        with stage(nc) as sem:
            quantised_block(nc, a, m, sem)


def rotary_tables():
    half = HD // 2
    inv = np.float32(1.0) / np.power(np.float32(10000.0), np.arange(half, dtype=np.float32) / np.float32(half))
    ang = np.arange(S, dtype=np.float32)[:, None] * inv
    cos, sin = np.cos(ang).T.astype(np.float32), np.sin(ang).T.astype(np.float32)
    return np.tile(np.concatenate([cos, cos]), (HEADS, 1)), np.tile(np.concatenate([-sin, sin]), (HEADS, 1))


def lay_out(i):
    swap = np.arange(D).reshape(HEADS, 2, HD // 2)[:, ::-1].reshape(D)
    i = {k: np.asarray(v) for k, v in i.items()}
    L0, L1, F = "L0_xcond_", "L1_xcond_", "L1_ffn_"

    def out_rows(w):
        r = np.zeros((4, 32, GROUPS, D), np.float32)
        r[:, 0:HD] = w.T.reshape(GROUPS, 4, HD, D).transpose(1, 2, 0, 3)
        return r.reshape(P, GROUPS * D)

    def layer(n):
        qkv = i[L1 + "qkv_w"][n]
        q, k, v = qkv[0:D], qkv[D:2 * D], qkv[2 * D:]
        cq, ck = i[L1 + "cq_w"][n], i[L1 + "ck_w"][n]
        f2 = i[L1 + "f2_w"][n].T.reshape(CH, P, D).transpose(1, 0, 2).reshape(P, HID)
        return np.concatenate([i[L1 + "n1_w"][n].T, q.T, q[swap].T, k.T, k[swap].T, v.T, out_rows(i[L1 + "so_w"][n]),
                               i[L1 + "n2_w"][n].T, cq.T, cq[swap].T, ck.T, ck[swap].T, i[L1 + "cv_w"][n].T, out_rows(i[L1 + "co_w"][n]),
                               i[L1 + "n3_w"][n].T, i[L1 + "f1_w"][n].T, f2], axis=1)

    def layer_cols(n):
        vecs = [i[L1 + k][n].reshape(-1, P) for k in ("n1_b", "n2_b", "n3_b", "f1_b")]
        return np.concatenate(vecs).T

    cos, sin = rotary_tables()
    got = {
        "x": i["x"], "ctx": i["ctx_1024"], "cond": i["cond_1024"], "condT": i["cond_1024"].T,
        "mask": i["mask_BxS_bf0"], "cmask": i["mask_BxS2_bf0"], "cos": cos, "sin": sin,
        "slot_mats": np.stack([i[L0 + k] for k in ("wk", "wv", "wq", "wu", "w1", "w2")], axis=1),
        "slot_cols": np.stack([i[L0 + k] for k in ("lnkv_g", "lnkv_b", "lnq_g", "lnq_b", "lnm_g", "lnm_b", "bk", "bv", "bq", "b1")], axis=1),
        "slot_rows": np.stack([i[L0 + k].reshape(D) for k in ("q_mu", "q_logsig", "lnp_g", "lnp_b", "bu", "b2")]),
        "w_g": i["L0_ffn_w_g"], "c_fc": i["L0_ffn_c_fc"],
        "c_proj": i["L0_ffn_c_proj"].reshape(EXPERTS, CH, P, D).transpose(0, 2, 1, 3),
        "w": np.stack([layer(n) for n in range(LAYERS)]), "cols": np.stack([layer_cols(n) for n in range(LAYERS)]),
        "f2_b": i[L1 + "f2_b"],
        "ffn_w1": i[F + "w1"].T, "ffn_w2": i[F + "w2"].T.reshape(CH, P, D).transpose(1, 0, 2).reshape(P, HID),
        "ffn_rows": np.concatenate([i[F + k] for k in ("ln1_w", "ln1_b", "b1", "ln2_w", "ln2_b", "b2")]),
    }
    return {k: np.ascontiguousarray(v) for k, v in got.items()}


SCRATCH = {"neg_mask": ((B, S), BF16), "neg_cmask": ((B, N_CTX), BF16), "queries": ((B, P, PRODUCTS, S), BF16),
           "keys": ((B, P, PRODUCTS, S), BF16), "ctx_keys": ((P, PRODUCTS, NC_ALL), BF16)}


def kernel(**inputs):
    import concourse.bacc as bacc
    from concourse.bass_utils import run_bass_kernel_spmd

    nc = bacc.Bacc("TRN2", target_bir_lowering=False, num_devices=1)
    arrays = lay_out(inputs)
    a = {k: nc.dram_tensor(f"in_{k}", v.shape, mybir.dt.from_np(v.dtype), kind="ExternalInput").ap() for k, v in arrays.items()}
    a |= {k: nc.dram_tensor(f"scratch_{k}", shape, dt, kind="Internal").ap() for k, (shape, dt) in SCRATCH.items()}
    a["out"] = nc.dram_tensor("out", (B, S, D), F32, kind="ExternalOutput").ap()
    build(nc, a)
    r = run_bass_kernel_spmd(nc, [{f"in_{k}": v for k, v in arrays.items()}], core_ids=[0])
    return r.results[0]["out"]
```

```python
from contextlib import ExitStack, contextmanager

import numpy as np

import concourse.bass as bass
from concourse import mybir

ALU = mybir.AluOpType
ACT = mybir.ActivationFunctionType
AX = mybir.AxisListType
F32 = mybir.dt.float32
BF16 = mybir.dt.bfloat16
I32 = mybir.dt.int32
U8 = mybir.dt.uint8

P = 128
B, S, D = 4, 512, 128
TB = S // P
T = B * TB
N_CTX = 77
NC_ALL = B * N_CTX
SLOT_STEPS = 3
EXPERTS, HID, TOP_K = 8, 512, 2
AT_ONCE = 4
CH = HID // P
CAPACITY = int(TOP_K * 1.25 * B * S / EXPERTS)
CAPACITY += CAPACITY % 2
LAYERS, HEADS, HD = 6, 16, 8
PAIRS = HEADS // 2
GROUPS = HEADS // 4
UNITS = B * GROUPS
LN_EPS = 1e-5
ROUND = 1.5 * 2.0 ** 23
TWO_ONES = float(np.frombuffer(np.array([0x3F803F80], np.uint32).tobytes(), np.float32)[0])
MASKED = -1e30
RSQRT_SEED = 0x5F3759DF
ROOT_STEPS = 3
MOMENTS = 2 * TB + 2

PRODUCTS = 6
ROWS_HEAD = HD * PRODUCTS
ROW_MASK = 2 * ROWS_HEAD
ROW_SHIFT = ROW_MASK + 1
ROWS_MAX = ROW_SHIFT
ROWS_ALL = ROW_SHIFT + 6

SECTIONS = (("n1", 2 * D), ("q", D), ("qr", D), ("k", D), ("kr", D), ("v", D), ("so", GROUPS * D), ("n2", 2 * D), ("cq", D), ("cqr", D),
            ("ck", D), ("ckr", D), ("cv", D), ("co", GROUPS * D), ("n3", 2 * D), ("f1", HID), ("f2", HID))
COLS, _at = {}, 0
for _name, _width in SECTIONS:
    COLS[_name] = (_at, _at + _width)
    _at += _width
W_COLS = _at
COLS_FIRST = 4
W_FIRST = COLS["so"][0]


class Memory:
    pass


class Statistics:
    pass


class Chain:

    def __init__(self, engine, sem):
        self.engine, self.sem, self.n = engine, sem, 0

    def link(self, instruction):
        self.n += 1
        instruction.then_inc(self.sem, 1)
        self.engine.wait_ge(self.sem, self.n)


def row_moments(dve, chain, rows, tiles, st, first=0):
    n = rows.shape[0]
    for t in range(first, first + tiles):
        last = dve.bn_stats(st.bn[:n, t, :], rows[:, t, :])
    chain.link(last)
    for t in range(first, first + tiles):
        last = dve.bn_aggr(st.mv[:n, t, :], st.bn[:n, t, :])
    chain.link(last)


def root_seed(dve, chain, n, tiles, st, first=0):
    var, a, r = (v[:n, first:first + tiles] for v in (st.var, st.tmp, st.rstd))
    chain.link(dve.tensor_scalar(var, st.mv[:n, first:first + tiles, 1], LN_EPS, None, ALU.add))
    chain.link(dve.tensor_scalar(a.bitcast(I32), var.bitcast(I32), 1, None, ALU.arith_shift_right))
    chain.link(dve.tensor_scalar(r.bitcast(I32), a.bitcast(I32), -1.0, float(RSQRT_SEED), ALU.mult, ALU.add))


def root_step(dve, chain, n, tiles, st, first=0):
    var, a, r = (v[:n, first:first + tiles] for v in (st.var, st.tmp, st.rstd))
    chain.link(dve.tensor_tensor(a, r, r, ALU.mult))
    chain.link(dve.scalar_tensor_tensor(out=a, in0=a, scalar=-0.5, in1=var, op0=ALU.mult, op1=ALU.mult))
    return dve.scalar_tensor_tensor(out=r, in0=a, scalar=1.5, in1=r, op0=ALU.add, op1=ALU.mult)


def row_statistics(dve, chain, rows, tiles, width, st):
    n = rows.shape[0]
    row_moments(dve, chain, rows, tiles, st)
    root_seed(dve, chain, n, tiles, st)
    for _ in range(ROOT_STEPS):
        chain.link(root_step(dve, chain, n, tiles, st))


def normalise_batch(dve, chain, out, rows, b, st):
    first = b * TB
    row_moments(dve, chain, rows, TB, st, first)
    root_seed(dve, chain, P, TB, st, first)
    for _ in range(ROOT_STEPS):
        chain.link(root_step(dve, chain, P, TB, st, first))
    for t in range(first, first + TB):
        last = normalise(dve, out, rows, t, st)
    return last


def normalise(dve, out, rows, t, st):
    n = rows.shape[0]
    return dve.tensor_scalar(out[:, t, :], rows[:, t, :], st.mv[:n, t, 0:1], st.rstd[:n, t:t + 1],
                             ALU.subtract, ALU.mult)


@contextmanager
def stage(nc):
    with ExitStack() as ctx:
        sems = []

        def sem(name):
            sems.append(ctx.enter_context(nc.semaphore(name)))
            return sems[-1]

        yield sem
        numbers = sorted(s.num for s in sems)
        for i, number in enumerate(numbers):
            if i == 0 or numbers[i - 1] != number - 1:
                first = number
            if i + 1 == len(numbers) or numbers[i + 1] != number + 1:
                nc.gpsimd.sem_clear(range(first, number + 1))
        nc.all_engine_barrier()


def load_and_prepare(nc, a, m, sem):
    x_in, ctx_in, mats, rows_in, consts = sem("x_in"), sem("ctx_in"), sem("mats_in"), sem("rows_in"), sem("consts_in")
    ident, ident0, lnx, lnc, ctx_ps, ctx_sb, kv_ps, kv_sb = (sem(n) for n in (
        "identity", "identity_zero", "noise_ready", "ctx_normal", "ctx_turned", "ctx_copied", "kv_ready", "kv_copied"))
    sig, dch, pch = sem("sigma"), sem("prep_dve"), sem("prep_pool")
    vu_ps, neg, neg_out, shift_out = sem("value_ready"), sem("neg_mask"), sem("neg_mask_out"), sem("shift_rows_out")
    stack0, ones = sem("stack_zero"), sem("stack_one")

    with nc.Block() as block:
        @block.sync
        def _(sp):
            sp.dma_start(m.x[:], a["x"].rearrange("b (t p) d -> p (b t) d", p=P)).then_inc(x_in, 16)
            sp.dma_start(m.ctx[0:N_CTX], a["ctx"].rearrange("b n d -> n b d")).then_inc(ctx_in, 16)
            sp.dma_start(m.rows0[:], a["slot_rows"].partition_broadcast(P)).then_inc(rows_in, 16)
            sp.dma_start(m.cols0[:], a["slot_cols"]).then_inc(mats, 16)
            sp.dma_start(m.mats0[:], a["slot_mats"]).then_inc(mats, 16)
            sp.dma_start(m.cond_rows[:], a["cond"].rearrange("b d -> (b d)").partition_broadcast(P)).then_inc(consts, 16)
            sp.dma_start(m.condT[:], a["condT"]).then_inc(consts, 16)
            sp.dma_start(m.cos[:], a["cos"]).then_inc(consts, 16)
            sp.dma_start(m.sin[:], a["sin"]).then_inc(consts, 16)
            sp.dma_start(m.mask_u8[:], a["mask"]).then_inc(consts, 16)
            sp.dma_start(m.cmask_u8[:], a["cmask"]).then_inc(consts, 16)
            sp.wait_ge(neg, 2)
            sp.dma_start(a["neg_mask"], m.negmask[:]).then_inc(neg_out, 16)
            sp.dma_start(a["neg_cmask"], m.negcmask[:]).then_inc(neg_out, 16)
            sp.wait_ge(neg_out, 32)
            sp.wait_ge(stack0, 2)
            sp.wait_ge(pch, 3)
            for i in range(2):
                sp.dma_start(m.k6[ROW_SHIFT:ROWS_ALL, i], m.shift_rows[:]).then_inc(shift_out, 16)
            for b in range(B):
                sp.dma_start(m.kc6[ROW_SHIFT:ROWS_ALL, b, :, 0:N_CTX], m.shift_rows[:, :, 0:N_CTX]).then_inc(shift_out, 16)
                sp.dma_start(m.kc6[ROW_MASK:ROW_MASK + 1, b, :, 0:N_CTX],
                             a["neg_cmask"][b:b + 1, :].unsqueeze(1).to_broadcast([1, HEADS, N_CTX])).then_inc(shift_out, 16)
            sp.wait_ge(shift_out, 16 * (2 + 2 * B))
            sp.wait_ge(consts, 96)

        @block.gpsimd
        def _(pool):
            chain = Chain(pool, pch)
            pool.memset(m.ident[:], 0.0).then_inc(ident0, 1)
            pool.wait_ge(ident0, 1)
            pool.affine_select(out=m.ident[:], in_=m.ident[:], compare_op=ALU.not_equal, fill=1.0, base=0,
                               pattern=[[-1, P]], channel_multiplier=1).then_inc(ident, 1)
            pool.wait_ge(ident, 1)
            pool.tensor_copy(m.ident_bf[:], m.ident[:]).then_inc(ident, 1)
            chain.link(pool.memset(m.shift_rows[:], -1.0))
            by_pair = m.shift_rows[:].rearrange("r (i u) n -> r i u n", u=2)
            chain.link(pool.affine_select(out=by_pair[:, :, 0, :], in_=by_pair[:, :, 0, :], compare_op=ALU.is_ge,
                                          fill=0.0, base=2, pattern=[[0, PAIRS], [0, S]], channel_multiplier=-1))
            chain.link(pool.affine_select(out=by_pair[:, :, 1, :], in_=by_pair[:, :, 1, :], compare_op=ALU.is_ge,
                                          fill=0.0, base=-3, pattern=[[0, PAIRS], [0, S]], channel_multiplier=1))
            chain.link(pool.memset(m.tri[:], 1.0))
            chain.link(pool.affine_select(out=m.tri[:], in_=m.tri[:], compare_op=ALU.is_ge, fill=0.0, base=0,
                                          pattern=[[1, P]], channel_multiplier=-1))
            for e in range(EXPERTS):
                last = pool.memset(m.prefer[:, e:e + 1], float(EXPERTS - e))
            chain.link(last)
            pool.memset(m.k6[:].rearrange("p i h n -> p (i h n)").bitcast(F32), 0.0).then_inc(stack0, 1)
            pool.wait_ge(stack0, 1)
            pool.memset(m.kc6[:].rearrange("p b h n -> p (b h n)").bitcast(F32), 0.0).then_inc(stack0, 1)
            pool.wait_ge(stack0, 2)
            chain.link(pool.memset(m.q6[:].rearrange("p i h n -> p (i h n)").bitcast(F32), 0.0))
            chain.link(pool.memset(m.q6[ROW_MASK:ROW_MASK + 1], 1.0))
            chain.link(pool.memset(m.vaug[:], 0.0))
            chain.link(pool.memset(m.vcaug[:], 0.0))
            chain.link(pool.memset(m.vaug[:, :, :, :, HD:HD + 1], 1.0))
            chain.link(pool.memset(m.vcaug[0:N_CTX, :, :, HD:HD + 1], 1.0))

        @block.scalar
        def _(act):
            act.wait_ge(rows_in, 16)
            nc.scalar.activation(m.sigma[:], m.rows0[:, 1, :], ACT.Exp).then_inc(sig, 1)
            act.wait_ge(mats, 32)
            act.wait_ge(ctx_ps, 1)
            nc.scalar.activation(m.ctxn[:], m.ps[:, 0, 0:NC_ALL], ACT.Identity, bias=m.cols0[:, 1:2],
                                 scale=m.cols0[:, 0:1]).then_inc(ctx_sb, 1)
            act.wait_ge(ctx_ps, 2)
            nc.scalar.copy(m.ctxT[:], m.ps[:, 1, 0:NC_ALL]).then_inc(ctx_sb, 1)
            act.wait_ge(kv_ps, 1)
            nc.scalar.activation(m.slot_k[:], m.ps[:, 2, 0:NC_ALL], ACT.Identity, bias=m.cols0[:, 6:7]).then_inc(kv_sb, 1)
            act.wait_ge(kv_ps, 2)
            nc.scalar.activation(m.slot_vT[:], m.ps[:, 3, 0:NC_ALL], ACT.Identity, bias=m.cols0[:, 7:8]).then_inc(kv_sb, 1)
            act.wait_ge(vu_ps, 1)
            nc.scalar.copy(m.slot_v[0:N_CTX, :, 0:D], m.ps[0:N_CTX, 4, :].rearrange("n (b d) -> n b d", b=B)).then_inc(kv_sb, 1)

        @block.tensor
        def _(pe):
            pe.wait_ge(ident, 2)
            pe.wait_ge(lnc, 1)
            for b in range(B):
                last = nc.tensor.transpose(m.ps[:, 0, b * N_CTX:(b + 1) * N_CTX], m.ctx_hat[0:N_CTX, b, :], m.ident[0:N_CTX, 0:N_CTX])
            last.then_inc(ctx_ps, 1)
            for b in range(B):
                last = nc.tensor.transpose(m.ps[:, 1, b * N_CTX:(b + 1) * N_CTX], m.ctx[0:N_CTX, b, :], m.ident[0:N_CTX, 0:N_CTX])
            last.then_inc(ctx_ps, 1)
            pe.wait_ge(mats, 32)
            pe.wait_ge(ctx_sb, 1)
            nc.tensor.matmul(m.ps[:, 2, 0:NC_ALL], m.mats0[:, 0, :], m.ctxn[:], start=True, stop=True).then_inc(kv_ps, 1)
            nc.tensor.matmul(m.ps[:, 3, 0:NC_ALL], m.mats0[:, 1, :], m.ctxn[:], start=True, stop=True).then_inc(kv_ps, 1)
            pe.wait_ge(kv_sb, 2)
            for b in range(B):
                last = nc.tensor.matmul(m.ps[0:N_CTX, 4, b * D:(b + 1) * D], m.slot_vT[:, b * N_CTX:(b + 1) * N_CTX],
                                        m.mats0[:, 3, :], start=True, stop=True)
            last.then_inc(vu_ps, 1)

        @block.vector
        def _(dve):
            chain = Chain(dve, dch)
            dve.memset(m.slot_v[:, :, D:D + 1], 1.0)
            chain.link(dve.memset(m.ones[:], 1.0))
            dve.wait_ge(consts, 96)
            dve.tensor_scalar(m.negmask[:], m.mask_u8[:], MASKED, None, ALU.mult).then_inc(neg, 1)
            dve.tensor_scalar(m.negcmask[:], m.cmask_u8[:], MASKED, None, ALU.mult).then_inc(neg, 1)
            dve.wait_ge(ctx_in, 16)
            row_statistics(dve, chain, m.ctx[0:N_CTX], B, D, m.st)
            for b in range(B):
                last = normalise(dve, m.ctx_hat[0:N_CTX], m.ctx[0:N_CTX], b, m.st)
            last.then_inc(lnc, 1)
            dve.wait_ge(lnc, 1)
            dve.wait_ge(x_in, 16)
            row_statistics(dve, chain, m.x[:], T, D, m.st)
            for t in range(T):
                last = normalise(dve, m.hat[:], m.x[:], t, m.st)
            chain.link(last)
            dve.wait_ge(sig, 1)
            chain.link(dve.tensor_tensor(m.hat[:], m.hat[:], m.sigma[:].unsqueeze(1).to_broadcast([P, T, D]), ALU.mult))
            chain.link(dve.tensor_tensor(m.state[:], m.hat[:], m.rows0[:, 0:1, :].to_broadcast([P, T, D]), ALU.add))
            dve.tensor_tensor(m.cond_rows[:], m.cond_rows[:], m.rows0[:, 5:6, :].to_broadcast([P, B, D]), ALU.add).then_inc(lnx, 1)


def slot_step(nc, a, m, sem):
    names = ("sl_dve", "sl_hat", "sl_turned", "sl_qin", "sl_q_ps", "sl_q", "sl_logits", "sl_max", "sl_p", "sl_attn",
             "sl_upd", "sl_new", "sl_biased")
    (dch, hat, turned, qin, q_ps, q_sb, logits, mx, probs, attn, upd, new, biased) = [sem(n) for n in names]
    scale = float(np.float32(1.0) / np.float32(D ** -0.5))
    with nc.Block() as block:
        @block.gpsimd
        def _(pool):
            pool.wait_ge(hat, B)
            nc.gpsimd.tensor_tensor(m.state[:], m.state[:], m.rows0[:, 4:5, :].to_broadcast([P, T, D]), ALU.add).then_inc(biased, 1)

        @block.tensor
        def _(pe):
            def turn(b):
                pe.wait_ge(hat, b + 1)
                if b >= 2:
                    pe.wait_ge(qin, b - 1)
                for t in range(TB):
                    last = nc.tensor.transpose(m.ps[:, b % 2, t * P:(t + 1) * P], m.hat[:, b * TB + t, :], m.ident[:])
                last.then_inc(turned, 1)

            def queries(b):
                pe.wait_ge(qin, b + 1)
                if b >= 2:
                    pe.wait_ge(q_sb, b - 1)
                nc.tensor.matmul(m.ps[:, 2 + b % 2, :], m.mats0[:, 2, :], m.xnT[:, b, :], start=True, stop=True).then_inc(q_ps, 1)

            def similarities(b):
                pe.wait_ge(q_sb, b + 1)
                if b >= 2:
                    pe.wait_ge(probs, b - 1)
                nc.tensor.matmul(m.ps[0:N_CTX, 4 + b % 2, :], m.slot_k[:, b * N_CTX:(b + 1) * N_CTX], m.qT[:, b, :],
                                 start=True, stop=True).then_inc(logits, 1)

            for k in range(B + 2):
                if k < B:
                    turn(k)
                if 0 <= k - 1 < B:
                    queries(k - 1)
                if k >= 2:
                    similarities(k - 2)
            for b in range(B):
                pe.wait_ge(attn, b + 1)
                for i in range(TB // 2):
                    n = b * TB // 2 + i
                    if n >= 2:
                        pe.wait_ge(new, n - 1)
                    for t in (2 * i, 2 * i + 1):
                        at = t % 2 * 2 * P
                        last = nc.tensor.matmul(m.ps[:, 6 + n % 2, at:at + D + 1], m.attn[0:N_CTX, b, t * P:(t + 1) * P],
                                                m.slot_v[0:N_CTX, b, :], start=True, stop=True)
                    last.then_inc(upd, 1)

        @block.scalar
        def _(act):
            for k in range(B + 2):
                if k < B:
                    act.wait_ge(turned, k + 1)
                    nc.scalar.activation(m.xnT[:, k, :], m.ps[:, k % 2, :], ACT.Identity, bias=m.cols0[:, 3:4],
                                         scale=m.cols0[:, 2:3]).then_inc(qin, 1)
                b = k - 1
                if 0 <= b < B:
                    act.wait_ge(q_ps, b + 1)
                    nc.scalar.activation(m.qT[:, b, :], m.ps[:, 2 + b % 2, :], ACT.Identity, bias=m.cols0[:, 8:9]).then_inc(q_sb, 1)
                b = k - 2
                if b >= 0:
                    act.wait_ge(mx, b + 1)
                    nc.scalar.activation(m.attn[0:N_CTX, b, :], m.ps[0:N_CTX, 4 + b % 2, :], ACT.Exp, bias=m.negmx[0:N_CTX, b:b + 1],
                                         scale=scale, accum_out=m.psum_rows[0:N_CTX, b:b + 1]).then_inc(probs, 1)

        @block.vector
        def _(dve):
            chain = Chain(dve, dch)
            row_statistics(dve, chain, m.state[:], T, D, m.st)
            for b in range(B):
                for t in range(TB):
                    last = normalise(dve, m.hat[:], m.state[:], b * TB + t, m.st)
                last.then_inc(hat, 1)
            for b in range(B):
                dve.wait_ge(logits, b + 1)
                chain.link(nc.vector.reduce_max(m.rowmx[0:N_CTX, b:b + 1], m.ps[0:N_CTX, 4 + b % 2, :], AX.X))
                nc.vector.tensor_scalar(m.negmx[0:N_CTX, b:b + 1], m.rowmx[0:N_CTX, b:b + 1], -scale, None, ALU.mult).then_inc(mx, 1)
                dve.wait_ge(probs, b + 1)
                chain.link(nc.vector.reciprocal(m.rowmx[0:N_CTX, b:b + 1], m.psum_rows[0:N_CTX, b:b + 1]))
                nc.vector.tensor_scalar(m.attn[0:N_CTX, b, :], m.attn[0:N_CTX, b, :], m.rowmx[0:N_CTX, b:b + 1], 1e-8,
                                        ALU.mult, ALU.add).then_inc(attn, 1)
            dve.wait_ge(biased, 1)
            for n in range(T // 2):
                dve.wait_ge(upd, n + 1)
                both = m.ps[:, 6 + n % 2, :].rearrange("p (t c) -> p t c", t=2)
                chain.link(nc.vector.reciprocal(m.colsum[:, 2 * n:2 * n + 2], both[:, :, D]))
                for t in range(2):
                    at = 2 * n + t
                    last = nc.vector.scalar_tensor_tensor(out=m.state[:, at, :], in0=both[:, t, 0:D], scalar=m.colsum[:, at:at + 1],
                                                          in1=m.state[:, at, :], op0=ALU.mult, op1=ALU.add)
                last.then_inc(new, 1)

    names = ("sm_dve", "sm_hat", "sm_turned", "sm_in", "sm_h_ps", "sm_h", "sm_out", "sm_added", "sm_normal", "sm_gained")
    (dch, hat, turned, hin, h_ps, h_sb, out_ps, added, normal, gained) = [sem(n) for n in names]
    with nc.Block() as block:
        @block.tensor
        def _(pe):
            def turn(b):
                pe.wait_ge(hat, b + 1)
                if b >= 2:
                    pe.wait_ge(hin, b - 1)
                for t in range(TB):
                    last = nc.tensor.transpose(m.ps[:, b % 2, t * P:(t + 1) * P], m.hat[:, b * TB + t, :], m.ident[:])
                last.then_inc(turned, 1)

            def up(b):
                pe.wait_ge(hin, b + 1)
                if b >= 2:
                    pe.wait_ge(h_sb, b - 1)
                nc.tensor.matmul(m.ps[:, 2 + b % 2, :], m.mats0[:, 4, :], m.xnT[:, b, :], start=True, stop=True).then_inc(h_ps, 1)

            def down(b):
                pe.wait_ge(h_sb, b + 1)
                for t in range(TB):
                    last = nc.tensor.matmul(m.ps[:, 4 + b, t * P:(t + 1) * P], m.qT[:, b, t * P:(t + 1) * P], m.mats0[:, 5, :],
                                            start=True, stop=True)
                last.then_inc(out_ps, 1)

            for k in range(B + 2):
                if k < B:
                    turn(k)
                if 0 <= k - 1 < B:
                    up(k - 1)
                if k >= 2:
                    down(k - 2)

        @block.scalar
        def _(act):
            for k in range(B + 1):
                if k < B:
                    act.wait_ge(turned, k + 1)
                    nc.scalar.activation(m.xnT[:, k, :], m.ps[:, k % 2, :], ACT.Identity, bias=m.cols0[:, 5:6],
                                         scale=m.cols0[:, 4:5]).then_inc(hin, 1)
                b = k - 1
                if b >= 0:
                    act.wait_ge(h_ps, b + 1)
                    nc.scalar.activation(m.qT[:, b, :], m.ps[:, 2 + b % 2, :], ACT.Gelu, bias=m.cols0[:, 9:10]).then_inc(h_sb, 1)

        @block.gpsimd
        def _(pool):
            pool.wait_ge(hat, B)
            for b in range(B):
                last = nc.gpsimd.tensor_tensor(m.state[:, b * TB:(b + 1) * TB, :], m.state[:, b * TB:(b + 1) * TB, :],
                                               m.cond_rows[:, b:b + 1, :].to_broadcast([P, TB, D]), ALU.add)
            last.then_inc(added, 1)

        @block.vector
        def _(dve):
            chain = Chain(dve, dch)
            row_statistics(dve, chain, m.state[:], T, D, m.st)
            for b in range(B):
                for t in range(TB):
                    last = normalise(dve, m.hat[:], m.state[:], b * TB + t, m.st)
                last.then_inc(hat, 1)
            dve.wait_ge(added, 1)
            for b in range(B):
                dve.wait_ge(out_ps, b + 1)
                last = nc.vector.tensor_tensor(m.state[:, b * TB:(b + 1) * TB, :], m.state[:, b * TB:(b + 1) * TB, :],
                                               m.ps[:, 4 + b, :].rearrange("p (t d) -> p t d", t=TB), ALU.add)
            chain.link(last)
            row_statistics(dve, chain, m.state[:], T, D, m.st)
            for t in range(T):
                last = normalise(dve, m.hat[:], m.state[:], t, m.st)
            chain.link(last)
            chain.link(nc.vector.tensor_tensor(m.hat[:], m.hat[:], m.rows0[:, 2:3, :].to_broadcast([P, T, D]), ALU.mult))
            nc.vector.tensor_tensor(m.state[:], m.hat[:], m.rows0[:, 3:4, :].to_broadcast([P, T, D]), ALU.add).then_inc(normal, 1)


def route_tokens(nc, a, m, sem):
    (dch, hat, turned, xt, logit, first, second, counted, wg_in, gate) = [sem(n) for n in (
        "rt_dve", "rt_hat", "rt_turned", "rt_xT", "rt_logits", "rt_first", "rt_second", "rt_counted", "rt_wg", "rt_gate")]
    expd = sem("rt_exp")
    by_e = [P, T, EXPERTS]
    with nc.Block() as block:
        @block.sync
        def _(sp):
            sp.dma_start(m.wg[:], a["w_g"]).then_inc(wg_in, 16)
            sp.wait_ge(wg_in, 16)

        @block.tensor
        def _(pe):
            pe.wait_ge(wg_in, 16)
            for b in range(B):
                pe.wait_ge(hat, b + 1)
                for t in range(TB):
                    last = nc.tensor.transpose(m.ps[:, b, t * P:(t + 1) * P], m.hat[:, b * TB + t, :], m.ident[:])
                last.then_inc(turned, 1)
            for b in range(B):
                pe.wait_ge(xt, b + 1)
                for t in range(TB):
                    at = (b * TB + t) * EXPERTS
                    last = nc.tensor.matmul(m.ps[:, 4, at:at + EXPERTS], m.xnT[:, b, t * P:(t + 1) * P], m.wg[:], start=True, stop=True)
            last.then_inc(logit, 1)
            for k, chosen in enumerate((first, second)):
                pe.wait_ge(chosen, 1)
                nc.tensor.matmul(m.ps[:, 5 + k, 0:P], m.tri[:], m.onehot_bf[:, k, :, :], start=True, stop=True)
                nc.tensor.matmul(m.ps[:, 5 + k, P:2 * P], m.ones[:], m.onehot_bf[:, k, :, :], start=True, stop=True).then_inc(counted, 1)

        @block.scalar
        def _(act):
            for b in range(B):
                act.wait_ge(turned, b + 1)
                nc.scalar.copy(m.xnT[:, b, :], m.ps[:, b, :]).then_inc(xt, 1)
            act.wait_ge(gate, 1)
            nc.scalar.activation(m.gate[:], m.gate[:], ACT.Exp).then_inc(expd, 1)

        @block.vector
        def _(dve):
            chain = Chain(dve, dch)
            chain.link(nc.vector.tensor_tensor(m.x[:], m.x[:], m.state[:], ALU.add))
            row_statistics(dve, chain, m.x[:], T, D, m.st)
            for b in range(B):
                for t in range(TB):
                    last = normalise(dve, m.hat[:], m.x[:], b * TB + t, m.st)
                last.then_inc(hat, 1)
            dve.wait_ge(logit, 1)
            lg, top, pick, rest = m.logits, m.top, m.pick, m.rest
            chain.link(nc.vector.tensor_copy(lg[:], m.ps[:, 4, 0:T * EXPERTS].rearrange("p (t e) -> p t e", e=EXPERTS)))
            chain.link(nc.vector.tensor_copy(rest[:], lg[:]))
            for k, chosen in enumerate((first, second)):
                chain.link(nc.vector.tensor_reduce(top[:, k, :], rest[:], AX.X, ALU.max))
                chain.link(nc.vector.tensor_tensor(pick[:], rest[:], top[:, k, :].unsqueeze(2).to_broadcast(by_e), ALU.is_equal))
                chain.link(nc.vector.tensor_tensor(pick[:], pick[:], m.prefer[:].unsqueeze(1).to_broadcast(by_e), ALU.mult))
                chain.link(nc.vector.tensor_reduce(m.best[:], pick[:], AX.X, ALU.max))
                chain.link(nc.vector.tensor_tensor(m.onehot[:, k], pick[:], m.best[:].unsqueeze(2).to_broadcast(by_e), ALU.is_equal))
                nc.vector.tensor_copy(m.onehot_bf[:, k], m.onehot[:, k]).then_inc(chosen, 1)
                if k == 0:
                    chain.link(nc.vector.scalar_tensor_tensor(out=rest[:], in0=m.onehot[:, 0], scalar=-3e38, in1=lg[:],
                                                              op0=ALU.mult, op1=ALU.add))
            both = m.pick
            chain.link(nc.vector.tensor_tensor(both[:], m.onehot[:, 0], m.onehot[:, 1], ALU.add))
            chain.link(nc.vector.tensor_tensor(m.gate[:], lg[:], both[:], ALU.mult))
            chain.link(nc.vector.tensor_scalar(rest[:], both[:], 1e9, -1e9, ALU.mult, ALU.add))
            chain.link(nc.vector.tensor_tensor(m.gate[:], m.gate[:], rest[:], ALU.add))
            chain.link(nc.vector.tensor_reduce(m.best[:], m.gate[:], AX.X, ALU.max))
            nc.vector.tensor_tensor(m.gate[:], m.gate[:], m.best[:].unsqueeze(2).to_broadcast(by_e), ALU.subtract).then_inc(gate, 1)
            dve.wait_ge(expd, 1)
            chain.link(nc.vector.tensor_reduce(m.best[:], m.gate[:], AX.X, ALU.add))
            chain.link(nc.vector.reciprocal(m.best[:], m.best[:]))
            chain.link(nc.vector.tensor_tensor(m.gate[:], m.gate[:], m.best[:].unsqueeze(2).to_broadcast(by_e), ALU.mult))
            dve.wait_ge(counted, 2)
            for k in range(TOP_K):
                tot, run = m.rank[:, 0], m.rank[:, 1]
                chain.link(nc.vector.tensor_copy(tot, m.ps[:, 5 + k, P:2 * P].rearrange("p (t e) -> p t e", e=EXPERTS)))
                if k == 0:
                    chain.link(nc.vector.memset(run[:, 0:1, :], 0.0))
                else:
                    chain.link(nc.vector.tensor_copy(run[:, 0:1, :], m.total[:].unsqueeze(1)))
                for t in range(1, T):
                    chain.link(nc.vector.tensor_tensor(run[:, t, :], run[:, t - 1, :], tot[:, t - 1, :], ALU.add))
                chain.link(nc.vector.tensor_tensor(m.total[:], run[:, T - 1, :], tot[:, T - 1, :], ALU.add))
                chain.link(nc.vector.tensor_tensor(run, run, m.ps[:, 5 + k, 0:P].rearrange("p (t e) -> p t e", e=EXPERTS), ALU.add))
                chain.link(nc.vector.scalar_tensor_tensor(out=m.onehot[:, k], in0=run, scalar=float(CAPACITY) + 0.5,
                                                          in1=m.onehot[:, k], op0=ALU.is_lt, op1=ALU.mult))
            chain.link(nc.vector.tensor_tensor(m.onehot[:, 0], m.onehot[:, 0], m.onehot[:, 1], ALU.add))
            nc.vector.tensor_tensor(m.share[:].rearrange("p e t -> p t e"), m.gate[:], m.onehot[:, 0], ALU.mult)
            nc.vector.memset(m.state[:], 0.0)


def some_experts(nc, a, m, sem, turn):
    (h_ps, h_sb, o_ps, o_sb, share) = [sem(n) for n in ("ex_h_ready", "ex_h", "ex_out_ready", "ex_added", "ex_share")]
    w_in = [sem(f"ex_weights{u}") for u in range(AT_ONCE)]
    steps = [(u, b) for u in range(AT_ONCE) for b in range(B)]
    with nc.Block() as block:
        @block.sync
        def _(sp):
            for u in range(AT_ONCE):
                sp.dma_start(m.fc[:, u], a["c_fc"][turn * AT_ONCE + u]).then_inc(w_in[u], 16)
                sp.dma_start(m.proj[:, u], a["c_proj"][turn * AT_ONCE + u]).then_inc(w_in[u], 16)
            for u in range(AT_ONCE):
                sp.wait_ge(w_in[u], 32)

        @block.tensor
        def _(pe):
            def up(i):
                u, b = steps[i]
                if b == 0:
                    pe.wait_ge(w_in[u], 32)
                for c in range(CH):
                    n = i * CH + c
                    if n >= 4:
                        pe.wait_ge(h_sb, n - 3)
                    nc.tensor.matmul(m.ps[:, n % 4, :], m.fc[:, u, c * P:(c + 1) * P], m.xnT[:, b, :], start=True, stop=True).then_inc(h_ps, 1)

            def down(i):
                u, b = steps[i]
                pe.wait_ge(h_sb, (i + 1) * CH)
                if i >= 2:
                    pe.wait_ge(o_sb, i - 1)
                for t in range(TB):
                    for c in range(CH):
                        last = nc.tensor.matmul(m.ps[:, 4 + i % 2, t * P:(t + 1) * P], m.hT[:, i % 2, c, t * P:(t + 1) * P],
                                                m.proj[:, u, c, :], start=(c == 0), stop=(c == CH - 1))
                last.then_inc(o_ps, 1)

            for i in range(len(steps) + 1):
                if i < len(steps):
                    up(i)
                if i >= 1:
                    down(i - 1)

        @block.scalar
        def _(act):
            for i in range(len(steps)):
                if i >= 2:
                    act.wait_ge(o_ps, i - 1)
                for c in range(CH):
                    act.wait_ge(h_ps, i * CH + c + 1)
                    nc.scalar.activation(m.hT[:, i % 2, c, :], m.ps[:, (i * CH + c) % 4, :], ACT.Gelu).then_inc(h_sb, 1)

        @block.vector
        def _(dve):
            nc.vector.tensor_copy(m.share2[:], m.share[:, bass.ts(turn, AT_ONCE), :]).then_inc(share, 1)
            dve.wait_ge(share, 1)
            for i, (u, b) in enumerate(steps):
                dve.wait_ge(o_ps, i + 1)
                if u >= 1:
                    dve.wait_ge(o_sb, i - B + 1)
                for t in range(TB):
                    at = b * TB + t
                    last = nc.vector.scalar_tensor_tensor(out=m.state[:, at, :], in0=m.ps[:, 4 + i % 2, t * P:(t + 1) * P],
                                                          scalar=m.share2[:, u, at:at + 1], in1=m.state[:, at, :],
                                                          op0=ALU.mult, op1=ALU.add)
                last.then_inc(o_sb, 1)


def load_first_weights(sp, a, m, layer, loaded):
    sp.dma_start(m.w[:, 0:W_FIRST], a["w"][layer][:, 0:W_FIRST]).then_inc(loaded, 16)
    sp.dma_start(m.cols[:, 0:COLS_FIRST], a["cols"][layer][:, 0:COLS_FIRST]).then_inc(loaded, 16)
    sp.wait_ge(loaded, 32)


def begin_layers(nc, a, m, sem):
    dch, start, loaded = sem("bl_dve"), sem("bl_start"), sem("bl_weights")
    with nc.Block() as block:
        @block.sync
        def _(sp):
            load_first_weights(sp, a, m, 0, loaded)

        @block.vector
        def _(dve):
            chain = Chain(dve, dch)
            chain.link(nc.vector.tensor_tensor(m.x[:], m.x[:], m.state[:], ALU.add))
            row_statistics(dve, chain, m.x[:], T, D, m.st)
            for t in range(T):
                last = normalise(dve, m.state[:], m.x[:], t, m.st)
            chain.link(last)
            row_statistics(dve, chain, m.state[:], T, D, m.st)
            for t in range((B - 1) * TB):
                last = normalise(dve, m.hat[:], m.state[:], t, m.st)
            last.then_inc(start, 1)


def w_of(m, name):
    lo, hi = COLS[name]
    return m.w[:, lo:hi]


def store_query_parts(sp, dst, parts, stored):
    sp.dma_start(dst[:, 0:3, :], parts[:, 0:3, :]).then_inc(stored, 16)
    sp.dma_start(dst[:, 3:5, :], parts[:, 0:2, :]).then_inc(stored, 16)
    sp.dma_start(dst[:, 5:6, :], parts[:, 0:1, :]).then_inc(stored, 16)


def store_key_parts(sp, dst, parts, stored):
    n = parts.shape[2]
    sp.dma_start(dst[:, 0:3, :], parts[:, 0:1, :].to_broadcast([P, 3, n])).then_inc(stored, 16)
    sp.dma_start(dst[:, 3:5, :], parts[:, 1:2, :].to_broadcast([P, 2, n])).then_inc(stored, 16)
    sp.dma_start(dst[:, 5:6, :], parts[:, 2:3, :]).then_inc(stored, 16)


def attend(nc, a, m, sem, layer):
    (w_rest, p_ada_ps, p_ada, p_dch, p_turned, p_xn, p_q_ps, p_read, p_rot, p_hi, p_low, p_mid, p_lo, p_v_ps, p_v_sb) = [
        sem(f"sp_{n}") for n in ("weights_rest", "ada_ready", "ada", "dve", "turned", "xn", "qk_ready", "qk_read",
                                     "rotated", "high", "less_high", "middle", "low", "v_ready", "v")]
    p_out = [sem(f"sp_stored{i}") for i in range(4)]
    p_norm = COLS["n1"][0]
    p_rounds = [(w, w + "r", b) for b in range(B) for w in "qk"]
    (kq0, kq1, s_ready, s_read, maxima, mt_ps, mt_sb, m_rows, st_ready, probs, pv, sums_ready, inverted, widened, u_sb, spread, on,
     o_ps, added, dch, p_hat) = [sem(f"sa_{n}") for n in (
        "stacked0", "stacked1", "max_scores", "max_read", "maxima", "shift_turned", "shift_copied", "shift_rows", "scores", "probs",
        "weighted", "sums", "sums_inverted", "inverse_widened", "unit_copied", "inverse_spread", "unit_done", "projected", "added", "dve", "last_normal")]
    (x_ada_ps, x_ada, x_v_ps, x_v, x_stats, x_hat, x_turned, x_xn, x_ps, x_read, x_rot, x_hi, x_low, x_mid, x_lo, x_stored, x_stacked, pch,
     t_hat, t_rot, t_swap, t_low, t_lo, x_moment) = [sem(f"cp_{n}") for n in (
        "ada_ready", "ada", "values_ready", "values", "statistics", "hat", "turned", "xn", "products", "products_read", "rotated",
        "high", "less_high", "middle", "low", "stored", "stacked", "pool", "last_hat", "last_rotated", "last_swapped", "last_less_high", "last_low",
        "moments")]
    kq, kq_first = (kq0, kq1), sem("sa_stacked_first")
    turn_bank, product_banks = 4, ((0, 1), (2, 6))
    x_rows, (x_q, x_swap, x_left) = m.hat[:, 0:TB, :], [m.hat[:, i * TB:(i + 1) * TB, :].rearrange("p t d -> p (t d)") for i in (1, 2, 3)]
    x_parts = m.xnT[:, 1:B, :].rearrange("p b n -> p (b n)").bitcast(BF16).rearrange("p (c n) -> p c n", n=S)[:, 0:3]
    last_round = B
    t_rows = m.big[:, 4 * S:5 * S].rearrange("p (t d) -> p t d", t=TB)
    t_q, t_swapped, t_left = (m.big[:, lo * S:(lo + 1) * S] for lo in (5, 6, 7))
    t_xn = m.big[:, 4 * S:5 * S]
    t_parts = m.big[:, 10 * S:10 * S + 3 * S // 2].bitcast(BF16).rearrange("p (c n) -> p c n", c=3)

    def x_width(r):
        return S if r else NC_ALL

    def of_context(r, *views):
        return [v[:, 0:x_width(r)] if r else v[:, 0:NC_ALL].rearrange("p (b n) -> p b n", b=B) for v in views]

    def table(r, v):
        return v[:] if r else v[:, 0:N_CTX].unsqueeze(1).to_broadcast([P, B, N_CTX])

    wo = w_of(m, "so")
    scale = float(np.float32(1.0) / np.float32(np.sqrt(HD)))
    st_bank, s_bank, pv_bank, aux = 0, 3, 6, 7
    steps = 4 * TB
    total = UNITS * steps
    ahead = 28
    turn_at, gather_at, spread_at, project_at = 6, 9, 12, 14
    values_at, gain_at = 3, 15
    turn_state_last = 15
    products_at = (3, 15)
    part_at = (8, 12)
    last_unit, last_product_at = UNITS - 1, 4

    (c_kq0, c_kq1, c_s_ready, c_s_read, c_maxima, c_mt_ps, c_mt_sb, c_m_rows, c_st_ready, c_probs, c_pv, c_sums_ready, c_inverted, c_widened, c_u_sb, c_spread, c_on,
     c_o_ps, c_added, c_dch, c_kq2, c_row_ones) = [sem(f"ca_{n}") for n in (
        "stacked0", "stacked1", "max_scores", "max_read", "maxima", "shift_turned", "shift_copied", "shift_rows", "scores", "probs",
        "weighted", "sums", "sums_inverted", "inverse_widened", "unit_copied", "inverse_spread", "unit_done", "projected", "added", "dve",
        "stacked2", "mask_row")]
    c_kq = (c_kq0, c_kq1, c_kq2)
    c_q6 = (m.q6[:, 0], m.q6[:, 1], m.q6_third)
    c_wo = w_of(m, "co")
    c_st_bank, c_s_bank, c_pv_bank, aux0, aux1 = 0, 3, 5, 6, 7
    c_steps = HEADS
    c_total = B * c_steps
    c_turn_at = 7
    turn_state_at, product_at = 12, (14, 16)
    c_max_from = total - 24
    c_turn_first = total - 6
    c_max_next = total + spread_at
    c_early = {total + 10: 0, total + 11: 1, total + 13: 2, total + 15: 3, total + 16: 4}
    c_weigh_at, c_copy_at, c_gather_at, c_spread_at, c_project_at = 6, 7, 9, 13, 28

    def c_max_early(at):
        if c_max_from <= at < c_max_from + c_steps:
            return range(at - c_max_from, at - c_max_from + 1)
        first = c_steps + 3 * (at - c_max_next)
        return range(first, min(first + 3, 2 * c_steps)) if at >= c_max_next else ()

    def c_max_due(at):
        for b, late in ((2, 12), (3, 31)):
            first = b * c_steps + 2 * (at - late)
            if b * c_steps <= first < (b + 1) * c_steps:
                return range(first, first + 2)
        return ()

    def group_at(at, lag):
        quad, rest = (at - lag) // 4, (at - lag) % 4
        return quad if rest == 0 and 0 <= quad < c_total // 4 else None

    with nc.Block() as block:
        @block.sync
        def _(sp):
            sp.dma_start(m.cols[:, COLS_FIRST:], a["cols"][layer][:, COLS_FIRST:]).then_inc(w_rest, 16)
            sp.dma_start(m.w[:, W_FIRST:W_COLS], a["w"][layer][:, W_FIRST:W_COLS]).then_inc(w_rest, 16)
            sp.dma_start(m.f2b[:], a["f2_b"][layer].partition_broadcast(P)).then_inc(w_rest, 16)
            def load(b):
                for i in (2 * b, 2 * b + 1):
                    sp.wait_ge(p_out[i % 4], 48 * (i // 4 + 1))
                if b >= 2:
                    sp.wait_ge(st_ready, (b - 1) * GROUPS * steps)
                if b == 0:
                    load_pairs(b, 0, 2, kq_first)
                load_pairs(b, 0 if b else 2, PAIRS, kq[b % 2])

            def load_pairs(b, i0, i1, loaded):
                src = a["queries"][b].rearrange("(i r) c n -> (r c) i n", i=PAIRS)
                sp.dma_start(m.q6[0:ROW_MASK, b % 2, i0:i1], src[:, i0:i1]).then_inc(loaded, 16)
                src = a["keys"][b].rearrange("(i u r) c n -> u (r c) i n", u=2, r=HD)
                for u in range(2):
                    dst = m.k6[u * ROWS_HEAD:(u + 1) * ROWS_HEAD, b % 2].rearrange("r (i u) n -> r u i n", u=2)[:, u]
                    sp.dma_start(dst[:, i0:i1], src[u][:, i0:i1]).then_inc(loaded, 16)
                sp.dma_start(m.k6[ROW_MASK:ROW_MASK + 1, b % 2, 2 * i0:2 * i1],
                             a["neg_mask"][b:b + 1, :].unsqueeze(1).to_broadcast([1, 2 * (i1 - i0), S])).then_inc(loaded, 16)

            def store(r):
                if r < last_round:
                    sp.wait_ge(x_lo, r + 1)
                else:
                    sp.wait_ge(t_lo, 1)
                if r == 0:
                    store_key_parts(sp, a["ctx_keys"], x_parts[:, :, 0:NC_ALL], x_stored)
                else:
                    store_query_parts(sp, a["queries"][r - 1], x_parts if r < last_round else t_parts, x_stored)

            def c_load(b):
                sp.wait_ge(x_stored, 48 * (b + 2))
                if b < 2:
                    sp.wait_ge(st_ready, (B - 1 + b) * GROUPS * steps)
                elif b == 2:
                    sp.wait_ge(o_ps, B)
                else:
                    sp.wait_ge(c_st_ready, (b - 2) * c_steps)
                sp.dma_start(c_q6[b % 3][0:ROW_MASK], a["queries"][b].rearrange("(i r) c n -> (r c) i n", i=PAIRS)).then_inc(c_kq[b % 3], 16)

            def c_shift(b):
                sp.wait_ge(c_mt_sb, b + 1)
                if b == 2:
                    sp.wait_ge(c_row_ones, 2)
                sp.dma_start(c_q6[b % 3][ROW_SHIFT:ROWS_ALL], m.mct[:, b % 2, :]).then_inc(c_m_rows, 16)

            for i, (name, _, b) in enumerate(p_rounds):
                sp.wait_ge(p_lo, i + 1)
                to_dram = store_query_parts if name == "q" else store_key_parts
                to_dram(sp, a["queries" if name == "q" else "keys"][b], m.parts[:, i % 4], p_out[i % 4])
                if i == 2:
                    load(0)
            sp.wait_ge(w_rest, 48)
            for n in range(UNITS):
                if n == UNITS - 2:
                    c_load(0)
                sp.wait_ge(mt_sb, n + 1)
                b, g = n // GROUPS, n % GROUPS
                sp.dma_start(m.q6[ROW_SHIFT:ROWS_ALL, b % 2, 2 * g:2 * g + 2, :], m.mt[:, n % 2, :]).then_inc(m_rows, 16)
                if g == 0 and b < B - 1:
                    load(b + 1)
                if n % 4 == 2 and n >= 6:
                    store(n // 4 - 1)
                if n == 7:
                    sp.wait_ge(x_stored, 48)
                    src = a["ctx_keys"].rearrange("(i u r) c (b n) -> u b (r c) i n", u=2, r=HD, b=B)
                    for b in range(B):
                        for u in range(2):
                            dst = m.kc6[u * ROWS_HEAD:(u + 1) * ROWS_HEAD, b, :, 0:N_CTX].rearrange("r (i u) n -> r u i n", u=2)[:, u]
                            sp.dma_start(dst, src[u, b]).then_inc(x_stacked, 16)

            c_shift(0)
            c_load(1)
            store(last_round - 1)
            c_load(2)
            c_shift(1)
            store(last_round)
            c_load(3)
            c_shift(2)
            c_shift(3)

        @block.tensor
        def _(pe):
            def max_scores(at):
                n, qt, h = at // steps, at % steps // 4, at % 4
                b, g = n // GROUPS, n % GROUPS
                if at == 0:
                    pe.wait_ge(kq_first, 64)
                elif at == steps or (at % (GROUPS * steps) == 0):
                    pe.wait_ge(kq[b % 2], 64 * (b // 2 + 1))
                if at >= 3:
                    pe.wait_ge(s_read, at - 2)
                nc.tensor.matmul(m.ps[:, s_bank + at % 3, :], m.q6[0:ROWS_MAX, b % 2, 2 * g + h // 2, qt * P:(qt + 1) * P],
                                 m.k6[0:ROWS_MAX, b % 2, 4 * g + h, :], start=True, stop=True).then_inc(s_ready, 1)

            reader = [None]

            def take_aux(next_reader, count):
                if reader[0] is not None:
                    pe.wait_ge(*reader[0])
                reader[0] = (next_reader, count)

            def turn_maxima(n):
                pe.wait_ge(maxima, n + 1)
                take_aux(mt_sb, n + 1)
                for t in range(TB):
                    last = nc.tensor.transpose(m.ps[0:12, aux, :].bitcast(BF16)[:, t * P:(t + 1) * P],
                                               m.mparts[:, n % 2, t].rearrange("p u c i -> p (u c i)"), m.ident_bf[:])
                last.then_inc(mt_ps, 1)

            def shifted_scores(at):
                n, kt, j = at // steps, at % steps // 4, at % 4
                b, g = n // GROUPS, n % GROUPS
                if at % steps == 0:
                    pe.wait_ge(m_rows, 16 * (n + 1))
                if at >= 3:
                    pe.wait_ge(probs, at - 2)
                nc.tensor.matmul(m.ps[:, st_bank + at % 3, :], m.k6[:, b % 2, 4 * g + j, kt * P:(kt + 1) * P],
                                 m.q6[:, b % 2, 2 * g + j // 2, :], start=True, stop=True).then_inc(st_ready, 1)

            def weigh_values(quad):
                n, kt = quad // TB, quad % TB
                b, g = n // GROUPS, n % GROUPS
                pe.wait_ge(probs, 4 * (quad + 1))
                if kt == 0 and n >= 1:
                    pe.wait_ge(u_sb, n)
                for j in range(4):
                    last = nc.tensor.matmul(m.ps[32 * j:32 * j + 32, pv_bank, :], m.vaug[:, b, kt, 4 * g + j, :], m.probs[:, quad % 2, j, :],
                                            start=(kt == 0), stop=(kt == TB - 1))
                last.then_inc(pv, 1)

            def gather_sums(n):
                pe.wait_ge(u_sb, n + 1)
                take_aux(inverted, n + 1)
                for t in range(TB):
                    last = nc.tensor.transpose(m.ps[:, aux, t * P:(t + 1) * P], m.unit[:, n % 2, t * P:(t + 1) * P], m.ident[:])
                last.then_inc(sums_ready, 1)

            def spread_inverse(n):
                pe.wait_ge(widened, n + 1)
                take_aux(on, n + 1)
                for t in range(TB):
                    last = nc.tensor.transpose(m.ps[:, aux, t * P:(t + 1) * P], m.inverse[:, n % 2, t, :, :].rearrange("p h r -> p (h r)"),
                                               m.ident[:])
                last.then_inc(spread, 1)

            def project_out(b, t):
                if t == 0:
                    pe.wait_ge(on, GROUPS * (b + 1))
                    take_aux(added, b + 1)
                for g in range(GROUPS):
                    last = nc.tensor.matmul(m.ps[:, aux, t * P:(t + 1) * P], m.on[:, g, t * P:(t + 1) * P], wo[:, g * D:(g + 1) * D],
                                            start=(g == 0), stop=(g == GROUPS - 1))
                if t == TB - 1:
                    last.then_inc(o_ps, 1)

            def context_values():
                take_aux(x_v, 1)
                for b in range(B):
                    last = nc.tensor.matmul(m.ps[0:N_CTX, aux, b * D:(b + 1) * D], m.ctxT[:, b * N_CTX:(b + 1) * N_CTX], w_of(m, "cv"),
                                            start=True, stop=True)
                last.then_inc(x_v_ps, 1)

            def normal_gain():
                take_aux(x_ada, 1)
                for half in range(2):
                    lo = COLS["n2"][0] + half * D
                    last = nc.tensor.matmul(m.ps[:, aux, half * B:(half + 1) * B], m.w[:, lo:lo + D], m.condT[:], start=True, stop=True)
                last.then_inc(x_ada_ps, 1)

            def turn_state(r):
                if r < last_round:
                    pe.wait_ge(x_hat, r)
                else:
                    pe.wait_ge(t_hat, 1)
                take_aux(x_xn, r)
                rows = x_rows if r < last_round else t_rows
                for t in range(TB):
                    last = nc.tensor.transpose(m.ps[:, aux, t * P:(t + 1) * P], rows[:, t, :], m.ident[:])
                last.then_inc(x_turned, 1)

            def product(r, half, bank=aux):
                if r:
                    pe.wait_ge(x_xn, r)
                name = (("ck", "ckr"), ("cq", "cqr"))[min(r, 1)][half]
                n = x_width(r)
                rhs = m.ctxT[:] if r == 0 else m.xnT[:, 0, :] if r < last_round else t_xn
                nc.tensor.matmul(m.ps[:, bank, 0:n], w_of(m, name), rhs, start=True, stop=True).then_inc(x_ps, 1)

            c_reader = [None]

            def c_take_aux(next_reader, count):
                if c_reader[0] is not None:
                    pe.wait_ge(*c_reader[0])
                c_reader[0] = (next_reader, count)

            def c_max_scores(at):
                b, qt, g = at // c_steps, at % c_steps // GROUPS, at % GROUPS
                if at % c_steps == 0:
                    pe.wait_ge(c_kq[b % 3], 16 * (b // 3 + 1))
                if at == 2 * c_steps:
                    pe.wait_ge(c_row_ones, 2)
                if at >= 2:
                    pe.wait_ge(c_s_read, at - 1)
                for h in range(4):
                    last = nc.tensor.matmul(m.ps[:, c_s_bank + at % 2, h * N_CTX:(h + 1) * N_CTX],
                                            c_q6[b % 3][0:ROWS_MAX, 2 * g + h // 2, qt * P:(qt + 1) * P],
                                            m.kc6[0:ROWS_MAX, b, 4 * g + h, 0:N_CTX], start=True, stop=True)
                last.then_inc(c_s_ready, 1)

            def c_turn_maxima(b):
                pe.wait_ge(c_maxima, b + 1)
                take_aux(c_mt_sb, b + 1)
                for t in range(TB):
                    last = nc.tensor.transpose(m.ps[0:3 * HEADS, aux1, :].bitcast(BF16)[:, t * P:(t + 1) * P],
                                               m.mcparts[:, t].rearrange("p u c i -> p (u c i)"), m.ident_bf[:])
                last.then_inc(c_mt_ps, 1)

            def c_shifted_scores(at):
                b, h = at // c_steps, at % c_steps
                if h == 0:
                    pe.wait_ge(c_m_rows, 16 * (b + 1))
                if at >= 3:
                    pe.wait_ge(c_probs, at - 2)
                nc.tensor.matmul(m.ps[:, c_st_bank + at % 3, :], m.kc6[:, b, h, :], c_q6[b % 3][:, h // 2, :],
                                 start=True, stop=True).then_inc(c_st_ready, 1)

            def c_weigh_values(quad):
                b, g = quad // GROUPS, quad % GROUPS
                pe.wait_ge(c_probs, 4 * (quad + 1))
                if quad >= 1:
                    pe.wait_ge(c_u_sb, quad)
                for j in range(4):
                    last = nc.tensor.matmul(m.ps[32 * j:32 * j + 32, c_pv_bank, :], m.vcaug[:, b, 4 * g + j, :],
                                            m.cprobs[quad % 2][:, j, :], start=True, stop=True)
                last.then_inc(c_pv, 1)

            def c_gather_sums(quad):
                pe.wait_ge(c_u_sb, quad + 1)
                c_take_aux(c_inverted, quad + 1)
                for t in range(TB):
                    last = nc.tensor.transpose(m.ps[:, aux0, t * P:(t + 1) * P],
                                               m.units[:, quad // GROUPS % 2, quad % GROUPS, t * P:(t + 1) * P], m.ident[:])
                last.then_inc(c_sums_ready, 1)

            def c_spread_inverse(quad):
                pe.wait_ge(c_widened, quad + 1)
                take_aux(c_on, quad + 1)
                for t in range(TB):
                    last = nc.tensor.transpose(m.ps[:, aux1, t * P:(t + 1) * P],
                                               m.inverses[:, quad % 2, 4 * t:4 * t + 4, :].rearrange("p h r -> p (h r)"), m.ident[:])
                last.then_inc(c_spread, 1)

            def c_project_out(b):
                pe.wait_ge(c_on, GROUPS * (b + 1))
                c_take_aux(c_added, b + 1)
                for t in range(TB):
                    for g in range(GROUPS):
                        last = nc.tensor.matmul(m.ps[:, aux0, t * P:(t + 1) * P], m.units[:, b % 2, g, t * P:(t + 1) * P],
                                                c_wo[:, g * D:(g + 1) * D], start=(g == 0), stop=(g == GROUPS - 1))
                last.then_inc(c_o_ps, 1)

            for half in range(2):
                last = nc.tensor.matmul(m.ps[:, aux, half * B:(half + 1) * B], m.w[:, p_norm + half * D:p_norm + (half + 1) * D], m.condT[:],
                                        start=True, stop=True)
            last.then_inc(p_ada_ps, 1)
            def turn_normal(b):
                if b >= 2:
                    pe.wait_ge(p_xn, b - 1)
                if b == B - 1:
                    pe.wait_ge(p_hat, 1)
                for t in range(TB):
                    last = nc.tensor.transpose(m.ps[:, turn_bank + b % 2, t * P:(t + 1) * P], m.hat[:, b * TB + t, :], m.ident[:])
                last.then_inc(p_turned, 1)

            for b in range(B - 1):
                turn_normal(b)
            for i, (name, swapped, b) in enumerate(p_rounds):
                if i == 2:
                    turn_normal(B - 1)
                banks = product_banks[i % 2]
                if i >= 2:
                    pe.wait_ge(p_read, i - 1)
                pe.wait_ge(p_xn, b + 1)
                nc.tensor.matmul(m.ps[:, banks[0], :], w_of(m, name), m.xnT[:, b, :], start=True, stop=True)
                nc.tensor.matmul(m.ps[:, banks[1], :], w_of(m, swapped), m.xnT[:, b, :], start=True, stop=True).then_inc(p_q_ps, 1)
                if name == "k":
                    if b >= 1:
                        pe.wait_ge(p_v_sb, b)
                    for t in range(TB):
                        last = nc.tensor.matmul(m.ps[:, aux, t * P:(t + 1) * P], m.xnT[:, b, t * P:(t + 1) * P], w_of(m, "v"),
                                                start=True, stop=True)
                    last.then_inc(p_v_ps, 1)
            pe.wait_ge(p_xn, B)
            for at in range(ahead):
                max_scores(at)
                if at == steps + 2:
                    pe.wait_ge(p_v_sb, B)
                    turn_maxima(0)
            pe.wait_ge(p_read, len(p_rounds))
            pe.wait_ge(w_rest, 48)
            for at in range(total + steps + 2):
                n, s = at // steps, at % steps
                if at == c_max_from:
                    pe.wait_ge(s_read, total)
                    pe.wait_ge(x_stacked, 16 * 2 * B)
                if at < total:
                    for due in c_max_early(at):
                        c_max_scores(due)
                    shifted_scores(at)
                if at + ahead < total:
                    max_scores(at + ahead)
                if s % 4 == 3 and 0 <= at // 4 - 1 < total // 4:
                    weigh_values(at // 4 - 1)
                if s == turn_at and n + 1 < UNITS:
                    turn_maxima(n + 1)
                if s == gather_at and n >= 1:
                    gather_sums(n - 1)
                if s == spread_at and n >= 1:
                    spread_inverse(n - 1)
                if project_at <= at % (GROUPS * steps) < project_at + TB and at > GROUPS * steps:
                    project_out(n // GROUPS - 1, at % (GROUPS * steps) - project_at)
                if s == values_at and n == 1:
                    context_values()
                if s == gain_at and n == 1:
                    normal_gain()
                if s == turn_state_last and n % 4 == 2 and 2 < n < UNITS:
                    turn_state(n // 4)
                if n == last_unit and s == last_product_at:
                    product(n // 4, 1, c_pv_bank)
                elif s in products_at and n % 4 == 3 and n < UNITS and (n, s) != (last_unit, products_at[1]):
                    half = products_at.index(s)
                    take_aux(x_read, 2 * (n // 4) + half + 1)
                    product(n // 4, half)
                if at == c_turn_first:
                    c_turn_maxima(0)
                if at >= total:
                    for due in c_max_early(at):
                        c_max_scores(due)
                if at in c_early:
                    pe.wait_ge(probs, total)
                    c_shifted_scores(c_early[at])
            for at in range(len(c_early), c_total + c_steps):
                b, s = at // c_steps, at % c_steps
                if at < c_total:
                    c_shifted_scores(at)
                for due in c_max_due(at):
                    c_max_scores(due)
                if group_at(at, c_weigh_at) is not None:
                    c_weigh_values(group_at(at, c_weigh_at))
                if s == c_turn_at and b + 1 < B:
                    c_turn_maxima(b + 1)
                if group_at(at, c_gather_at) is not None:
                    c_gather_sums(group_at(at, c_gather_at))
                if group_at(at, c_spread_at) is not None:
                    c_spread_inverse(group_at(at, c_spread_at))
                if at == turn_state_at:
                    turn_state(last_round)
                if at in product_at:
                    half = product_at.index(at)
                    take_aux(t_swap, half + 1)
                    product(last_round, half)
                if at >= c_project_at and (at - c_project_at) % c_steps == 0:
                    c_project_out((at - c_project_at) // c_steps)

        @block.scalar
        def _(act):
            def copy_maxima(n):
                act.wait_ge(mt_ps, n + 1)
                if n >= 2:
                    act.wait_ge(m_rows, 16 * (n - 1))
                nc.scalar.copy(m.mt[0:12, n % 2, :], m.ps[0:12, aux, :].bitcast(BF16)[:, 0:S]).then_inc(mt_sb, 1)

            def copy_unit(n):
                act.wait_ge(pv, TB * (n + 1))
                if n >= 2:
                    act.wait_ge(on, n - 1)
                nc.scalar.copy(m.unit[:, n % 2, :], m.ps[:, pv_bank, :]).then_inc(u_sb, 1)

            def scale_shift(r):
                act.wait_ge(x_turned, r)
                act.wait_ge(x_ps, 2 * r)
                if r == 1:
                    act.wait_ge(x_ada, 1)
                b = r - 1
                nc.scalar.activation(m.xnT[:, 0, :] if r < last_round else t_xn, m.ps[:, aux, :], ACT.Identity, bias=m.ada[:, B + b:B + b + 1],
                                     scale=m.ada[:, b:b + 1]).then_inc(x_xn, 1)

            def copy_product(r, half, bank=aux):
                act.wait_ge(x_ps, 2 * r + half + 1)
                if r >= 1:
                    act.wait_ge(x_lo, r)
                n = x_width(r)
                nc.scalar.copy((x_q, x_swap)[half][:, 0:n], m.ps[:, bank, 0:n]).then_inc(x_read, 1)

            def first_part(r, rotated, count):
                act.wait_ge(rotated, count)
                if r >= 1:
                    act.wait_ge(x_stored, 48 * r)
                n = x_width(r)
                parts, whole = (x_parts, x_q) if r < last_round else (t_parts, t_q)
                nc.scalar.copy(parts[:, 0, 0:n], whole[:, 0:n]).then_inc(x_hi, 1)

            def second_part(r, less_high, count):
                act.wait_ge(less_high, count)
                n = x_width(r)
                parts, left = (x_parts, x_left) if r < last_round else (t_parts, t_left)
                nc.scalar.copy(parts[:, 1, 0:n], left[:, 0:n]).then_inc(x_mid, 1)

            def c_copy_maxima(b):
                act.wait_ge(c_mt_ps, b + 1)
                if b >= 2:
                    act.wait_ge(c_m_rows, 16 * (b - 1))
                nc.scalar.copy(m.mct[:, b % 2, :], m.ps[0:3 * HEADS, aux1, :].bitcast(BF16)[:, 0:S]).then_inc(c_mt_sb, 1)

            def c_copy_unit(quad):
                b, g = quad // GROUPS, quad % GROUPS
                act.wait_ge(c_pv, quad + 1)
                if g == 0 and b >= 2:
                    act.wait_ge(c_o_ps, b - 1)
                nc.scalar.copy(m.units[:, b % 2, g, :], m.ps[:, c_pv_bank, :]).then_inc(c_u_sb, 1)

            def p_first_part(i):
                act.wait_ge(p_rot, i + 1)
                if i >= 4:
                    act.wait_ge(p_out[i % 4], 48 * (i // 4))
                nc.scalar.copy(m.parts[:, i % 4, 0], m.rot[:, i % 2]).then_inc(p_hi, 1)

            def p_second_part(i):
                act.wait_ge(p_low, i + 1)
                nc.scalar.copy(m.parts[:, i % 4, 1], m.left[:, i % 2]).then_inc(p_mid, 1)

            act.wait_ge(p_ada, 1)
            for b in range(B):
                act.wait_ge(p_turned, b + 1)
                nc.scalar.activation(m.xnT[:, b, :], m.ps[:, turn_bank + b % 2, :], ACT.Identity, bias=m.ada[:, B + b:B + b + 1],
                                     scale=m.ada[:, b:b + 1]).then_inc(p_xn, 1)
            for i in range(len(p_rounds) + 1):
                if i < len(p_rounds):
                    p_first_part(i)
                if i < len(p_rounds) and p_rounds[i][0] == "k":
                    b = p_rounds[i][2]
                    act.wait_ge(p_v_ps, b + 1)
                    nc.scalar.copy(m.vaug[:, b, :, :, 0:HD], m.ps[:, aux, :].rearrange("p (t h d) -> p t h d", t=TB, d=HD)).then_inc(p_v_sb, 1)
                if i >= 1:
                    p_second_part(i - 1)

            copy_maxima(0)
            act.wait_ge(p_lo, len(p_rounds))
            for at in range(total):
                n, s = at // steps, at % steps
                act.wait_ge(st_ready, at + 1)
                if s % 4 == 0 and at >= 8:
                    act.wait_ge(pv, at // 4 - 1)
                nc.scalar.activation(m.probs[:, at // 4 % 2, at % 4, :], m.ps[:, st_bank + at % 3, :], ACT.Exp, scale=scale).then_inc(probs, 1)
                if s == 0 and n % 4 == 3 and n > 3:
                    scale_shift(n // 4)
                if s == products_at[0] + 1 and n % 4 == 3:
                    copy_product(n // 4, 0)
                if n == last_unit and s == last_product_at + 1:
                    copy_product(n // 4, 1, c_pv_bank)
                if s == 0 and n % 4 == 0 and n > 0:
                    copy_product(n // 4 - 1, 1)
                if s == 4 and n >= 1:
                    copy_unit(n - 1)
                if s == turn_at + 1 and n + 1 < UNITS:
                    copy_maxima(n + 1)
                if s == values_at + 2 and n == 1:
                    act.wait_ge(x_v_ps, 1)
                    nc.scalar.copy(m.vcaug[0:N_CTX, :, :, 0:HD],
                                   m.ps[0:N_CTX, aux, :].rearrange("n (b h d) -> n b h d", b=B, d=HD)).then_inc(x_v, 1)
                if s == part_at[0] and n % 4 == 0 and n > 0:
                    first_part(n // 4 - 1, x_rot, n // 4)
                if s == part_at[1] and n % 4 == 0 and n > 0:
                    second_part(n // 4 - 1, x_low, n // 4)
                if at == c_turn_first + 1:
                    act.wait_ge(m_rows, 16 * UNITS)
                    c_copy_maxima(0)
            first_part(last_round - 1, x_rot, last_round)
            copy_unit(UNITS - 1)
            second_part(last_round - 1, x_low, last_round)
            act.wait_ge(x_stored, 48 * last_round)
            for at in range(c_total):
                b, s = at // c_steps, at % c_steps
                act.wait_ge(c_st_ready, at + 1)
                if at % 4 == 0 and at >= 8:
                    act.wait_ge(c_pv, at // 4 - 1)
                nc.scalar.activation(m.cprobs[at // 4 % 2][:, at % 4, :], m.ps[:, c_st_bank + at % 3, :], ACT.Exp,
                                     scale=scale).then_inc(c_probs, 1)
                if at == turn_state_at:
                    scale_shift(last_round)
                if at == product_at[1] + 2:
                    first_part(last_round, t_rot, 1)
                if at == product_at[1] + 5:
                    second_part(last_round, t_low, 1)
                if at == 16 + c_copy_at:
                    act.wait_ge(t_lo, 1)
                if group_at(at, c_copy_at) is not None:
                    c_copy_unit(group_at(at, c_copy_at))
                if s == c_turn_at + 1 and b + 1 < B:
                    c_copy_maxima(b + 1)
            for quad in range((c_total - 1 - c_copy_at) // 4 + 1, c_total // 4):
                c_copy_unit(quad)

        @block.gpsimd
        def _(pool):
            chain = Chain(pool, pch)

            def normalise_batch(r):
                pool.wait_ge(x_stats, r)
                if r >= 2:
                    pool.wait_ge(x_turned, r - 1)
                b, var, a, root = r - 1, m.st.var[:, 0:TB], m.st.tmp[:, 0:TB], m.st.rstd[:, 0:TB]
                for _ in range(ROOT_STEPS):
                    chain.link(nc.gpsimd.tensor_tensor(a, root, root, ALU.mult))
                    chain.link(nc.gpsimd.tensor_tensor(a, a, var, ALU.mult))
                    chain.link(nc.gpsimd.tensor_scalar(a, a, -0.5, 1.5, ALU.mult, ALU.add))
                    chain.link(nc.gpsimd.tensor_tensor(root, root, a, ALU.mult))
                for t in range(TB):
                    last = normalise(nc.gpsimd, x_rows, m.state[:, b * TB:(b + 1) * TB, :], t, m.st)
                last.then_inc(x_hat, 1)

            def rotate(r):
                pool.wait_ge(x_read, 2 * r + 2)
                x, y = of_context(r, x_q, x_swap)
                nc.gpsimd.tensor_tensor(x, x, table(r, m.cos), ALU.mult)
                chain.link(nc.gpsimd.tensor_tensor(y, y, table(r, m.sin), ALU.mult))
                nc.gpsimd.tensor_tensor(x, x, y, ALU.add).then_inc(x_rot, 1)

            def split(r):
                n = x_width(r)
                pool.wait_ge(x_hi, r + 1)
                nc.gpsimd.tensor_tensor(x_left[:, 0:n], x_q[:, 0:n], x_parts[:, 0, 0:n], ALU.subtract).then_inc(x_low, 1)
                pool.wait_ge(x_mid, r + 1)
                nc.gpsimd.tensor_tensor(x_parts[:, 2, 0:n], x_left[:, 0:n], x_parts[:, 1, 0:n], ALU.subtract).then_inc(x_lo, 1)

            def widen(n):
                pool.wait_ge(inverted, n + 1)
                if n >= 2:
                    pool.wait_ge(spread, n - 1)
                nc.gpsimd.tensor_copy(m.inverse[:, n % 2].rearrange("p t h r -> p (t h) r"),
                                      m.invsum[:, 0].rearrange("p t h -> p (t h)").unsqueeze(2).to_broadcast([P, 4 * TB, 32])).then_inc(widened, 1)

            def p_less_first(i):
                pool.wait_ge(p_hi, i + 1)
                if i >= 2:
                    pool.wait_ge(p_lo, i - 1)
                nc.gpsimd.tensor_tensor(m.left[:, i % 2], m.rot[:, i % 2], m.parts[:, i % 4, 0],
                                        ALU.subtract).then_inc(p_low, 1)

            def p_third_part(i):
                pool.wait_ge(p_mid, i + 1)
                nc.gpsimd.tensor_tensor(m.parts[:, i % 4, 2], m.left[:, i % 2], m.parts[:, i % 4, 1],
                                        ALU.subtract).then_inc(p_lo, 1)

            for i in range(len(p_rounds) + 1):
                if i < len(p_rounds):
                    p_less_first(i)
                if i >= 1:
                    p_third_part(i - 1)

            for i in range(4):
                pool.wait_ge(p_out[i], 48 * len(range(i, len(p_rounds), 4)))
            for n in range(1, UNITS):
                if n % 4 == 0:
                    rotate(n // 4 - 1)
                widen(n - 1)
                if n % 4 == 0:
                    split(n // 4 - 1)
                if n == last_unit:
                    rotate(last_round - 1)
                    split(last_round - 1)
                if n % 4 == 1 and n > 1:
                    normalise_batch(n // 4)
            pool.wait_ge(o_ps, B)
            pool.wait_ge(x_lo, last_round)
            third = m.q6_third.rearrange("p i n -> p (i n)").bitcast(F32)
            pool.memset(third[ROW_MASK:P], 0.0).then_inc(c_row_ones, 1)
            pool.wait_ge(c_row_ones, 1)
            pool.memset(third[ROW_MASK:ROW_MASK + 1], TWO_ONES).then_inc(c_row_ones, 1)
            pool.wait_ge(c_row_ones, 2)
            for quad in range(c_total // 4):
                pool.wait_ge(c_inverted, quad + 1)
                if quad >= 2:
                    pool.wait_ge(c_spread, quad - 1)
                g = quad % GROUPS
                nc.gpsimd.tensor_copy(m.inverses[:, quad % 2], m.invsum[:, g].rearrange("p t h -> p (t h)").unsqueeze(2)
                                      .to_broadcast([P, 4 * TB, 32])).then_inc(c_widened, 1)

        @block.vector
        def _(dve):
            chain = Chain(dve, dch)

            def row_maxima(at):
                dve.wait_ge(s_ready, at + 1)
                qt, h = at % steps // 4, at % 4
                nc.vector.reduce_max(m.maxima[:, qt, h:h + 1], m.ps[:, s_bank + at % 3, :], AX.X).then_inc(s_read, 1)

            def split_maxima(n):
                dve.wait_ge(s_read, (n + 1) * steps)
                if n >= 2:
                    dve.wait_ge(mt_ps, n - 1)
                parts, left = m.mparts[:, n % 2], m.maxima[:, :, 0:4].rearrange("p t (i u) -> p t u i", u=2)
                chain.link(nc.vector.tensor_copy(parts[:, :, :, 0], left))
                chain.link(nc.vector.tensor_tensor(left, left, parts[:, :, :, 0], ALU.subtract))
                chain.link(nc.vector.tensor_copy(parts[:, :, :, 1], left))
                nc.vector.tensor_tensor(parts[:, :, :, 2], left, parts[:, :, :, 1], ALU.subtract).then_inc(maxima, 1)
                dve.wait_ge(maxima, n + 1)

            def invert_sums(n):
                dve.wait_ge(sums_ready, n + 1)
                if n >= 1:
                    dve.wait_ge(widened, n)
                nc.vector.reciprocal(m.invsum[:, 0], m.ps[:, aux, :].rearrange("p (t h r) -> p t h r", t=TB, h=4)[:, :, :, HD]).then_inc(inverted, 1)
                if n == UNITS - 1:
                    dve.wait_ge(inverted, UNITS)
                    dve.wait_ge(spread, UNITS - 2)
                    nc.vector.tensor_copy(m.inverse[:, n % 2].rearrange("p t h r -> p (t h) r"),
                                          m.invsum[:, 0].rearrange("p t h -> p (t h)").unsqueeze(2).to_broadcast([P, 4 * TB, 32])).then_inc(widened, 1)

            def divide_unit(n):
                dve.wait_ge(spread, n + 1)
                if n % GROUPS == 0 and n >= GROUPS:
                    dve.wait_ge(o_ps, n // GROUPS)
                nc.vector.tensor_tensor(m.on[:, n % GROUPS, :], m.unit[:, n % 2, :], m.ps[:, aux, :], ALU.mult).then_inc(on, 1)

            def add_to_state(b):
                dve.wait_ge(o_ps, b + 1)
                nc.vector.tensor_tensor(m.state[:, b * TB:(b + 1) * TB, :], m.state[:, b * TB:(b + 1) * TB, :],
                                        m.ps[:, aux, :].rearrange("p (t d) -> p t d", t=TB), ALU.add).then_inc(added, 1)

            def batch_statistics(r, s):
                b, var, half = r - 1, m.st.var[:, 0:TB], m.st.tmp[:, 0:TB]
                if s == 2:
                    dve.wait_ge(added, r)
                    if r >= 2:
                        dve.wait_ge(x_hat, r - 1)
                s -= 2
                if 0 <= s < TB:
                    nc.vector.bn_stats(m.st.bn[:, s, :], m.state[:, b * TB + s, :]).then_inc(x_moment, 1)
                elif TB <= s < 2 * TB:
                    dve.wait_ge(x_moment, MOMENTS * (r - 1) + TB)
                    nc.vector.bn_aggr(m.st.mv[:, s - TB, :], m.st.bn[:, s - TB, :]).then_inc(x_moment, 1)
                elif s == 2 * TB:
                    dve.wait_ge(x_moment, MOMENTS * (r - 1) + 2 * TB)
                    nc.vector.tensor_scalar(var, m.st.mv[:, 0:TB, 1], LN_EPS, None, ALU.add).then_inc(x_moment, 1)
                elif s == 2 * TB + 1:
                    dve.wait_ge(x_moment, MOMENTS * (r - 1) + 2 * TB + 1)
                    nc.vector.tensor_scalar(half.bitcast(I32), var.bitcast(I32), 1, None, ALU.arith_shift_right).then_inc(x_moment, 1)
                elif s == 2 * TB + 2:
                    dve.wait_ge(x_moment, MOMENTS * r)
                    nc.vector.tensor_scalar(m.st.rstd[:, 0:TB].bitcast(I32), half.bitcast(I32), -1.0, float(RSQRT_SEED),
                                            ALU.mult, ALU.add).then_inc(x_stats, 1)

            def reduce_scores(at):
                row_maxima(at)
                if at % steps == steps - 1:
                    split_maxima(at // steps)

            c_chain = Chain(dve, c_dch)

            def c_row_maxima(at):
                dve.wait_ge(c_s_ready, at + 1)
                qt, g = at % c_steps // GROUPS, at % GROUPS
                nc.vector.tensor_reduce(m.maxima[:, qt, 4 * g:4 * g + 4],
                                        m.ps[:, c_s_bank + at % 2, 0:4 * N_CTX].rearrange("p (h n) -> p h n", h=4),
                                        AX.X, ALU.max).then_inc(c_s_read, 1)

            def c_split_maxima(b):
                dve.wait_ge(c_s_read, (b + 1) * c_steps)
                if b >= 1:
                    dve.wait_ge(c_mt_ps, b)
                parts, left = m.mcparts, m.maxima[:].rearrange("p t (i u) -> p t u i", u=2)
                c_chain.link(nc.vector.tensor_copy(parts[:, :, :, 0], left))
                c_chain.link(nc.vector.tensor_tensor(left, left, parts[:, :, :, 0], ALU.subtract))
                c_chain.link(nc.vector.tensor_copy(parts[:, :, :, 1], left))
                nc.vector.tensor_tensor(parts[:, :, :, 2], left, parts[:, :, :, 1], ALU.subtract).then_inc(c_maxima, 1)
                dve.wait_ge(c_maxima, b + 1)

            def c_invert_sums(quad):
                dve.wait_ge(c_sums_ready, quad + 1)
                if quad >= GROUPS:
                    dve.wait_ge(c_widened, quad - GROUPS + 1)
                nc.vector.reciprocal(m.invsum[:, quad % GROUPS],
                                     m.ps[:, aux0, :].rearrange("p (t h r) -> p t h r", t=TB, h=4)[:, :, :, HD]).then_inc(c_inverted, 1)

            def divide_group(quad):
                dve.wait_ge(c_spread, quad + 1)
                rows = m.units[:, quad // GROUPS % 2, quad % GROUPS, :]
                nc.vector.tensor_tensor(rows, rows, m.ps[:, aux1, :], ALU.mult).then_inc(c_on, 1)

            def c_add_to_state(b):
                dve.wait_ge(c_o_ps, b + 1)
                nc.vector.tensor_tensor(m.state[:, b * TB:(b + 1) * TB, :], m.state[:, b * TB:(b + 1) * TB, :],
                                        m.ps[:, aux0, :].rearrange("p (t d) -> p t d", t=TB), ALU.add).then_inc(c_added, 1)

            def c_reduce_scores(at):
                c_row_maxima(at)
                if at % c_steps == c_steps - 1:
                    c_split_maxima(at // c_steps)

            p_chain = Chain(dve, p_dch)
            dve.wait_ge(p_ada_ps, 1)
            nc.vector.tensor_scalar(m.ada[:, 0:B], m.ps[:, aux, 0:B], m.cols[:, 0:1], 1.0, ALU.add, ALU.add)
            nc.vector.tensor_scalar(m.ada[:, B:2 * B], m.ps[:, aux, B:2 * B], m.cols[:, 1:2], None, ALU.add).then_inc(p_ada, 1)
            normalise_batch(dve, p_chain, m.hat[:], m.state[:], B - 1, m.st).then_inc(p_hat, 1)
            for i in range(len(p_rounds)):
                banks = product_banks[i % 2]
                dve.wait_ge(p_q_ps, i + 1)
                if i >= 2:
                    dve.wait_ge(p_low, i - 1)
                nc.vector.tensor_tensor(m.rot[:, i % 2], m.ps[:, banks[0], :], m.cos[:], ALU.mult)
                nc.vector.tensor_tensor(m.swap[:, i % 2], m.ps[:, banks[1], :], m.sin[:], ALU.mult).then_inc(p_read, 1)
                dve.wait_ge(p_read, i + 1)
                nc.vector.tensor_tensor(m.rot[:, i % 2], m.rot[:, i % 2], m.swap[:, i % 2], ALU.add).then_inc(p_rot, 1)
            for at in range(ahead):
                reduce_scores(at)
            for at in range(total + steps + 2):
                n, s = at // steps, at % steps
                if at < total:
                    for due in c_max_early(at):
                        c_reduce_scores(due)
                if at + ahead < total:
                    reduce_scores(at + ahead)
                if s == gather_at and n >= 1:
                    invert_sums(n - 1)
                if s == spread_at and n >= 1:
                    divide_unit(n - 1)
                if at % (GROUPS * steps) == project_at + TB - 1 and at > GROUPS * steps:
                    add_to_state(n // GROUPS - 1)
                if at >= total:
                    for due in c_max_early(at):
                        c_reduce_scores(due)
                if s == gain_at and n == 1:
                    dve.wait_ge(x_ada_ps, 1)
                    nc.vector.tensor_scalar(m.ada[:, 0:B], m.ps[:, aux, 0:B], m.cols[:, 2:3], 1.0, ALU.add, ALU.add)
                    nc.vector.tensor_scalar(m.ada[:, B:2 * B], m.ps[:, aux, B:2 * B], m.cols[:, 3:4], None, ALU.add).then_inc(x_ada, 1)
                if n % 4 == 1 and 1 < n < UNITS:
                    batch_statistics(n // 4, s)
            dve.wait_ge(added, B)
            dve.wait_ge(x_hat, last_round - 1)
            row_statistics(dve, chain, m.state[:, (B - 1) * TB:B * TB, :], TB, D, m.st)
            for t in range(TB):
                last = normalise(dve, t_rows, m.state[:, (B - 1) * TB:B * TB, :], t, m.st)
            last.then_inc(t_hat, 1)
            for at in range(c_total + c_steps):
                b, s = at // c_steps, at % c_steps
                for due in c_max_due(at):
                    c_reduce_scores(due)
                if group_at(at, c_gather_at) is not None:
                    c_invert_sums(group_at(at, c_gather_at))
                if group_at(at, c_spread_at) is not None:
                    divide_group(group_at(at, c_spread_at))
                if at in product_at:
                    half = product_at.index(at)
                    dve.wait_ge(x_ps, 2 * last_round + half + 1)
                    nc.vector.tensor_tensor((t_q, t_swapped)[half], m.ps[:, aux, :], (m.cos, m.sin)[half][:], ALU.mult).then_inc(t_swap, 1)
                if at == product_at[1] + 1:
                    dve.wait_ge(t_swap, 2)
                    nc.vector.tensor_tensor(t_q, t_q, t_swapped, ALU.add).then_inc(t_rot, 1)
                if at == product_at[1] + 4:
                    dve.wait_ge(x_hi, last_round + 1)
                    nc.vector.tensor_tensor(t_left, t_q, t_parts[:, 0], ALU.subtract).then_inc(t_low, 1)
                if at == product_at[1] + 7:
                    dve.wait_ge(x_mid, last_round + 1)
                    nc.vector.tensor_tensor(t_parts[:, 2], t_left, t_parts[:, 1], ALU.subtract).then_inc(t_lo, 1)
                if at >= c_project_at and (at - c_project_at) % c_steps == 0:
                    b = (at - c_project_at) // c_steps
                    if b == B - 1:
                        tiles = (B - 1) * TB
                        root_seed(dve, chain, P, tiles, m.st)
                        for _ in range(ROOT_STEPS):
                            chain.link(root_step(dve, chain, P, tiles, m.st))
                        dve.wait_ge(c_pv, B * GROUPS)
                        for t in range(tiles):
                            normalise(dve, m.hat[:], m.state[:], t, m.st)
                    c_add_to_state(b)
                    if b < B - 1:
                        dve.wait_ge(c_added, b + 1)
                        row_moments(dve, chain, m.state[:], TB, m.st, b * TB)


def feed_forward(nc, a, m, sem, layer):
    (ada_ps, ada, dch, hat, turned, xn, h_ps, h_sb, o_ps, biased, added, normal) = [sem(f"ff_{n}") for n in (
        "ada_ready", "ada", "dve", "hat", "turned", "xn", "h_ready", "h", "out_ready", "biased", "added", "next_normal")]
    w1, w2 = w_of(m, "f1"), w_of(m, "f2")
    loaded = sem("ff_next_weights")
    with nc.Block() as block:
        @block.sync
        def _(sp):
            load_first_weights(sp, a, m, layer + 1, loaded)

        @block.tensor
        def _(pe):
            lo_c = COLS["n3"][0]
            for half in range(2):
                last = nc.tensor.matmul(m.ps[:, 7, half * B:(half + 1) * B], m.w[:, lo_c + half * D:lo_c + (half + 1) * D], m.condT[:],
                                        start=True, stop=True)
            last.then_inc(ada_ps, 1)

            def turn(b):
                if b == B - 1:
                    pe.wait_ge(hat, 1)
                pe.wait_ge(ada, 1)
                for t in range(TB):
                    last = nc.tensor.transpose(m.ps[:, 6 + b % 2, t * P:(t + 1) * P], m.hat[:, b * TB + t, :], m.ident[:])
                last.then_inc(turned, 1)

            def up(b):
                pe.wait_ge(xn, b + 1)
                for c in range(CH):
                    n = b * CH + c
                    if n >= 4:
                        pe.wait_ge(h_sb, n - 3)
                    nc.tensor.matmul(m.ps[:, n % 4, :], w1[:, c * P:(c + 1) * P], m.xnT[:, b, :], start=True, stop=True).then_inc(h_ps, 1)

            def down(b):
                pe.wait_ge(h_sb, (b + 1) * CH)
                if b >= 2:
                    pe.wait_ge(added, b - 1)
                for t in range(TB):
                    for c in range(CH):
                        last = nc.tensor.matmul(m.ps[:, 4 + b % 2, t * P:(t + 1) * P], m.hT[:, b % 2, c, t * P:(t + 1) * P],
                                                w2[:, c * P:(c + 1) * P], start=(c == 0), stop=(c == CH - 1))
                last.then_inc(o_ps, 1)

            turn(0)
            turn(1)
            for b in range(B + 1):
                if b < B:
                    up(b)
                if b + 2 < B:
                    turn(b + 2)
                if b >= 1:
                    down(b - 1)

        @block.scalar
        def _(act):
            act.wait_ge(ada, 1)

            def scale_shift(b):
                act.wait_ge(turned, b + 1)
                nc.scalar.activation(m.xnT[:, b, :], m.ps[:, 6 + b % 2, :], ACT.Identity, bias=m.ada[:, B + b:B + b + 1],
                                     scale=m.ada[:, b:b + 1]).then_inc(xn, 1)

            scale_shift(0)
            scale_shift(1)
            for b in range(B):
                if b >= 2:
                    act.wait_ge(o_ps, b - 1)
                for c in range(CH):
                    act.wait_ge(h_ps, b * CH + c + 1)
                    nc.scalar.activation(m.hT[:, b % 2, c, :], m.ps[:, (b * CH + c) % 4, :], ACT.Gelu,
                                         bias=m.cols[:, 6 + c:7 + c]).then_inc(h_sb, 1)
                if b + 2 < B:
                    scale_shift(b + 2)

        @block.gpsimd
        def _(pool):
            pool.wait_ge(hat, 1)
            nc.gpsimd.tensor_tensor(m.state[:], m.state[:], m.f2b[:].unsqueeze(1).to_broadcast([P, T, D]), ALU.add).then_inc(biased, 1)

        @block.vector
        def _(dve):
            chain = Chain(dve, dch)
            dve.wait_ge(ada_ps, 1)
            nc.vector.tensor_scalar(m.ada[:, 0:B], m.ps[:, 7, 0:B], m.cols[:, 4:5], 1.0, ALU.add, ALU.add)
            nc.vector.tensor_scalar(m.ada[:, B:2 * B], m.ps[:, 7, B:2 * B], m.cols[:, 5:6], None, ALU.add).then_inc(ada, 1)
            normalise_batch(dve, chain, m.hat[:], m.state[:], B - 1, m.st).then_inc(hat, 1)
            dve.wait_ge(biased, 1)
            for b in range(B):
                dve.wait_ge(o_ps, b + 1)
                nc.vector.tensor_tensor(m.state[:, b * TB:(b + 1) * TB, :], m.state[:, b * TB:(b + 1) * TB, :],
                                        m.ps[:, 4 + b % 2, :].rearrange("p (t d) -> p t d", t=TB), ALU.add).then_inc(added, 1)
                if b < B - 1:
                    dve.wait_ge(added, b + 1)
                    last = normalise_batch(dve, chain, m.hat[:], m.state[:], b, m.st)
            last.then_inc(normal, 1)


def quantised_block(nc, a, m, sem):
    names = ("weights", "dve", "abs", "abs_sum", "ternary", "rows_normal", "rows_gained", "rows_scaled", "q1", "q1_turned", "q1T",
             "h_ready", "h_in", "h", "statistics", "h_normal", "h_gained", "h_scaled", "q2", "q2_turned", "q2T", "out_ready", "biased",
             "done", "stored", "rows", "pool")
    (w_in, dch, wabs, wsum, wq, r_hat, r_gained, r_scaled, q1, q1_ps, q1T, h_ps, h_in, h_sb, stat, h_hat, h_gained, h_scaled, q2, q2_ps,
     q2T, o_ps, biased, done, out, rows_in, pch) = [sem(f"qb_{n}") for n in names]
    w_n = float(D * HID)
    hid = m.hid
    at = 2 * D
    half = T // 2

    def quantise(dve, chain, rows, b):
        t0, t1 = b * TB, (b + 1) * TB
        big = m.absmax[:, t0:t1]
        chain.link(nc.vector.tensor_reduce(big, rows[:, t0:t1, :], AX.X, ALU.max, apply_absolute_value=True))
        chain.link(nc.vector.tensor_scalar(big, big, LN_EPS, None, ALU.max))
        chain.link(nc.vector.reciprocal(m.qscale[:, t0:t1], big))
        chain.link(nc.vector.tensor_scalar(m.qscale[:, t0:t1], m.qscale[:, t0:t1], 127.0, None, ALU.mult))
        nc.vector.reciprocal(m.step[:, t0:t1], m.qscale[:, t0:t1])
        for t in range(t0, t1):
            last = nc.vector.tensor_scalar(rows[:, t, :], rows[:, t, :], m.qscale[:, t:t + 1], 127.0, ALU.mult, ALU.min)
        chain.link(last)
        return nc.vector.tensor_scalar(rows[:, t0:t1, :], rows[:, t0:t1, :], -128.0, ROUND, ALU.max, ALU.add)

    with nc.Block() as block:
        @block.sync
        def _(sp):
            sp.dma_start(m.tw[:, 0, :], a["ffn_w1"]).then_inc(w_in, 16)
            sp.dma_start(m.tw[:, 1, :], a["ffn_w2"]).then_inc(w_in, 16)
            sp.dma_start(m.frow[:], a["ffn_rows"].partition_broadcast(P)).then_inc(rows_in, 16)
            for b in range(B):
                sp.wait_ge(done, b + 1)
                sp.dma_start(a["out"][b].rearrange("(t p) d -> p t d", p=P), m.x[:, b * TB:(b + 1) * TB, :]).then_inc(out, 16)
            sp.wait_ge(out, 16 * B)

        @block.tensor
        def _(pe):
            pe.wait_ge(wabs, 1)
            nc.tensor.matmul(m.ps[:, 7, 0:2], m.ones32[:], m.wabs[:], start=True, stop=True).then_inc(wsum, 1)

            def turn1(b):
                pe.wait_ge(q1, b + 1)
                for t in range(TB):
                    last = nc.tensor.transpose(m.ps[:, b % 2, :].bitcast(BF16)[:, t * P:(t + 1) * P], m.qrow[:, b * TB + t, :], m.ident_bf[:])
                last.then_inc(q1_ps, 1)

            pe.wait_ge(wq, 1)
            for b in range(B):
                if b >= 2:
                    pe.wait_ge(q1T, b - 1)
                turn1(b)
                pe.wait_ge(q1T, b + 1)
                for t in range(TB):
                    n = b * TB + t
                    if n >= 4:
                        pe.wait_ge(h_in, n - 3)
                    nc.tensor.matmul(m.ps[:, 2 + n % 4, :], m.qT_bf[:, b % 2, t * P:(t + 1) * P], m.tern[:, 0, :], start=True, stop=True).then_inc(h_ps, 1)
            for n in range(T):
                pe.wait_ge(q2, n // TB + 1)
                if n >= 2:
                    pe.wait_ge(q2T, n - 1)
                if n < 2:
                    pe.wait_ge(q1T, B)
                for c in range(CH):
                    last = nc.tensor.transpose(m.ps[:, n % 2, :].bitcast(BF16)[:, c * P:(c + 1) * P],
                                               m.qhid[:, n, c * P:(c + 1) * P], m.ident_bf[:])
                last.then_inc(q2_ps, 1)
                pe.wait_ge(q2T, n + 1)
                b, t = n // TB, n % TB
                if t == 0:
                    pe.wait_ge(h_in, T)
                    if b >= 2:
                        pe.wait_ge(done, b - 1)
                for c in range(CH):
                    last = nc.tensor.matmul(m.ps[:, 4 + b % 2, t * P:(t + 1) * P], m.qT_bf[:, n % 2, c * P:(c + 1) * P],
                                            m.tern[:, 1, c * P:(c + 1) * P], start=(c == 0), stop=(c == CH - 1))
                last.then_inc(o_ps, 1)

        @block.scalar
        def _(act):
            def turn_rows(b):
                act.wait_ge(r_scaled, b + 1)
                nc.scalar.activation(m.qrow[:, b * TB:(b + 1) * TB, :], m.hat[:, b * TB:(b + 1) * TB, :], ACT.Identity,
                                     bias=m.minus_round[:]).then_inc(q1, 1)
                act.wait_ge(q1_ps, b + 1)
                if b >= 2:
                    act.wait_ge(h_ps, TB * (b - 1))
                nc.scalar.copy(m.qT_bf[:, b % 2, :], m.ps[:, b % 2, :].bitcast(BF16)[:, 0:S]).then_inc(q1T, 1)

            def gelu(b):
                for n in range(b * TB, (b + 1) * TB):
                    act.wait_ge(h_in, n + 1)
                    nc.scalar.activation(hid[:, n, :], hid[:, n, :], ACT.Gelu).then_inc(h_sb, 1)

            def normal(b):
                act.wait_ge(stat, b + 1)
                for t in range(b * TB, (b + 1) * TB):
                    last = nc.scalar.activation(hid[:, t, :], hid[:, t, :], ACT.Identity, bias=m.shift[:, t:t + 1], scale=m.st.rstd[:, t:t + 1])
                last.then_inc(h_hat, 1)

            def turn_hidden(b):
                act.wait_ge(h_scaled, b + 1)
                nc.scalar.activation(m.qhid[:, b * TB:(b + 1) * TB, :], hid[:, b * TB:(b + 1) * TB, :], ACT.Identity,
                                     bias=m.minus_round[:]).then_inc(q2, 1)
                for n in range(b * TB, (b + 1) * TB):
                    act.wait_ge(q2_ps, n + 1)
                    if n >= 2:
                        act.wait_ge(o_ps, n - 1)
                    nc.scalar.copy(m.qT_bf[:, n % 2, :], m.ps[:, n % 2, :].bitcast(BF16)[:, 0:HID]).then_inc(q2T, 1)

            act.wait_ge(pch, 2)
            turn_rows(0)
            turn_rows(1)
            gelu(0)
            turn_rows(2)
            gelu(1)
            turn_rows(3)
            gelu(2)
            normal(0)
            gelu(3)
            normal(1)
            normal(2)
            turn_hidden(0)
            normal(3)
            for b in range(1, B):
                turn_hidden(b)

        @block.gpsimd
        def _(pool):
            chain = Chain(pool, pch)
            chain.link(nc.gpsimd.memset(m.ones32[:], 1.0))
            chain.link(nc.gpsimd.memset(m.minus_round[:], -ROUND))
            pool.wait_ge(rows_in, 16)
            for b in range(B):
                if b % 2 == 0:
                    pool.wait_ge(r_hat, b // 2 + 1)
                rows = m.hat[:, b * TB:(b + 1) * TB, :]
                chain.link(nc.gpsimd.tensor_tensor(rows, rows, m.frow[:, 0:D].unsqueeze(1).to_broadcast([P, TB, D]), ALU.mult))
                nc.gpsimd.tensor_tensor(rows, rows, m.frow[:, D:2 * D].unsqueeze(1).to_broadcast([P, TB, D]), ALU.add).then_inc(r_gained, 1)
                pool.wait_ge(r_gained, b + 1)
            nc.gpsimd.tensor_tensor(m.x[:], m.x[:], m.frow[:, at + 3 * HID:at + 3 * HID + D].unsqueeze(1).to_broadcast([P, T, D]),
                                    ALU.add).then_inc(biased, 1)
            pool.wait_ge(biased, 1)
            for b in range(B):
                pool.wait_ge(h_hat, b + 1)
                rows = hid[:, b * TB:(b + 1) * TB, :]
                chain.link(nc.gpsimd.tensor_tensor(rows, rows, m.frow[:, at + HID:at + 2 * HID].unsqueeze(1).to_broadcast([P, TB, HID]), ALU.mult))
                nc.gpsimd.tensor_tensor(rows, rows, m.frow[:, at + 2 * HID:at + 3 * HID].unsqueeze(1).to_broadcast([P, TB, HID]),
                                        ALU.add).then_inc(h_gained, 1)
                pool.wait_ge(h_gained, b + 1)

        @block.vector
        def _(dve):
            chain = Chain(dve, dch)

            def statistics(rows, first, tiles):
                row_moments(dve, chain, rows, tiles, m.st, first)
                root_seed(dve, chain, P, tiles, m.st, first)
                for _ in range(ROOT_STEPS):
                    chain.link(root_step(dve, chain, P, tiles, m.st, first))

            def normal_twice(i):
                tiles = range(i * half, (i + 1) * half)
                rows = m.x[:, i * half:(i + 1) * half, :]
                chain.link(nc.vector.tensor_tensor(rows, rows, m.state[:, i * half:(i + 1) * half, :], ALU.add))
                statistics(m.x[:], i * half, half)
                for t in tiles:
                    last = normalise(dve, m.state[:], m.x[:], t, m.st)
                chain.link(last)
                statistics(m.state[:], i * half, half)
                for t in tiles:
                    last = normalise(dve, m.hat[:], m.state[:], t, m.st)
                last.then_inc(r_hat, 1)

            def quantise_rows(b):
                dve.wait_ge(r_gained, b + 1)
                quantise(dve, chain, m.hat[:], b).then_inc(r_scaled, 1)
                dve.wait_ge(r_scaled, b + 1)
                step = m.step[:, b * TB:(b + 1) * TB]
                chain.link(nc.vector.tensor_scalar(step, step, m.wmean[:, 0:1], None, ALU.mult))

            def hidden(b):
                for n in range(b * TB, (b + 1) * TB):
                    dve.wait_ge(h_ps, n + 1)
                    nc.vector.scalar_tensor_tensor(out=hid[:, n, :], in0=m.ps[:, 2 + n % 4, :], scalar=m.step[:, n:n + 1],
                                                   in1=m.frow[:, at:at + HID], op0=ALU.mult, op1=ALU.add).then_inc(h_in, 1)

            def hidden_statistics(b):
                dve.wait_ge(h_sb, TB * (b + 1))
                t0, t1 = b * TB, (b + 1) * TB
                statistics(hid, t0, TB)
                nc.vector.scalar_tensor_tensor(out=m.shift[:, t0:t1], in0=m.st.mv[:, t0:t1, 0], scalar=-1.0, in1=m.st.rstd[:, t0:t1],
                                               op0=ALU.mult, op1=ALU.mult).then_inc(stat, 1)

            def quantise_hidden(b):
                dve.wait_ge(h_gained, b + 1)
                quantise(dve, chain, hid, b).then_inc(h_scaled, 1)
                dve.wait_ge(h_scaled, b + 1)
                step = m.step[:, b * TB:(b + 1) * TB]
                chain.link(nc.vector.tensor_scalar(step, step, m.wmean[:, 1:2], None, ALU.mult))

            def output(b):
                dve.wait_ge(o_ps, (b + 1) * TB)
                for n in range(b * TB, (b + 1) * TB):
                    last = nc.vector.scalar_tensor_tensor(out=m.x[:, n, :], in0=m.ps[:, 4 + b % 2, n % TB * P:(n % TB + 1) * P],
                                                          scalar=m.step[:, n:n + 1], in1=m.x[:, n, :], op0=ALU.mult, op1=ALU.add)
                last.then_inc(done, 1)

            normal_twice(0)
            dve.wait_ge(w_in, 32)
            for i in range(2):
                last = nc.vector.tensor_reduce(m.wabs[:, i:i + 1], m.tw[:, i, :], AX.X, ALU.add, apply_absolute_value=True)
            dve.wait_ge(pch, 1)
            chain.link(last)
            nc.vector.tensor_copy(m.wmean[:], m.wabs[:]).then_inc(wabs, 1)
            normal_twice(1)
            dve.wait_ge(wsum, 1)
            chain.link(nc.vector.tensor_scalar(m.wmean[:], m.ps[:, 7, 0:2], 1.0 / w_n, LN_EPS, ALU.mult, ALU.max))
            chain.link(nc.vector.reciprocal(m.wscale[:], m.wmean[:]))
            chain.link(nc.vector.reciprocal(m.wmean[:], m.wscale[:]))
            for i in range(2):
                last = nc.vector.tensor_scalar(m.tw[:, i, :], m.tw[:, i, :], m.wscale[:, i:i + 1], ROUND, ALU.mult, ALU.add)
            chain.link(last)
            chain.link(nc.vector.tensor_scalar(m.tw[:], m.tw[:], ROUND, 1.0, ALU.subtract, ALU.min))
            nc.vector.tensor_scalar(m.tern[:], m.tw[:], -1.0, None, ALU.max).then_inc(wq, 1)
            quantise_rows(0)
            quantise_rows(1)
            hidden(0)
            quantise_rows(2)
            hidden(1)
            quantise_rows(3)
            hidden(2)
            hidden_statistics(0)
            hidden(3)
            hidden_statistics(1)
            hidden_statistics(2)
            quantise_hidden(0)
            hidden_statistics(3)
            quantise_hidden(1)
            dve.wait_ge(biased, 1)
            quantise_hidden(2)
            output(0)
            quantise_hidden(3)
            for b in range(1, B):
                output(b)


def build(nc, a):
    with ExitStack() as ctx:
        def sb(name, shape, dt=F32):
            return ctx.enter_context(nc.sbuf_tensor(name, shape, dt))

        big = sb("big", [P, T * HID])
        k6 = sb("k6", [P, 2, HEADS, S], BF16)
        w = sb("w", [P, W_COLS])
        vaug = sb("vaug", [P, B, TB, HEADS, 32])
        def early(lo, *shape):
            names = [f"d{i}" for i in range(len(shape))]
            flat = w[:, lo:lo + int(np.prod(shape))]
            return flat.rearrange(f"p ({' '.join(names)}) -> p {' '.join(names)}", **dict(zip(names, shape)))

        m = Memory()
        m.big = big
        m.ps = ctx.enter_context(nc.psum_tensor("ps", [P, 8, 512], F32))
        m.x = sb("x", [P, T, D])
        m.state = sb("state", [P, T, D])
        m.hat = sb("hat", [P, T, D])
        m.xnT = sb("xnT", [P, B, S])
        m.ident = sb("ident", [P, P])
        m.ident_bf = sb("ident_bf", [P, P], BF16)
        m.st = Statistics()
        m.st.bn = sb("bn", [P, T, 6])
        m.st.mv = sb("mv", [P, T, 2])
        m.st.var = sb("var", [P, T])
        m.st.tmp = sb("tmp", [P, T])
        m.st.rstd = sb("rstd", [P, T])
        m.ctx = sb("ctx", [P, B, D])
        m.ctx_hat = early(1536, B, D)
        m.ctxn = early(2048, NC_ALL)
        m.ctxT = sb("ctxT", [P, NC_ALL])
        m.rows0 = early(0, 6, D)
        m.cols0 = sb("cols0", [P, 10])
        m.mats0 = early(768, 6, D)
        m.sigma = early(3620, D)
        m.cond_rows = sb("cond_rows", [P, B, D])
        m.condT = sb("condT", [P, B])
        m.cos = sb("cos", [P, S])
        m.sin = sb("sin", [P, S])
        m.mask_u8 = sb("mask_u8", [B, S], U8)
        m.cmask_u8 = sb("cmask_u8", [B, N_CTX], U8)
        m.negmask = sb("negmask", [B, S], BF16)
        m.negcmask = sb("negcmask", [B, N_CTX], BF16)
        m.shift_rows = big[0:6, 0:HEADS * S // 2].bitcast(BF16).rearrange("r (h n) -> r h n", h=HEADS)
        m.tri = sb("tri", [P, P], BF16)
        m.ones = sb("ones", [P, P], BF16)
        m.invsum = sb("invsum", [P, GROUPS, TB, 4])
        m.prefer = sb("prefer", [P, EXPERTS])
        m.slot_k = early(2400, NC_ALL)
        m.slot_vT = early(2750, NC_ALL)
        m.slot_v = early(3100, B, D + 1)
        m.qT = big[:, 0:B * S].rearrange("p (b n) -> p b n", b=B)
        m.attn = big[:, B * S:2 * B * S].rearrange("p (b n) -> p b n", b=B)
        m.rowmx = sb("rowmx", [P, B])
        m.negmx = sb("negmx", [P, B])
        m.psum_rows = sb("psum_rows", [P, B])
        m.colsum = sb("colsum", [P, T])
        m.wg = sb("wg", [P, EXPERTS])
        m.logits = sb("logits", [P, T, EXPERTS])
        m.rest = sb("rest", [P, T, EXPERTS])
        m.pick = sb("pick", [P, T, EXPERTS])
        m.gate = sb("gate", [P, T, EXPERTS])
        m.top = sb("top", [P, TOP_K, T])
        m.best = sb("best", [P, T])
        m.onehot = sb("onehot", [P, TOP_K, T, EXPERTS])
        m.onehot_bf = sb("onehot_bf", [P, TOP_K, T, EXPERTS], BF16)
        m.rank = sb("rank", [P, 2, T, EXPERTS])
        m.total = sb("total", [P, EXPERTS])
        m.share = sb("share", [P, EXPERTS, T])
        m.share2 = sb("share2", [P, AT_ONCE, T])
        m.hT = big[:, 0:2 * CH * S].rearrange("p (i c n) -> p i c n", i=2, c=CH)
        m.fc = big[:, 8 * S:8 * S + AT_ONCE * HID].rearrange("p (u n) -> p u n", u=AT_ONCE)
        m.proj = big[:, 8 * S + AT_ONCE * HID:8 * S + 2 * AT_ONCE * HID].rearrange("p (u c n) -> p u c n", u=AT_ONCE, c=CH)
        m.w = w
        m.cols = sb("cols", [P, 10])
        m.f2b = sb("f2b", [P, D])
        m.ada = sb("ada", [P, 2 * B])
        m.k6 = k6
        m.kc6 = sb("kc6", [P, B, HEADS, P], BF16)
        m.q6 = sb("q6", [P, 2, PAIRS, S], BF16)
        m.vaug = vaug
        m.vcaug = sb("vcaug", [P, B, HEADS, 32])
        m.rot = big[:, 0:2 * S].rearrange("p (i n) -> p i n", i=2)
        m.left = big[:, 4 * S:6 * S].rearrange("p (i n) -> p i n", i=2)
        m.swap = big[:, 8 * S:10 * S].rearrange("p (i n) -> p i n", i=2)
        m.parts = big[:, 10 * S:16 * S].bitcast(BF16).rearrange("p (i c n) -> p i c n", i=4, c=3)
        m.probs = big[:, 0:8 * S].rearrange("p (i u n) -> p i u n", i=2, u=4)
        m.unit = big[:, 8 * S:10 * S].rearrange("p (i n) -> p i n", i=2)
        m.inverse = big[:, 10 * S:12 * S].rearrange("p (i t h r) -> p i t h r", i=2, t=TB, h=4)
        m.on = big[:, 12 * S:16 * S].rearrange("p (g n) -> p g n", g=GROUPS)
        m.units = big[:, 0:8 * S].rearrange("p (i g n) -> p i g n", i=2, g=GROUPS)
        m.inverses = big[:, 8 * S:10 * S].rearrange("p (i t r) -> p i t r", i=2, r=32)
        m.q6_third = big[:, 12 * S:16 * S].bitcast(BF16).rearrange("p (i n) -> p i n", i=PAIRS)
        m.cprobs = (m.xnT, m.hat[:].rearrange("p t d -> p (t d)").rearrange("p (j n) -> p j n", j=4))
        m.maxima = sb("maxima", [P, TB, HEADS])
        m.mcparts = sb("mcparts", [P, TB, 2, 3, PAIRS], BF16)
        m.mct = sb("mct", [3 * HEADS, 2, S], BF16)
        m.mparts = sb("mparts", [P, 2, TB, 2, 3, 2], BF16)
        m.mt = m.mct[0:12]
        m.hid = big[:].rearrange("p (t n) -> p t n", t=T)
        m.tw = w[:, 0:2 * HID].rearrange("p (i n) -> p i n", i=2)
        m.tern = vaug[:, 1, 0].rearrange("p h n -> p (h n)").bitcast(BF16).rearrange("p (i n) -> p i n", i=2)
        m.frow = w[:, 2 * HID:5 * HID + 3 * D]
        m.wabs = sb("wabs", [P, 2])
        m.wmean = sb("wmean", [P, 2])
        m.wscale = sb("wscale", [P, 2])
        m.ones32 = sb("ones32", [P, P])
        m.absmax = sb("absmax", [P, T])
        m.qscale = sb("qscale", [P, T])
        m.shift = sb("shift", [P, T])
        m.minus_round = sb("minus_round", [P, 1])
        m.step = sb("step", [P, T])
        m.qrow = vaug[:, 0, 0:2].rearrange("p t h n -> p (t h n)").bitcast(BF16).rearrange("p (t d) -> p t d", t=T)
        m.qT_bf = vaug[:, 1, 1].rearrange("p h n -> p (h n)").bitcast(BF16).rearrange("p (i n) -> p i n", i=2)
        m.qhid = k6[:, 0].rearrange("p h n -> p (h n)")[:, 0:T * HID].rearrange("p (t n) -> p t n", t=T)
        with stage(nc) as sem:
            load_and_prepare(nc, a, m, sem)
        with nc.Fori(0, SLOT_STEPS), stage(nc) as sem:
            slot_step(nc, a, m, sem)
        with stage(nc) as sem:
            route_tokens(nc, a, m, sem)
        with nc.Fori(0, EXPERTS // AT_ONCE) as turn, stage(nc) as sem:
            some_experts(nc, a, m, sem, turn)
        with stage(nc) as sem:
            begin_layers(nc, a, m, sem)
        with nc.Fori(0, LAYERS) as layer, stage(nc) as sem:
            attend(nc, a, m, sem, layer)
            feed_forward(nc, a, m, sem, layer)
        with stage(nc) as sem:
            quantised_block(nc, a, m, sem)


def rotary_tables():
    half = HD // 2
    inv = np.float32(1.0) / np.power(np.float32(10000.0), np.arange(half, dtype=np.float32) / np.float32(half))
    ang = np.arange(S, dtype=np.float32)[:, None] * inv
    cos, sin = np.cos(ang).T.astype(np.float32), np.sin(ang).T.astype(np.float32)
    return np.tile(np.concatenate([cos, cos]), (HEADS, 1)), np.tile(np.concatenate([-sin, sin]), (HEADS, 1))


def lay_out(i):
    swap = np.arange(D).reshape(HEADS, 2, HD // 2)[:, ::-1].reshape(D)
    i = {k: np.asarray(v) for k, v in i.items()}
    L0, L1, F = "L0_xcond_", "L1_xcond_", "L1_ffn_"

    def out_rows(w):
        r = np.zeros((4, 32, GROUPS, D), np.float32)
        r[:, 0:HD] = w.T.reshape(GROUPS, 4, HD, D).transpose(1, 2, 0, 3)
        return r.reshape(P, GROUPS * D)

    def layer(n):
        qkv = i[L1 + "qkv_w"][n]
        q, k, v = qkv[0:D], qkv[D:2 * D], qkv[2 * D:]
        cq, ck = i[L1 + "cq_w"][n], i[L1 + "ck_w"][n]
        f2 = i[L1 + "f2_w"][n].T.reshape(CH, P, D).transpose(1, 0, 2).reshape(P, HID)
        return np.concatenate([i[L1 + "n1_w"][n].T, q.T, q[swap].T, k.T, k[swap].T, v.T, out_rows(i[L1 + "so_w"][n]),
                               i[L1 + "n2_w"][n].T, cq.T, cq[swap].T, ck.T, ck[swap].T, i[L1 + "cv_w"][n].T, out_rows(i[L1 + "co_w"][n]),
                               i[L1 + "n3_w"][n].T, i[L1 + "f1_w"][n].T, f2], axis=1)

    def layer_cols(n):
        vecs = [i[L1 + k][n].reshape(-1, P) for k in ("n1_b", "n2_b", "n3_b", "f1_b")]
        return np.concatenate(vecs).T

    cos, sin = rotary_tables()
    got = {
        "x": i["x"], "ctx": i["ctx_1024"], "cond": i["cond_1024"], "condT": i["cond_1024"].T,
        "mask": i["mask_BxS_bf0"], "cmask": i["mask_BxS2_bf0"], "cos": cos, "sin": sin,
        "slot_mats": np.stack([i[L0 + k] for k in ("wk", "wv", "wq", "wu", "w1", "w2")], axis=1),
        "slot_cols": np.stack([i[L0 + k] for k in ("lnkv_g", "lnkv_b", "lnq_g", "lnq_b", "lnm_g", "lnm_b", "bk", "bv", "bq", "b1")], axis=1),
        "slot_rows": np.stack([i[L0 + k].reshape(D) for k in ("q_mu", "q_logsig", "lnp_g", "lnp_b", "bu", "b2")]),
        "w_g": i["L0_ffn_w_g"], "c_fc": i["L0_ffn_c_fc"],
        "c_proj": i["L0_ffn_c_proj"].reshape(EXPERTS, CH, P, D).transpose(0, 2, 1, 3),
        "w": np.stack([layer(min(n, LAYERS - 1)) for n in range(LAYERS + 1)]),
        "cols": np.stack([layer_cols(min(n, LAYERS - 1)) for n in range(LAYERS + 1)]),
        "f2_b": i[L1 + "f2_b"],
        "ffn_w1": i[F + "w1"].T, "ffn_w2": i[F + "w2"].T.reshape(CH, P, D).transpose(1, 0, 2).reshape(P, HID),
        "ffn_rows": np.concatenate([i[F + k] for k in ("ln1_w", "ln1_b", "b1", "ln2_w", "ln2_b", "b2")]),
    }
    return {k: np.ascontiguousarray(v) for k, v in got.items()}


SCRATCH = {"neg_mask": ((B, S), BF16), "neg_cmask": ((B, N_CTX), BF16), "queries": ((B, P, PRODUCTS, S), BF16),
           "keys": ((B, P, PRODUCTS, S), BF16), "ctx_keys": ((P, PRODUCTS, NC_ALL), BF16)}


def kernel(**inputs):
    import concourse.bacc as bacc
    from concourse.bass_utils import run_bass_kernel_spmd

    nc = bacc.Bacc("TRN2", target_bir_lowering=False, num_devices=1)
    arrays = lay_out(inputs)
    a = {k: nc.dram_tensor(f"in_{k}", v.shape, mybir.dt.from_np(v.dtype), kind="ExternalInput").ap() for k, v in arrays.items()}
    a |= {k: nc.dram_tensor(f"scratch_{k}", shape, dt, kind="Internal").ap() for k, (shape, dt) in SCRATCH.items()}
    a["out"] = nc.dram_tensor("out", (B, S, D), F32, kind="ExternalOutput").ap()
    build(nc, a)
    r = run_bass_kernel_spmd(nc, [{f"in_{k}": v for k, v in arrays.items()}], core_ids=[0])
    return r.results[0]["out"]
```
